# Optimizing a Trainium2 kernel written in Bass

```python
import numpy as np
import jax
import jax.numpy as jnp

def _softmax(x, axis=-1):
    return jax.nn.softmax(x, axis=axis)

def _gelu(x):
    return jax.nn.gelu(x, approximate=True)

def _silu(x):
    return jax.nn.silu(x)

def _sigmoid(x):
    return jax.nn.sigmoid(x)

def _layernorm(x, axis=-1, eps=1e-05):
    m = jnp.mean(x, axis=axis, keepdims=True)
    v = jnp.var(x, axis=axis, keepdims=True)
    return (x - m) / jnp.sqrt(v + eps)

def _scatter_add(tgt, idx, src, axis=0):
    return tgt.at[idx].add(src)

def _segment_sum(src, seg, n):
    return jax.ops.segment_sum(src, seg, n)
kernel_name = 'mk_vit_tower_cls_d1_tok_img768_r4_6aee12'

def setup_inputs(seed: int=0):
    np.random.seed(seed)
    _w = jnp.asarray

    def _rec_inputs():
        import jax
        import jax.numpy as jnp
        _rk = jax.random.key(seed)
        x = -0.000147625 + 0.999875 * jax.random.normal(jax.random.fold_in(_rk, 1), (64, 3, 224, 224), jnp.float32)
        cls_tok = 0.02 * jax.random.normal(jax.random.fold_in(_rk, 5), (1, 1, 192), jnp.float32)
        return (x, cls_tok)
    x, cls_tok = _rec_inputs()

    def _L0_tok_setup():
        import jax, jax.numpy as jnp
        import numpy as np
        EPS = 1e-05
        P = 16

        def _layernorm(x, gamma, beta):
            mu = jnp.mean(x, axis=-1, keepdims=True)
            var = jnp.mean(jnp.square(x - mu), axis=-1, keepdims=True)
            return (x - mu) * jax.lax.rsqrt(var + EPS) * gamma + beta
        key = jax.random.key(seed)
        ks = jax.random.split(key, 9)
        B, C, H, W = (64, 3, 224, 224)
        dim = 192
        patch_dim = C * P * P
        num_patches = (H // P) ** 2
        img = jax.random.normal(ks[0], (B, C, H, W), dtype=jnp.float32)
        ln1_g = jnp.ones((patch_dim,), jnp.float32)
        ln1_b = jnp.zeros((patch_dim,), jnp.float32)
        W_proj = jax.random.normal(ks[1], (patch_dim, dim), jnp.float32) / np.sqrt(patch_dim)
        b_proj = jnp.zeros((dim,), jnp.float32)
        ln2_g = jnp.ones((dim,), jnp.float32)
        ln2_b = jnp.zeros((dim,), jnp.float32)
        pos_embedding = jax.random.normal(ks[2], (1, num_patches + 1, dim), jnp.float32)
        cls_token = jax.random.normal(ks[3], (1, 1, dim), jnp.float32)
        return {'img': img, 'ln1_g': ln1_g, 'ln1_b': ln1_b, 'W_proj': W_proj, 'b_proj': b_proj, 'ln2_g': ln2_g, 'ln2_b': ln2_b, 'pos_embedding': pos_embedding, 'cls_token': cls_token}
    _L0_tok_all = _L0_tok_setup()
    _L0_tok_in = {k: v for k, v in _L0_tok_all.items() if k in ('ln1_g', 'ln1_b', 'W_proj', 'b_proj', 'ln2_g', 'ln2_b', 'pos_embedding', 'cls_token')}
    del _L0_tok_all

    def _L0_attn_setup():
        import jax, jax.numpy as jnp
        import numpy as np
        B, N, DIM = (16, 577, 192)
        HEADS, HEAD_DIM = (12, 64)
        QKV_DIM = HEADS * HEAD_DIM
        MAX_REL = 14
        TABLE_ROWS = 2 * MAX_REL + 2

        def _rel_indices(n, max_rel):
            m = n - 1
            side = int(m ** 0.5)
            r = np.arange(m)
            dv = r[None, :] // side - r[:, None] // side
            dh = r[None, :] % side - r[:, None] % side
            iv = np.clip(dv, -max_rel, max_rel) + max_rel + 1
            ih = np.clip(dh, -max_rel, max_rel) + max_rel + 1
            iv = np.pad(iv, ((1, 0), (1, 0)))
            ih = np.pad(ih, ((1, 0), (1, 0)))
            return (jnp.asarray(iv), jnp.asarray(ih))
        key = jax.random.key(seed)
        ks = jax.random.split(key, 8)
        return {'x': jax.random.normal(ks[0], (B, N, DIM), jnp.float32), 'qkv_w': jax.random.normal(ks[1], (3 * QKV_DIM, DIM), jnp.float32) * 0.02, 'proj_w': jax.random.normal(ks[2], (DIM, QKV_DIM), jnp.float32) * 0.02, 'proj_b': jnp.zeros((DIM,), jnp.float32), 'tab_kv': jax.random.normal(ks[3], (TABLE_ROWS, HEAD_DIM), jnp.float32) * 0.02, 'tab_kh': jax.random.normal(ks[4], (TABLE_ROWS, HEAD_DIM), jnp.float32) * 0.02, 'tab_vv': jax.random.normal(ks[5], (TABLE_ROWS, HEAD_DIM), jnp.float32) * 0.02, 'tab_vh': jax.random.normal(ks[6], (TABLE_ROWS, HEAD_DIM), jnp.float32) * 0.02}
    _L0_attn_all = _L0_attn_setup()
    _L0_attn_in = {k: v for k, v in _L0_attn_all.items() if k in ('qkv_w', 'proj_w', 'proj_b', 'tab_kv', 'tab_kh', 'tab_vv', 'tab_vh')}
    del _L0_attn_all

    def _L0_ffn_setup():
        import jax, jax.numpy as jnp
        import numpy as np
        B, T, C = (4, 512, 192)
        E, K = (8, 2)

        def _mlp(x, wfc, wproj):
            h = jnp.square(jax.nn.relu(x @ wfc))
            return h @ wproj
        key = jax.random.key(seed)
        ks = jax.random.split(key, 6)
        s = 0.02
        return {'x': jax.random.normal(ks[0], (B, T, C), jnp.float32), 'w_fc_sh': jax.random.normal(ks[1], (C, C), jnp.float32) * s, 'w_proj_sh': jax.random.normal(ks[2], (C, C), jnp.float32) * s, 'w1': jax.random.normal(ks[3], (E, C, C), jnp.float32) * s, 'w2': jax.random.normal(ks[4], (E, C, C), jnp.float32) * s, 'router_w': jax.random.normal(ks[5], (E, C), jnp.float32) * s, 'balance_bias': jnp.zeros((E,), jnp.float32)}
    _L0_ffn_all = _L0_ffn_setup()
    _L0_ffn_in = {k: v for k, v in _L0_ffn_all.items() if k in ('w_fc_sh', 'w_proj_sh', 'w1', 'w2', 'router_w', 'balance_bias')}
    del _L0_ffn_all
    return {'x': x, 'cls_tok': cls_tok, 'L0_tok_ln1_g': _L0_tok_in['ln1_g'], 'L0_tok_ln1_b': _L0_tok_in['ln1_b'], 'L0_tok_W_proj': _L0_tok_in['W_proj'], 'L0_tok_b_proj': _L0_tok_in['b_proj'], 'L0_tok_ln2_g': _L0_tok_in['ln2_g'], 'L0_tok_ln2_b': _L0_tok_in['ln2_b'], 'L0_tok_pos_embedding': _L0_tok_in['pos_embedding'], 'L0_tok_cls_token': _L0_tok_in['cls_token'], 'L0_attn_qkv_w': _L0_attn_in['qkv_w'], 'L0_attn_proj_w': _L0_attn_in['proj_w'], 'L0_attn_proj_b': _L0_attn_in['proj_b'], 'L0_attn_tab_kv': _L0_attn_in['tab_kv'], 'L0_attn_tab_kh': _L0_attn_in['tab_kh'], 'L0_attn_tab_vv': _L0_attn_in['tab_vv'], 'L0_attn_tab_vh': _L0_attn_in['tab_vh'], 'L0_ffn_w_fc_sh': _L0_ffn_in['w_fc_sh'], 'L0_ffn_w_proj_sh': _L0_ffn_in['w_proj_sh'], 'L0_ffn_w1': _L0_ffn_in['w1'], 'L0_ffn_w2': _L0_ffn_in['w2'], 'L0_ffn_router_w': _L0_ffn_in['router_w'], 'L0_ffn_balance_bias': _L0_ffn_in['balance_bias']}

def reference(x, cls_tok, L0_tok_ln1_g, L0_tok_ln1_b, L0_tok_W_proj, L0_tok_b_proj, L0_tok_ln2_g, L0_tok_ln2_b, L0_tok_pos_embedding, L0_tok_cls_token, L0_attn_qkv_w, L0_attn_proj_w, L0_attn_proj_b, L0_attn_tab_kv, L0_attn_tab_kh, L0_attn_tab_vv, L0_attn_tab_vh, L0_ffn_w_fc_sh, L0_ffn_w_proj_sh, L0_ffn_w1, L0_ffn_w2, L0_ffn_router_w, L0_ffn_balance_bias):
    import jax
    import jax.numpy as jnp

    def _L0_tok_ref(img, ln1_g, ln1_b, W_proj, b_proj, ln2_g, ln2_b, pos_embedding, cls_token):
        import jax, jax.numpy as jnp
        import numpy as np
        EPS = 1e-05
        P = 16

        def _layernorm(x, gamma, beta):
            mu = jnp.mean(x, axis=-1, keepdims=True)
            var = jnp.mean(jnp.square(x - mu), axis=-1, keepdims=True)
            return (x - mu) * jax.lax.rsqrt(var + EPS) * gamma + beta
        B, C, H, Wd = img.shape
        h, w = (H // P, Wd // P)
        x = img.reshape(B, C, h, P, w, P)
        x = jnp.transpose(x, (0, 2, 4, 3, 5, 1)).reshape(B, h * w, P * P * C)
        x = _layernorm(x, ln1_g, ln1_b)
        x = jnp.einsum('bnp,pd->bnd', x, W_proj) + b_proj
        x = _layernorm(x, ln2_g, ln2_b)
        cls = jnp.broadcast_to(cls_token, (B, 1, cls_token.shape[-1]))
        x = jnp.concatenate([cls, x], axis=1)
        x = x + pos_embedding
        return x

    def _L0_attn_ref(x, qkv_w, proj_w, proj_b, tab_kv, tab_kh, tab_vv, tab_vh):
        import jax, jax.numpy as jnp
        import numpy as np
        B, N, DIM = (16, 577, 192)
        HEADS, HEAD_DIM = (12, 64)
        QKV_DIM = HEADS * HEAD_DIM
        MAX_REL = 14
        TABLE_ROWS = 2 * MAX_REL + 2

        def _rel_indices(n, max_rel):
            m = n - 1
            side = int(m ** 0.5)
            r = np.arange(m)
            dv = r[None, :] // side - r[:, None] // side
            dh = r[None, :] % side - r[:, None] % side
            iv = np.clip(dv, -max_rel, max_rel) + max_rel + 1
            ih = np.clip(dh, -max_rel, max_rel) + max_rel + 1
            iv = np.pad(iv, ((1, 0), (1, 0)))
            ih = np.pad(ih, ((1, 0), (1, 0)))
            return (jnp.asarray(iv), jnp.asarray(ih))
        b, n, _ = x.shape
        scale = HEAD_DIM ** (-0.5)
        qkv = (x @ qkv_w.T).reshape(b, n, 3, HEADS, HEAD_DIM).transpose(2, 0, 3, 1, 4)
        q, k, v = (qkv[0], qkv[1], qkv[2])
        attn = jnp.einsum('bhqd,bhkd->bhqk', q, k) * scale
        iv, ih = _rel_indices(n, MAX_REL)
        r_p_k = tab_kv[iv] + tab_kh[ih]
        attn = attn + jnp.einsum('bhqd,qkd->bhqk', q, r_p_k) * scale
        attn = jax.nn.softmax(attn, axis=-1)
        out = jnp.einsum('bhqk,bhkd->bhqd', attn, v)
        r_p_v = tab_vv[iv] + tab_vh[ih]
        out = out + jnp.einsum('bhqk,qkd->bhqd', attn, r_p_v)
        out = out.transpose(0, 2, 1, 3).reshape(b, n, QKV_DIM)
        return out @ proj_w.T + proj_b

    def _L0_ffn_ref(x, w_fc_sh, w_proj_sh, w1, w2, router_w, balance_bias):
        import jax, jax.numpy as jnp
        import numpy as np
        B, T, C = (4, 512, 192)
        E, K = (8, 2)

        def _mlp(x, wfc, wproj):
            h = jnp.square(jax.nn.relu(x @ wfc))
            return h @ wproj
        Bx, Tx, Cx = x.shape
        shared = _mlp(x, w_fc_sh, w_proj_sh)
        xf = x.reshape(-1, Cx)
        logits = xf.astype(jnp.float32) @ router_w.T
        scores = jax.nn.sigmoid(logits)
        _, idx = jax.lax.top_k(scores + balance_bias, K)
        tw = jnp.take_along_axis(scores, idx, axis=-1)
        tw = tw / (tw.sum(-1, keepdims=True) + 1e-20)
        combine = (jax.nn.one_hot(idx, E, dtype=tw.dtype) * tw[..., None]).sum(1)
        h = jnp.square(jax.nn.relu(jnp.einsum('nc,ech->neh', xf, w1)))
        y = jnp.einsum('neh,ehc->nec', h, w2)
        routed = jnp.einsum('nec,ne->nc', y, combine)
        return shared + routed.reshape(Bx, Tx, Cx)
    h = _L0_tok_ref(x, L0_tok_ln1_g, L0_tok_ln1_b, L0_tok_W_proj, L0_tok_b_proj, L0_tok_ln2_g, L0_tok_ln2_b, L0_tok_pos_embedding, L0_tok_cls_token)
    h = jnp.concatenate([jnp.broadcast_to(cls_tok, (h.shape[0], 1, h.shape[2])), h], axis=1)
    h = h + _L0_attn_ref(_layernorm(h, axis=-1), L0_attn_qkv_w, L0_attn_proj_w, L0_attn_proj_b, L0_attn_tab_kv, L0_attn_tab_kh, L0_attn_tab_vv, L0_attn_tab_vh)
    h = h + _L0_ffn_ref(_layernorm(h, axis=-1), L0_ffn_w_fc_sh, L0_ffn_w_proj_sh, L0_ffn_w1, L0_ffn_w2, L0_ffn_router_w, L0_ffn_balance_bias)
    return h

_drawn_inputs = setup_inputs


def setup_inputs(seed=0):
    import zlib

    import numpy as np

    out = dict(_drawn_inputs(seed))
    spreads = {'L0_tok_ln1_g': (1.0, 0.2),
     'L0_tok_ln1_b': (0.0, 0.1),
     'L0_tok_b_proj': (0.0, 0.1),
     'L0_tok_ln2_g': (1.0, 0.2),
     'L0_tok_ln2_b': (0.0, 0.1),
     'L0_attn_proj_b': (0.0, 0.1),
     'L0_ffn_balance_bias': (0.0, 0.603)}
    factors = {'cls_tok': 8.0,
     'L0_attn_qkv_w': 3.663,
     'L0_attn_proj_w': 3.538,
     'L0_attn_tab_kv': 8.0,
     'L0_attn_tab_kh': 8.0,
     'L0_attn_tab_vv': 8.0,
     'L0_attn_tab_vh': 8.0,
     'L0_ffn_w_fc_sh': 3.439,
     'L0_ffn_w_proj_sh': 3.171,
     'L0_ffn_w1': 4.858,
     'L0_ffn_w2': 4.39,
     'L0_ffn_router_w': 7.017}
    for name, (base, spread) in spreads.items():
        noise = np.random.default_rng([zlib.crc32(name.encode()), seed]).standard_normal(out[name].shape)
        drawn = base * np.exp(spread * noise) if base else spread * noise
        out[name] = jnp.asarray(drawn.astype(out[name].dtype))
    for name, factor in factors.items():
        out[name] = (out[name] * factor).astype(out[name].dtype)
    return out
```

```python
import numpy as np
import concourse.bass as bass
from concourse import mybir
from contextlib import ExitStack

fp32 = mybir.dt.float32
ALU = mybir.AluOpType
ACT = mybir.ActivationFunctionType
AX = mybir.AxisListType

B, CH, IMG, PATCH = 64, 3, 224, 16
SIDE = IMG // PATCH
NTOK = SIDE * SIDE + 2
DIM = 192
PDIM = PATCH * PATCH * CH
HEADS, HD = 12, 64
PAIRS = HEADS // 2
EXPERTS = 8
EPS = 1e-5
SCALE = HD ** -0.5
GB = 8
GROUPS = B // GB
GT = GB * NTOK
HALF = NTOK // 2
TILES = 2 * GB
PRIMED = 1
C0, C1 = 128, DIM - 128


class Steps:

    def __init__(self, eng, sem, base=0):
        self.eng, self.sem, self.base, self.n = eng, sem, base, 0

    def did(self, ins):
        ins.then_inc(self.sem, 1)
        self.n += 1

    def settle(self):
        self.eng.wait_ge(self.sem, self.base + self.n)

    def settle_apart(self, passed):
        self.settle()
        self.eng.sem_inc(passed, 1)


class Memory:

    def __init__(self, nc, ctx, stage):
        self.nc, self.ctx, self.stage = nc, ctx, stage

    def sb(self, name, shape, dt=fp32):
        return self.ctx.enter_context(self.nc.sbuf_tensor(f"{self.stage}_{name}", shape, dt))

    def bank(self, name):
        return self.ctx.enter_context(self.nc.psum_tensor(f"{self.stage}_{name}", [128, 512], fp32))

    def sem(self, name):
        return self.ctx.enter_context(self.nc.semaphore(f"{self.stage}_{name}"))


def view(ap, dims, offset=0):
    return bass.AP(tensor=ap.tensor, offset=ap.offset + offset, ap=[list(ap.ap[0])] + [list(d) for d in dims])


def make_identity(pool, nc, ident, sem):
    nc.gpsimd.memset(ident[:, :], 0.0).then_inc(sem, 1)
    pool.wait_ge(sem, 1)
    nc.gpsimd.affine_select(out=ident[:, :], in_=ident[:, :], compare_op=ALU.not_equal, fill=1.0, base=0,
                            pattern=[[-1, 128]], channel_multiplier=1).then_inc(sem, 1)


def tokens_stage(nc, x, cls_tok, ln1_g, ln1_b, w_proj, b_proj, ln2_g, ln2_b, pos, cls_token, hidden0):
    P = GB * SIDE
    KC = PDIM // 128
    XROW = PATCH * IMG
    with ExitStack() as ctx:
        m = Memory(nc, ctx, "tok")
        pixels = m.sb("pixels", [P, 2, CH, XROW])
        normed = m.sb("normed", [P, 2, PDIM])
        patchT = m.sb("patchT", [128, 2, KC, P])
        w = m.sb("w", [128, 2, CH, DIM])
        g1, b1 = m.sb("g1", [128, 2, CH]), m.sb("b1", [128, 2, CH])
        b1x = m.sb("b1x", [128, KC, P])
        bias = m.sb("bias", [P, DIM])
        g2, b2 = m.sb("g2", [P, DIM]), m.sb("b2", [P, DIM])
        posb = m.sb("posb", [P, SIDE, DIM])
        stat1, mv1, sd1 = m.sb("stat1", [P, 2, CH, 6]), m.sb("mv1", [P, 2, 2]), m.sb("sd1", [P, 2, 1])
        eps = m.sb("eps", [128, 1])
        stat2, mv2, sd2 = m.sb("stat2", [P, 2, 6]), m.sb("mv2", [P, 2, 2]), m.sb("sd2", [P, 2, 1])
        mv1_made, sd1_made, mv2_made, sd2_made = m.sem("mv1_made"), m.sem("sd1_made"), m.sem("mv2_made"), m.sem("sd2_made")
        y = m.sb("y", [P, 2, DIM])
        yn = m.sb("yn", [P, 2, DIM])
        yg = m.sb("yg", [P, 2, DIM])
        rows = m.sb("rows", [P, 2, SIDE, DIM])
        cls = m.sb("cls", [B, 2, DIM])
        clsp = m.sb("clsp", [B, DIM])
        ident = m.sb("ident", [128, 128])
        t_bank = [[m.bank(f"t{v}{i}") for i in range(2)] for v in range(2)]
        y_bank = [m.bank(f"y{v}") for v in range(2)]
        pixels_in = [m.sem(f"pixels_in{s}") for s in range(2)]
        consts_in, ident_made = m.sem("consts_in"), m.sem("ident_made")
        bias_full, w_scaled = m.sem("bias_full"), m.sem("w_scaled")
        dve_step, pool_step, passed = m.sem("dve_step"), m.sem("pool_step"), m.sem("passed")
        normed_made, turned, patchT_made = m.sem("normed_made"), m.sem("turned"), m.sem("patchT_made")
        projected, y_made, yn_made, row_made = m.sem("projected"), m.sem("y_made"), m.sem("yn_made"), m.sem("row_made")
        rows_out = [m.sem(f"rows_out{s}") for s in range(2)]
        pixels_used, b1x_made, cls_made, cls_out, posb_made = (m.sem("pixels_used"), m.sem("b1x_made"),
                                                              m.sem("cls_made"), m.sem("cls_out"), m.sem("posb_made"))
        x_rows = x.rearrange("b c (r p) w -> b r c (p w)", p=PATCH)
        hid_rows = hidden0[:, 2:NTOK, :].rearrange("b (r w) d -> b r w d", w=SIDE)
        CONSTS = 3 + 3 + GB + 3

        with nc.Block() as block:

            @block.sync
            def _(sp):
                for s in (*rows_out, turned, row_made, patchT_made, yn_made):
                    sp.sem_inc(s, PRIMED)
                def load(g, s):
                    for j in range(GB):
                        sp.dma_start(pixels[SIDE * j:SIDE * (j + 1), s, :, :],
                                     x_rows[bass.ds(g * GB + j, 1)].rearrange("a r c n -> (a r) c n")
                                     ).then_inc(pixels_in[s], 16)
                def store(g, s):
                    sp.wait_ge(row_made, (g + 1) * SIDE + PRIMED)
                    for j in range(GB):
                        sp.dma_start(hid_rows[bass.ds(g * GB + j, 1)].rearrange("a r w d -> (a r) w d"),
                                     rows[SIDE * j:SIDE * (j + 1), s, :, :]).then_inc(rows_out[s], 16)

                load(0, 0)
                load(1, 1)
                with sp.Fori(0, (GROUPS - 2) // 2) as pair:
                    gg = pair * 2
                    for s in range(2):
                        sp.wait_ge(normed_made, (gg + s + 1) * SIDE)
                        load(gg + s + 2, s)
                        store(gg + s, s)
                for s in range(2):
                    store(GROUPS - 2 + s, s)
                for s in range(2):
                    sp.wait_ge(rows_out[s], 16 * GB * (GROUPS // 2) + PRIMED)

            @block.scalar
            def _(act):
                act.wait_ge(b1x_made, 1)
                with act.Fori(0, GROUPS) as g:
                    for wv in range(SIDE + 1):
                        if wv < SIDE:
                            v, t = wv % 2, g * SIDE + wv
                            act.wait_ge(mv1_made, t + 1)
                            nc.scalar.activation(sd1[:, v, :], mv1[:, v, 1:2], ACT.Sqrt, bias=eps[0:P, :]).then_inc(sd1_made, 1)
                            act.wait_ge(turned, t + 1 + PRIMED)
                            for i in range(2):
                                ins = nc.scalar.activation(patchT[:, v, 3 * i:3 * i + 3, :],
                                                           t_bank[v][i][:, 0:3 * P].rearrange("p (k n) -> p k n", k=3),
                                                           ACT.Copy)
                            ins.then_inc(patchT_made, 1)
                        if wv:
                            v, t = (wv - 1) % 2, g * SIDE + wv - 1
                            act.wait_ge(mv2_made, t + 1)
                            nc.scalar.activation(sd2[:, v, :], mv2[:, v, 1:2], ACT.Sqrt, bias=eps[0:P, :]).then_inc(sd2_made, 1)

            @block.gpsimd
            def _(pool):
                make_identity(pool, nc, ident, ident_made)
                pool.dma_start(w[:, :, :, :], w_proj.rearrange("(h q c) d -> q h c d", q=128, c=CH)).then_inc(consts_in, 16)
                for dst, src in ((g1, ln1_g), (b1, ln1_b)):
                    pool.dma_start(dst[:, :, :], src.rearrange("(h q c) -> q h c", q=128, c=CH)).then_inc(consts_in, 16)
                for dst, src in ((bias, b_proj), (g2, ln2_g), (b2, ln2_b)):
                    pool.dma_start(dst[:, :], bass.AP(tensor=src.tensor, offset=src.offset, ap=[[0, P], [1, DIM]])
                                   ).then_inc(consts_in, 16)
                for j in range(GB):
                    pool.dma_start(posb[SIDE * j:SIDE * (j + 1), :, :],
                                   pos[0, 1:SIDE * SIDE + 1, :].rearrange("(r w) d -> r w d", w=SIDE)).then_inc(consts_in, 16)
                for dst, src in ((cls[:, 0, :], cls_tok[0, 0, :]), (cls[:, 1, :], cls_token[0, 0, :]), (clsp[:, :], pos[0, 0, :])):
                    pool.dma_start(dst, bass.AP(tensor=src.tensor, offset=src.offset, ap=[[0, B], [1, DIM]])
                                   ).then_inc(consts_in, 16)
                pool.wait_ge(consts_in, 16 * CONSTS)
                nc.gpsimd.tensor_tensor(cls[:, 1, :], cls[:, 1, :], clsp[:, :], ALU.add).then_inc(cls_made, 1)
                nc.gpsimd.tensor_tensor(posb[:, :, :], posb[:, :, :],
                                        view(b2[:, :], [[0, SIDE], [1, DIM]]), ALU.add).then_inc(posb_made, 1)
                pool.wait_ge(cls_made, 1)
                pool.dma_start(hidden0[:, 0:2, :], cls[:, :, :]).then_inc(cls_out, 16)
                pool.wait_ge(posb_made, 1)
                with pool.Fori(0, GROUPS // 2) as pair:
                    gg = pair * 2
                    for s in range(2):
                        g = gg + s
                        pool.wait_ge(rows_out[s], gg * (8 * GB) + PRIMED)
                        for wv in range(SIDE):
                            v = wv % 2
                            t = g * SIDE + wv
                            pool.wait_ge(yn_made, t + 1 + PRIMED)
                            nc.gpsimd.tensor_tensor(yg[:, v, :], yn[:, v, :], g2[:, :], ALU.mult).then_inc(pool_step, 1)
                            pool.wait_ge(pool_step, t + 1)
                            nc.gpsimd.tensor_tensor(rows[:, s, wv, :], yg[:, v, :], posb[:, wv, :], ALU.add).then_inc(row_made, 1)
                pool.wait_ge(cls_out, 16)

            @block.vector
            def _(dve):
                dve.wait_ge(consts_in, 16 * CONSTS)
                nc.vector.memset(eps[:, :], EPS)
                for k in range(KC):
                    ins = nc.vector.tensor_copy(b1x[:, k, :], b1[:, k % 2, k // 2:k // 2 + 1].broadcast_to([128, P]))
                ins.then_inc(b1x_made, 1)
                dve.wait_ge(bias_full, 1)
                nc.vector.tensor_tensor(bias[:, :], y_bank[0][0:P, 0:DIM], bias[:, :], ALU.add)
                for k in range(KC):
                    ins = nc.vector.tensor_scalar(w[:, k % 2, k // 2, :], w[:, k % 2, k // 2, :], g1[:, k % 2, k // 2:k // 2 + 1], None, ALU.mult)
                ins.then_inc(w_scaled, 1)
                dve.wait_ge(w_scaled, 1)

                def front(g, s, wv, t, st):
                    v = wv % 2
                    px = pixels[:, s, :, :].rearrange("p c (y w z) -> p c y w z", w=SIDE, z=PATCH)[:, :, :, wv, :]
                    for c in range(CH):
                        ins = nc.vector.bn_stats(stat1[:, v, c, :], px[:, c, :, :])
                    st.did(ins)
                    st.settle_apart(passed)
                    nc.vector.bn_aggr(mv1[:, v, :], stat1[:, v, :, :]).then_inc(mv1_made, 1)
                    dve.wait_ge(sd1_made, t + 1)
                    st.did(nc.vector.reciprocal(sd1[:, v, :], sd1[:, v, :]))
                    st.settle()
                    if wv >= 2:
                        dve.wait_ge(turned, t - 1 + PRIMED)
                    else:
                        dve.wait_ge(turned, g * SIDE + PRIMED)
                    nc.vector.tensor_scalar(normed[:, v, :].rearrange("p (c y z) -> p c y z", c=CH, z=PATCH), px,
                                            mv1[:, v, 0:1], sd1[:, v, :], ALU.subtract, ALU.mult).then_inc(normed_made, 1)

                def back(wv, t, st):
                    v = wv % 2
                    dve.wait_ge(projected, t + 1)
                    st.did(nc.vector.tensor_tensor(y[:, v, :], y_bank[v][0:P, 0:DIM], bias[:, :], ALU.add))
                    st.settle()
                    st.did(nc.vector.bn_stats(stat2[:, v, :], y[:, v, :]))
                    st.settle_apart(passed)
                    nc.vector.bn_aggr(mv2[:, v, :], stat2[:, v, :]).then_inc(mv2_made, 1)
                    dve.wait_ge(sd2_made, t + 1)
                    st.did(nc.vector.reciprocal(sd2[:, v, :], sd2[:, v, :]))
                    st.settle()
                    if wv >= 2:
                        dve.wait_ge(row_made, t - 1 + PRIMED)
                    nc.vector.tensor_scalar(yn[:, v, :], y[:, v, :], mv2[:, v, 0:1], sd2[:, v, :],
                                            ALU.subtract, ALU.mult).then_inc(yn_made, 1)

                PER_GROUP = SIDE * 5
                with dve.Fori(0, GROUPS // 2) as pair:
                    gg = pair * 2
                    for s in range(2):
                        g = gg + s
                        st = Steps(dve, dve_step, g * PER_GROUP)
                        dve.wait_ge(pixels_in[s], gg * (8 * GB) + 16 * GB)
                        dve.wait_ge(row_made, g * SIDE + PRIMED)
                        for wv in range(SIDE + 1):
                            if wv < SIDE:
                                front(g, s, wv, g * SIDE + wv, st)
                            if wv:
                                back(wv - 1, g * SIDE + wv - 1, st)
                        assert st.n == PER_GROUP

            @block.tensor
            def _(pe):
                pe.wait_ge(b1x_made, 1)
                for k in range(KC):
                    ins = nc.tensor.matmul(y_bank[0][0:P, 0:DIM], b1x[:, k, :], w[:, k % 2, k // 2, :], start=(k == 0), stop=(k == KC - 1))
                ins.then_inc(bias_full, 1)
                pe.wait_ge(w_scaled, 1)
                pe.wait_ge(ident_made, 2)

                def turn(wv, t, g):
                    v = wv % 2
                    pe.wait_ge(normed_made, t + 1)
                    if wv >= 2:
                        pe.wait_ge(patchT_made, t - 1 + PRIMED)
                    else:
                        pe.wait_ge(patchT_made, g * SIDE + PRIMED)
                    for k in range(KC):
                        ins = nc.tensor.transpose(t_bank[v][k // 3][:, (k % 3) * P:(k % 3 + 1) * P],
                                                  normed[:, v, 128 * k:128 * (k + 1)], ident[0:P, 0:P])
                    ins.then_inc(turned, 1)

                def project(wv, t, g):
                    v = wv % 2
                    pe.wait_ge(patchT_made, t + 1 + PRIMED)
                    if wv >= 2:
                        pe.wait_ge(yn_made, t - 1 + PRIMED)
                    else:
                        pe.wait_ge(yn_made, g * SIDE + PRIMED)
                    for k in range(KC):
                        ins = nc.tensor.matmul(y_bank[v][0:P, 0:DIM], patchT[:, v, k, :], w[:, k % 2, k // 2, :],
                                               start=(k == 0), stop=(k == KC - 1))
                    ins.then_inc(projected, 1)

                with pe.Fori(0, GROUPS) as g:
                    for wv in range(SIDE + 1):
                        if wv < SIDE:
                            turn(wv, g * SIDE + wv, g)
                        if wv:
                            project(wv - 1, g * SIDE + wv - 1, g)


def attention_stage(nc, hidden0, qkv_w, proj_w, proj_b, tab_kv, tab_kh, tab_vv, tab_vh, hidden1):
    ROWS = 30
    EXT = 32
    NG = 30
    CLSG = 15
    HC = 396
    BANKJOBS = 4
    U_JOBS = 14
    G_JOBS = 4 + PAIRS * U_JOBS + 4
    PERB = TILES
    with ExitStack() as ctx:
        m = Memory(nc, ctx, "att")
        hid = m.sb("hid", [HALF, TILES, DIM])
        resid = m.sb("resid", [HALF, TILES, DIM])
        norm = m.sb("norm", [HALF, TILES, DIM])
        xT0, xT1 = m.sb("xT0", [C0, GT]), m.sb("xT1", [C1, GT])
        wT0, wT1 = m.sb("wT0", [C0, 3, PAIRS, 128]), m.sb("wT1", [C1, 3, PAIRS, 128])
        w0, w1 = m.sb("w0", [C0, 3, 128]), m.sb("w1", [C1, 3, 128])
        pw = m.sb("pw", [128, PAIRS, DIM])
        pbias = m.sb("pbias", [HALF, DIM])
        raw = m.sb("raw", [128, 2, HEADS * HD])
        q2 = m.sb("q2", [128, GT])
        qx, kx = m.sb("qx", [128, 2, GT]), m.sb("kx", [128, 2, GT])
        vx = m.sb("vx", [HALF, TILES, 160])
        oT = m.sb("oT", [128, PAIRS, GT])
        rx = m.sb("rx", [96, GT])
        tq = m.sb("tq", [128, NG, 96])
        tv = m.sb("tv", [96, NG, 128])
        tabT = m.sb("tabT", [128, 2, ROWS])
        onehot = m.sb("onehot", [EXT, 1 + 15 * SIDE])
        rowhot = m.sb("rowhot", [EXT, 1 + 15 * SIDE])
        ident = m.sb("ident", [128, 128])
        prob = m.sb("prob", [HALF, 2, 2, NTOK])
        probT = m.sb("probT", [HALF, 2, 2 * NTOK])
        peak, npeak, total = m.sb("peak", [HALF, 2, 2]), m.sb("npeak", [HALF, 2, 2]), m.sb("total", [HALF, 2, 2])
        stat, mv, sd = m.sb("stat", [HALF, TILES, 6]), m.sb("mv", [HALF, TILES, 2]), m.sb("sd", [HALF, TILES, 1])
        eps = m.sb("eps", [128, 1])
        mv_made, sd_made = m.sem("mv_made"), m.sem("sd_made")
        p_bank = [m.bank(f"p{i}") for i in range(2)]
        s_bank = [m.bank(f"s{i}") for i in range(2)]
        t_bank = [m.bank(f"t{i}") for i in range(2)]
        o_bank = [m.bank(f"o{i}") for i in range(2)]
        consts_in, onehot_made, zeroed = m.sem("consts_in"), m.sem("onehot_made"), m.sem("zeroed")
        tables_in, tables_made, raw_in = m.sem("tables_in"), m.sem("tables_made"), [m.sem(f"raw_in{i}") for i in range(2)]
        hid_in, resid_made = m.sem("hid_in"), m.sem("resid_made")
        norm_made, dve_step, passed = m.sem("norm_made"), m.sem("dve_step"), m.sem("passed")
        full = [m.sem(f"full{i}") for i in range(2)]
        free = [m.sem(f"free{i}") for i in range(2)]
        prep_full, prep_free = m.sem("prep_full"), m.sem("prep_free")
        w_made = m.sem("w_made")
        scores, peaks, exps, probs, turned, probT_made, outs, outs_used = (
            m.sem("scores"), m.sem("peaks"), m.sem("exps"), m.sem("probs"), m.sem("turned"), m.sem("probT_made"),
            m.sem("outs"), m.sem("outs_used"))
        hidden_out = m.sem("hidden_out")

        h0_tiles = hidden0.rearrange("b (h p) d -> p (b h) d", p=HALF)
        h1_tiles = hidden1.rearrange("b (h p) d -> p (b h) d", p=HALF)
        QROWS = 3 * HEADS * HD

        def q_cols(a):
            if a < CLSG:
                row = 14 - a
                return 1 + SIDE * row, (SIDE if row < SIDE else 1), 1
            if a == CLSG:
                return 0, 1, 1
            return 1 + (13 - (a - 16)), SIDE, SIDE

        def group_rhs(src, a):
            off, n, step = q_cols(a)
            return view(src, [[NTOK, GB], [step, n]], off)

        ROWBANKS = [[(CLSG, 0)] + [(14 - r, 1 + SIDE * r) for r in range(4)],
                    [(14 - r, SIDE * (r - 4)) for r in range(4, 8)],
                    [(14 - r, SIDE * (r - 8)) for r in range(8, 12)],
                    [(14 - r, SIDE * (r - 12)) for r in range(12, 15)]]
        ROWSPAN = [(0, 57), (57, 56), (113, 56), (169, 29)]
        COLBANKS = [range(0, 4), range(4, 8), range(8, 12), range(12, 14)]

        def prep_jobs():
            return [("qkv", t) for t in range(QROWS // 128)] + [("proj", p) for p in range(PAIRS)]

        with nc.Block() as block:

            @block.sync
            def _(sp):
                for s in (hidden_out, scores, *free):
                    sp.sem_inc(s, PRIMED)
                sp.dma_start(hid[:, :, :], h0_tiles[:, 0:TILES, :]).then_inc(hid_in, 16)
                with sp.Fori(0, GROUPS - 1) as g:
                    sp.wait_ge(norm_made, (g + 1) * GB)
                    sp.wait_ge(resid_made, g + 1)
                    sp.dma_start(hid[:, :, :], h0_tiles[:, bass.ds((g + 1) * TILES, TILES), :]).then_inc(hid_in, 16)
                    for bank in range(2):
                        sp.wait_ge(free[bank], (g + 1) * G_JOBS + PRIMED)
                    sp.dma_start(h1_tiles[:, bass.ds(g * TILES, TILES), :], resid[:, :, :]).then_inc(hidden_out, 16)
                for bank in range(2):
                    sp.wait_ge(free[bank], GROUPS * G_JOBS + PRIMED)
                sp.dma_start(h1_tiles[:, (GROUPS - 1) * TILES:, :], resid[:, :, :]).then_inc(hidden_out, 16)
                sp.wait_ge(hidden_out, 16 * GROUPS + PRIMED)

            @block.gpsimd
            def _(pool):
                for t in (qx, kx, rx, tq, tv):
                    ins = nc.gpsimd.memset(t[:], 0.0)
                ins.then_inc(zeroed, 1)
                make_identity(pool, nc, ident, onehot_made)
                W = 1 + 15 * SIDE
                nc.gpsimd.memset(onehot[:, :], 0.0)
                nc.gpsimd.memset(rowhot[:, :], 1.0).then_inc(onehot_made, 1)
                cols = onehot[:, 1:W].rearrange("p (r c) -> p r c", c=SIDE)
                for n, (dst, pattern, base, mult, op, fill) in enumerate((
                        (cols, [[0, 15], [1, SIDE]], 16, -1, ALU.not_equal, 1.0),
                        (onehot[:, 0:1], [[0, 1]], -15, 1, ALU.not_equal, 1.0),
                        (onehot[:, 0:1], [[0, 1]], -30, 1, ALU.not_equal, 1.0),
                        (rowhot[:, :], [[1, W]], -1, -SIDE, ALU.is_ge, 0.0),
                        (rowhot[:, :], [[-1, W]], SIDE, SIDE, ALU.is_ge, 0.0))):
                    pool.wait_ge(onehot_made, 3 + n)
                    nc.gpsimd.affine_select(out=dst, in_=dst, compare_op=op, fill=fill, base=base, pattern=pattern,
                                            channel_multiplier=mult).then_inc(onehot_made, 1)
                pool.wait_ge(onehot_made, 8)
                nc.gpsimd.tensor_tensor(onehot[:, :], onehot[:, :], rowhot[:, :], ALU.add).then_inc(onehot_made, 1)

                pool.wait_ge(zeroed, 1)
                for half, head in ((64, 0), (32, 1)):
                    def rows_of(p, n, a, na, tab, first, astep):
                        pool.dma_start(tv[half + p:half + p + n, a:a + na, 64 * head:64 * head + 64],
                                       bass.AP(tensor=tab.tensor, offset=tab.offset + first * HD,
                                               ap=[[HD if astep >= 0 else 0, n], [max(astep, 0) * HD, na], [1, HD]])
                                       ).then_inc(tables_in, 16)
                    rows_of(0, 15, 0, 15, tab_vv, 1, 1)
                    rows_of(15, 1, 0, 15, tab_vv, 0, 0)
                    rows_of(0, 16, CLSG, 1, tab_vv, 0, -1)
                    rows_of(16, 15, CLSG, 1, tab_vh, 0, -1)
                    rows_of(16, 14, 0, 1, tab_vh, 15, 0)
                    rows_of(30, 1, 0, 1, tab_vh, 0, 0)
                    rows_of(16, 14, 16, 14, tab_vh, 2, 1)
                    rows_of(30, 1, 16, 14, tab_vh, 0, 0)
                for half in range(2):
                    for i, tab in enumerate((tab_kv, tab_kh)):
                        with nc.allow_non_contiguous_dma(reason="a small table, transposed"):
                            pool.dma_start(tabT[64 * half:64 * half + 64, i, :], tab.rearrange("r d -> d r")).then_inc(consts_in, 16)
                pool.dma_start(pbias[:, :], bass.AP(tensor=proj_b.tensor, offset=proj_b.offset, ap=[[0, HALF], [1, DIM]])
                               ).then_inc(consts_in, 16)
                pool.wait_ge(tables_in, 16 * 16)
                pool.wait_ge(consts_in, 16 * 5)
                pool.wait_ge(prep_free, len(prep_jobs()))

                with pool.Fori(0, GROUPS) as g:
                    pool.wait_ge(hid_in, g * 16 + 16)
                    pool.wait_ge(hidden_out, g * 16 + PRIMED)
                    nc.gpsimd.tensor_tensor(resid[:, :, :], hid[:, :, :], view(pbias[:, :], [[0, TILES], [1, DIM]]),
                                            ALU.add).then_inc(resid_made, 1)
                    with pool.Fori(0, PAIRS) as p:
                        u = g * PAIRS + p
                        pool.wait_ge(scores, u * PERB + PRIMED)
                        nc.gpsimd.tensor_copy(w0[:, :, :], wT0[:, :, bass.ds(p, 1), :].rearrange("p k a n -> p k (a n)"))
                        nc.gpsimd.tensor_copy(w1[:, :, :], wT1[:, :, bass.ds(p, 1), :].rearrange("p k a n -> p k (a n)")
                                              ).then_inc(w_made, 1)

            @block.scalar
            def _(act):
                for n, (kind, t) in enumerate(prep_jobs()):
                    if n >= 2:
                        act.wait_ge(prep_full, n - 1)
                    dst = raw[:, n % 2, :]
                    if kind == "qkv":
                        act.dma_start(dst[:, 0:DIM], qkv_w[128 * t:128 * t + 128, :]).then_inc(raw_in[n % 2], 16)
                    else:
                        act.dma_start(dst[:, 0:128], proj_w[0:128, 128 * t:128 * t + 128]).then_inc(raw_in[n % 2], 16)
                        act.dma_start(dst[0:C1, 128:256], proj_w[128:DIM, 128 * t:128 * t + 128]).then_inc(raw_in[n % 2], 16)

                def read(bank, value):
                    act.wait_ge(full[bank], value)

                with act.Fori(0, GROUPS) as g:
                    act.wait_ge(mv_made, g + 1)
                    nc.scalar.activation(sd[:, :, :], mv[:, :, 1:2], ACT.Sqrt, bias=eps[0:HALF, :]).then_inc(sd_made, 1)
                    base = g * G_JOBS
                    for j in range(BANKJOBS):
                        read(0, base + j + 1)
                        cols = slice(2 * j * NTOK, 2 * j * NTOK + NTOK)
                        nc.scalar.activation(xT0[:, cols], p_bank[0][:, 0:NTOK], ACT.Copy)
                        nc.scalar.activation(xT1[:, cols], p_bank[0][0:C1, NTOK:2 * NTOK], ACT.Copy).then_inc(free[0], 1)
                    with act.Fori(0, PAIRS) as p:
                        u = g * PAIRS + p
                        at = base + BANKJOBS + p * U_JOBS
                        for j in range(2):
                            read(0, at + j + 1)
                            cols = slice(2 * j * HC, 2 * j * HC + HC)
                            nc.scalar.activation(q2[:, cols], p_bank[0][:, 0:HC], ACT.Copy)
                            nc.scalar.activation(qx[0:64, 0, cols], p_bank[0][0:64, 0:HC], ACT.Copy)
                            nc.scalar.activation(qx[64:128, 1, cols], p_bank[0][64:128, 0:HC], ACT.Copy).then_inc(free[0], 1)
                        for j in range(2):
                            read(0, at + 2 + j + 1)
                            cols = slice(2 * j * HC, 2 * j * HC + HC)
                            nc.scalar.activation(kx[0:64, 0, cols], p_bank[0][0:64, 0:HC], ACT.Copy)
                            nc.scalar.activation(kx[64:128, 1, cols], p_bank[0][64:128, 0:HC], ACT.Copy).then_inc(free[0], 1)
                        for j in (0, 2):
                            read(0, at + 4 + j // 2 + 1)
                            first, n = ROWSPAN[j]
                            for lo, head in ((64, 0), (32, 1)):
                                ins = nc.scalar.activation(view(qx[lo:lo + 32, head, :], [[NTOK, GB], [1, n]], first),
                                                           view(p_bank[0][lo:lo + 32, :], [[n, GB], [1, n]]), ACT.Copy)
                            ins.then_inc(free[0], 1)
                        for j in range(2):
                            read(0, at + 8 + j + 1)
                            nc.scalar.activation(view(vx[:, 8 * j:8 * j + 4, :], [[160, 4], [96, 2], [1, HD]]),
                                                 view(p_bank[0][0:HALF, :], [[128, 4], [HD, 2], [1, HD]]), ACT.Copy
                                                 ).then_inc(free[0], 1)
                        for i in range(PERB + 2):
                            n = u * PERB + i
                            if i < PERB:
                                act.wait_ge(peaks, n + 1)
                                if i >= 2:
                                    act.wait_ge(turned, n - 1)
                                for h in range(2):
                                    ins = nc.scalar.activation(prob[:, i % 2, h, :], s_bank[i % 2][0:HALF, h * NTOK:(h + 1) * NTOK],
                                                               ACT.Exp, bias=npeak[:, i % 2, h:h + 1], scale=SCALE,
                                                               accum_out=total[:, i % 2, h:h + 1])
                                ins.then_inc(exps, 1)
                            if i >= 2:
                                j = i - 2
                                act.wait_ge(turned, n - 2 + 1)
                                if j >= 2:
                                    act.wait_ge(outs, n - 2 - 1)
                                nc.scalar.activation(probT[:, j % 2, :], t_bank[j % 2][0:HALF, 0:2 * NTOK], ACT.Copy
                                                     ).then_inc(probT_made, 1)

            @block.vector
            def _(dve):
                nc.vector.memset(eps[:, :], EPS)
                dve.wait_ge(consts_in, 16 * 5)
                dve.wait_ge(zeroed, 1)
                for lo, at in ((0, 64), (64, 32)):
                    src = tabT[lo:lo + 64, :, :]

                    def table(a, na, col, n, which, first, cstep, astep):
                        nc.vector.tensor_copy(tq[lo:lo + 64, a:a + na, at + col:at + col + n],
                                              view(src, [[astep, na], [cstep, n]], which * ROWS + first))
                    table(0, 15, 0, 15, 0, 1, 1, 1)
                    table(0, 15, 15, 1, 0, 0, 0, 0)
                    table(CLSG, 1, 0, 16, 0, 0, 0, 0)
                    table(CLSG, 1, 16, 15, 1, 0, 0, 0)
                    table(0, 1, 16, 14, 1, 15, 1, 0)
                    table(0, 1, 30, 1, 1, 0, 0, 0)
                    table(16, 14, 16, 14, 1, 2, 1, 1)
                    table(16, 14, 30, 1, 1, 0, 0, 0)
                dve.wait_ge(onehot_made, 9)
                for lo, head in ((64, 0), (32, 1)):
                    ins = nc.vector.tensor_copy(view(kx[lo:lo + 32, head, :], [[NTOK, GB], [1, NTOK]]),
                                                view(onehot[:, :], [[0, GB], [1, NTOK]]))
                ins.then_inc(tables_made, 1)
                for n, (kind, t) in enumerate(prep_jobs()):
                    dve.wait_ge(prep_full, n + 1)
                    bank = p_bank[n % 2]
                    if kind == "qkv":
                        nc.vector.tensor_copy(wT0[:, t // 6, t % 6, :], bank[:, 0:128])
                        nc.vector.tensor_copy(wT1[:, t // 6, t % 6, :], bank[0:C1, 128:256]).then_inc(prep_free, 1)
                    else:
                        nc.vector.tensor_copy(pw[:, t, 0:DIM], bank[:, 0:DIM]).then_inc(prep_free, 1)
                for h in range(2):
                    dve.wait_ge(prep_full, 1 + h + len(prep_jobs()))
                    ins = nc.vector.tensor_copy(view(vx[:, h:h + 1, 64:96], [[2 * 160, GB], [1, EXT]]),
                                                view(s_bank[h][0:HALF, 0:EXT], [[0, GB], [1, EXT]]))
                ins.then_inc(tables_made, 1)

                K_GROUP = 2
                K_UNIT = 2 * PERB
                PER_GROUP = K_GROUP + PAIRS * K_UNIT
                with dve.Fori(0, GROUPS) as g:
                    st = Steps(dve, dve_step, g * PER_GROUP)
                    dve.wait_ge(hid_in, g * 16 + 16)
                    for t in range(TILES):
                        ins = nc.vector.bn_stats(stat[:, t, :], hid[:, t, :])
                    st.did(ins)
                    st.settle_apart(passed)
                    for t in range(TILES):
                        ins = nc.vector.bn_aggr(mv[:, t, :], stat[:, t, :])
                    ins.then_inc(mv_made, 1)
                    dve.wait_ge(sd_made, g + 1)
                    st.did(nc.vector.reciprocal(sd[:, :, :], sd[:, :, :]))
                    st.settle()
                    for t in range(TILES):
                        ins = nc.vector.tensor_scalar(norm[:, t, :], hid[:, t, :], mv[:, t, 0:1], sd[:, t, :],
                                                      ALU.subtract, ALU.mult)
                        if t % 2:
                            ins.then_inc(norm_made, 1)
                    dve.wait_ge(norm_made, (g + 1) * 8)
                    base = g * G_JOBS
                    for j in range(BANKJOBS):
                        dve.wait_ge(full[1], base + j + 1)
                        cols = slice((2 * j + 1) * NTOK, (2 * j + 2) * NTOK)
                        nc.vector.tensor_copy(xT0[:, cols], p_bank[1][:, 0:NTOK])
                        nc.vector.tensor_copy(xT1[:, cols], p_bank[1][0:C1, NTOK:2 * NTOK]).then_inc(free[1], 1)
                    with dve.Fori(0, PAIRS) as p:
                        u = g * PAIRS + p
                        us = Steps(dve, dve_step, g * PER_GROUP + K_GROUP + p * K_UNIT)
                        at = base + BANKJOBS + p * U_JOBS
                        for j in range(2):
                            dve.wait_ge(full[1], at + j + 1)
                            cols = slice((2 * j + 1) * HC, (2 * j + 2) * HC)
                            nc.vector.tensor_copy(q2[:, cols], p_bank[1][:, 0:HC])
                            nc.vector.tensor_copy(qx[0:64, 0, cols], p_bank[1][0:64, 0:HC])
                            nc.vector.tensor_copy(qx[64:128, 1, cols], p_bank[1][64:128, 0:HC]).then_inc(free[1], 1)
                        for j in range(2):
                            dve.wait_ge(full[1], at + 2 + j + 1)
                            cols = slice((2 * j + 1) * HC, (2 * j + 2) * HC)
                            nc.vector.tensor_copy(kx[0:64, 0, cols], p_bank[1][0:64, 0:HC])
                            nc.vector.tensor_copy(kx[64:128, 1, cols], p_bank[1][64:128, 0:HC]).then_inc(free[1], 1)
                        for j in (1, 3):
                            dve.wait_ge(full[1], at + 4 + j // 2 + 1)
                            first, n = ROWSPAN[j]
                            for lo, head in ((64, 0), (32, 1)):
                                ins = nc.vector.tensor_copy(view(qx[lo:lo + 32, head, :], [[NTOK, GB], [1, n]], first),
                                                            view(p_bank[1][lo:lo + 32, :], [[n, GB], [1, n]]))
                            ins.then_inc(free[1], 1)
                        dve.wait_ge(free[0], at + 4 + 2 + PRIMED)
                        dve.wait_ge(free[1], at + 4 + 2 + PRIMED)
                        for j, span in enumerate(COLBANKS):
                            bank = p_bank[j % 2]
                            dve.wait_ge(full[j % 2], at + 6 + j // 2 + 1)
                            n = len(span)
                            for lo, head in ((64, 0), (32, 1)):
                                dst = view(qx[lo:lo + 32, head, :], [[NTOK, GB], [SIDE, SIDE], [1, n]], 1 + span[0])
                                ins = nc.vector.tensor_tensor(
                                    dst, view(bank[lo:lo + 32, :], [[n * SIDE, GB], [1, SIDE], [SIDE, n]]), dst, ALU.add)
                            ins.then_inc(free[j % 2], 1)
                        for j in range(2):
                            dve.wait_ge(full[1], at + 8 + j + 1)
                            nc.vector.tensor_copy(view(vx[:, 8 * j + 4:8 * j + 8, :], [[160, 4], [96, 2], [1, HD]]),
                                                  view(p_bank[1][0:HALF, :], [[128, 4], [HD, 2], [1, HD]])).then_inc(free[1], 1)
                        for i in range(PERB + 3):
                            n = u * PERB + i
                            if i < PERB:
                                dve.wait_ge(scores, n + 1 + PRIMED)
                                us.did(nc.vector.tensor_reduce(peak[:, i % 2, :], s_bank[i % 2][0:HALF, 0:2 * NTOK].rearrange(
                                    "p (h k) -> p h k", h=2), AX.X, ALU.max))
                                us.settle()
                                nc.vector.tensor_scalar(npeak[:, i % 2, :], peak[:, i % 2, :], -SCALE, None, ALU.mult
                                                        ).then_inc(peaks, 1)
                            if 1 <= i <= PERB:
                                j = i - 1
                                dve.wait_ge(exps, n - 1 + 1)
                                us.did(nc.vector.reciprocal(total[:, j % 2, :], total[:, j % 2, :]))
                                us.settle()
                                for h in range(2):
                                    ins = nc.vector.tensor_scalar(prob[:, j % 2, h, :], prob[:, j % 2, h, :],
                                                                  total[:, j % 2, h:h + 1], None, ALU.mult)
                                ins.then_inc(probs, 1)
                            if i >= 3:
                                j = i - 3
                                b, head = j // 2, j % 2
                                dve.wait_ge(outs, n - 3 + 1)
                                cols = slice(b * NTOK, (b + 1) * NTOK)
                                lo = 64 * head
                                ext = 32 if head else 64
                                nc.vector.tensor_copy(oT[lo:lo + 64, bass.ds(p, 1), cols].rearrange("p a n -> p (a n)"),
                                                      o_bank[j % 2][lo:lo + 64, 0:NTOK])
                                nc.vector.tensor_copy(rx[ext:ext + 32, cols], o_bank[j % 2][ext:ext + 32, 0:NTOK]
                                                      ).then_inc(outs_used, 1)
                        dve.wait_ge(outs_used, (u + 1) * PERB)
                        for j in range(4):
                            bank, (first, n) = p_bank[j % 2], ROWSPAN[j]
                            dve.wait_ge(full[j % 2], at + 10 + j // 2 + 1)
                            dst = view(oT[:, bass.ds(p, 1), :], [[NTOK, GB], [1, n]], first)
                            ins = nc.vector.tensor_tensor(dst, view(bank[:, :], [[n, GB], [1, n]]), dst, ALU.add)
                            ins.then_inc(free[j % 2], 1)
                        dve.wait_ge(free[0], at + 12 + PRIMED)
                        dve.wait_ge(free[1], at + 12 + PRIMED)
                        for j, span in enumerate(COLBANKS):
                            bank, n = p_bank[j % 2], len(span)
                            dve.wait_ge(full[j % 2], at + 12 + j // 2 + 1)
                            dst = view(oT[:, bass.ds(p, 1), :], [[NTOK, GB], [SIDE, SIDE], [1, n]], 1 + span[0])
                            nc.vector.tensor_tensor(dst, view(bank[:, :], [[n * SIDE, GB], [1, SIDE], [SIDE, n]]), dst, ALU.add
                                                    ).then_inc(free[j % 2], 1)
                        assert us.n == K_UNIT
                    at = base + BANKJOBS + PAIRS * U_JOBS
                    dve.wait_ge(resid_made, g + 1)
                    for j in range(8):
                        dve.wait_ge(full[j % 2], at + j // 2 + 1)
                        dst = resid[:, 2 * j:2 * j + 2, :]
                        ins = nc.vector.tensor_tensor(dst, p_bank[j % 2][0:HALF, 0:2 * DIM].rearrange("p (t d) -> p t d", t=2),
                                                      dst, ALU.add)
                        ins.then_inc(free[j % 2], 1)
                    assert st.n == K_GROUP

            @block.tensor
            def _(pe):
                pe.wait_ge(onehot_made, 9)
                for n, (kind, t) in enumerate(prep_jobs()):
                    pe.wait_ge(raw_in[n % 2], 16 * sum(1 if k == "qkv" else 2 for k, _ in prep_jobs()[n % 2:n + 1:2]))
                    if n >= 2:
                        pe.wait_ge(prep_free, n - 1)
                    src, bank = raw[:, n % 2, :], p_bank[n % 2]
                    if kind == "qkv":
                        nc.tensor.transpose(bank[:, 0:128], src[:, 0:C0], ident[:, :])
                        ins = nc.tensor.transpose(bank[0:C1, 128:256], src[:, C0:DIM], ident[:, :])
                    else:
                        nc.tensor.transpose(bank[:, 0:128], src[:, 0:128], ident[:, :])
                        ins = nc.tensor.transpose(bank[:, 128:DIM], src[0:C1, 128:256], ident[0:C1, 0:C1])
                    ins.then_inc(prep_full, 1)
                for h in range(2):
                    nc.tensor.transpose(s_bank[h][0:HALF, 0:EXT], onehot[:, h * HALF:(h + 1) * HALF], ident[0:EXT, 0:EXT]
                                        ).then_inc(prep_full, 1)
                pe.wait_ge(prep_free, len(prep_jobs()))
                pe.wait_ge(tables_made, 2)
                pe.wait_ge(tables_in, 16 * 16)

                with pe.Fori(0, GROUPS) as g:
                    base = g * G_JOBS
                    for j in range(8):
                        pe.wait_ge(norm_made, g * 8 + j + 1)
                        pe.wait_ge(free[j % 2], base + j // 2 + PRIMED)
                        bank = p_bank[j % 2]
                        for t in range(2):
                            src = norm[:, 2 * j + t, :]
                            nc.tensor.transpose(bank[:, t * HALF:(t + 1) * HALF], src[:, 0:C0], ident[0:HALF, 0:HALF])
                            ins = nc.tensor.transpose(bank[0:C1, NTOK + t * HALF:NTOK + (t + 1) * HALF], src[:, C0:DIM],
                                                      ident[0:HALF, 0:HALF])
                        ins.then_inc(full[j % 2], 1)
                    pe.wait_ge(free[0], base + 4 + PRIMED)
                    pe.wait_ge(free[1], base + 4 + PRIMED)
                    pe.sem_inc(passed, 1)
                    with pe.Fori(0, PAIRS) as p:
                        u = g * PAIRS + p
                        at = base + BANKJOBS + p * U_JOBS

                        def job(k):
                            pe.wait_ge(free[k % 2], at + k // 2 + PRIMED)
                            return p_bank[k % 2]

                        pe.wait_ge(w_made, u + 1)
                        for kind in range(2):
                            for j in range(4):
                                bank = job(4 * kind + j)
                                cols = slice(j * HC, (j + 1) * HC)
                                nc.tensor.matmul(bank[:, 0:HC], w0[:, kind, :], xT0[:, cols], start=True, stop=False)
                                nc.tensor.matmul(bank[:, 0:HC], w1[:, kind, :], xT1[:, cols], start=False, stop=True
                                                 ).then_inc(full[j % 2], 1)
                        pe.wait_ge(free[0], at + 2 + PRIMED)
                        pe.wait_ge(free[1], at + 2 + PRIMED)
                        for j, span in enumerate(ROWBANKS):
                            bank, n = job(8 + j), ROWSPAN[j][1]
                            for a, col in span:
                                ins = nc.tensor.matmul(view(bank[0:96, :], [[n, GB], [1, q_cols(a)[1]]], col), tq[:, a, :],
                                                       group_rhs(q2[:, :], a), start=True, stop=True)
                            ins.then_inc(full[j % 2], 1)
                        for j, span in enumerate(COLBANKS):
                            bank, n = job(12 + j), len(span)
                            for i, c in enumerate(span):
                                ins = nc.tensor.matmul(view(bank[0:96, :], [[n * SIDE, GB], [1, SIDE]], i * SIDE), tq[:, 16 + 13 - c, :],
                                                       group_rhs(q2[:, :], 16 + 13 - c), start=True, stop=True)
                            ins.then_inc(full[j % 2], 1)
                        for j in range(4):
                            bank = job(16 + j)
                            for t in range(4):
                                cols = slice((4 * j + t) * HALF, (4 * j + t + 1) * HALF)
                                out = bank[0:HALF, t * 128:(t + 1) * 128]
                                nc.tensor.matmul(out, xT0[:, cols], w0[:, 2, :], start=True, stop=False)
                                ins = nc.tensor.matmul(out, xT1[:, cols], w1[:, 2, :], start=False, stop=True)
                            ins.then_inc(full[j % 2], 1)
                        pe.wait_ge(free[0], at + 10 + PRIMED)
                        pe.wait_ge(free[1], at + 10 + PRIMED)
                        for i in range(PERB + 3):
                            n = u * PERB + i
                            if i < PERB:
                                b, head = i // 2, i % 2
                                K = 128 if head else 96
                                if i >= 2:
                                    pe.wait_ge(exps, n - 1)
                                for h in range(2):
                                    q0 = b * NTOK + h * HALF
                                    ins = nc.tensor.matmul(s_bank[i % 2][0:HALF, h * NTOK:(h + 1) * NTOK],
                                                           qx[0:K, head, q0:q0 + HALF], kx[0:K, head, b * NTOK:(b + 1) * NTOK],
                                                           start=True, stop=True)
                                ins.then_inc(scores, 1)
                            if 2 <= i < PERB + 2:
                                j = i - 2
                                pe.wait_ge(probs, n - 2 + 1)
                                if j >= 2:
                                    pe.wait_ge(probT_made, n - 2 - 1)
                                for k in range(2):
                                    for h in range(2):
                                        ins = nc.tensor.transpose(
                                            t_bank[j % 2][0:HALF, k * NTOK + h * HALF:k * NTOK + (h + 1) * HALF],
                                            prob[:, j % 2, h, k * HALF:(k + 1) * HALF], ident[0:HALF, 0:HALF])
                                ins.then_inc(turned, 1)
                            if i >= 3:
                                j = i - 3
                                b, head = j // 2, j % 2
                                M, v0 = (128, 32) if head else (96, 0)
                                pe.wait_ge(probT_made, n - 3 + 1)
                                if j >= 2:
                                    pe.wait_ge(outs_used, n - 3 - 1)
                                for k in range(2):
                                    ins = nc.tensor.matmul(o_bank[j % 2][0:M, 0:NTOK], vx[:, 2 * b + k, v0:v0 + M],
                                                           probT[:, j % 2, k * NTOK:(k + 1) * NTOK],
                                                           start=(k == 0), stop=(k == 1))
                                ins.then_inc(outs, 1)
                        pe.wait_ge(outs_used, (u + 1) * PERB)
                        for j, span in enumerate(ROWBANKS):
                            bank, n = job(20 + j), ROWSPAN[j][1]
                            for a, col in span:
                                ins = nc.tensor.matmul(view(bank[:, :], [[n, GB], [1, q_cols(a)[1]]], col), tv[:, a, :],
                                                       group_rhs(rx[:, :], a), start=True, stop=True)
                            ins.then_inc(full[j % 2], 1)
                        for j, span in enumerate(COLBANKS):
                            bank, n = job(24 + j), len(span)
                            for i, c in enumerate(span):
                                ins = nc.tensor.matmul(view(bank[:, :], [[n * SIDE, GB], [1, SIDE]], i * SIDE), tv[:, 16 + 13 - c, :],
                                                       group_rhs(rx[:, :], 16 + 13 - c), start=True, stop=True)
                            ins.then_inc(full[j % 2], 1)
                    at = base + BANKJOBS + PAIRS * U_JOBS
                    pe.wait_ge(free[0], at + PRIMED)
                    pe.wait_ge(free[1], at + PRIMED)
                    for j in range(8):
                        bank = p_bank[j % 2]
                        pe.wait_ge(free[j % 2], at + j // 2 + PRIMED)
                        for t in range(2):
                            cols = slice((2 * j + t) * HALF, (2 * j + t + 1) * HALF)
                            for p in range(PAIRS):
                                ins = nc.tensor.matmul(bank[0:HALF, t * DIM:(t + 1) * DIM], oT[:, p, cols], pw[:, p, :],
                                                       start=(p == 0), stop=(p == PAIRS - 1))
                        ins.then_inc(full[j % 2], 1)


def experts_stage(nc, hidden1, w_fc_sh, w_proj_sh, w1, w2, router_w, balance_bias, out):
    TB = 3
    BT = TB * 128
    BLOCKS = B * NTOK // BT
    MLPS = EXPERTS + 1
    HID = MLPS * DIM
    HT = (HID + 127) // 128
    with ExitStack() as ctx:
        m = Memory(nc, ctx, "ffn")
        hid = m.sb("hid", [128, 2, TB, DIM])
        norm = m.sb("norm", [128, TB, DIM])
        acc = m.sb("acc", [128, 2, TB, DIM])
        xT0, xT1 = m.sb("xT0", [C0, 2, BT]), m.sb("xT1", [C1, 2, BT])
        up0, up1 = m.sb("up0", [C0, HID]), m.sb("up1", [C1, HID])
        down = m.sb("down", [128, HT, DIM])
        hidden = m.sb("hidden", [128, HT, BT])
        relu = m.sb("relu", [128, 4, BT])
        rw0, rw1 = m.sb("rw0", [C0, EXPERTS]), m.sb("rw1", [C1, EXPERTS])
        bb, ranks = m.sb("bb", [128, EXPERTS]), m.sb("ranks", [128, EXPERTS])
        ident = m.sb("ident", [128, 128])
        stat, mv, sd = m.sb("stat", [128, TB, 6]), m.sb("mv", [128, TB, 2]), m.sb("sd", [128, TB, 1])
        eps = m.sb("eps", [128, 1])
        mv_made, sd_made = m.sem("mv_made"), m.sem("sd_made")
        expo, sc, sb_, eq, first, left, second, weight, gate = (m.sb(n, [128, TB, EXPERTS]) for n in (
            "expo", "score", "biased", "eq", "first", "left", "second", "weight", "gate"))
        top = m.sb("top", [128, TB, 1])
        t_bank = [m.bank(f"t{i}") for i in range(2)]
        h_bank = [m.bank(f"h{i}") for i in range(2)]
        y_bank = [m.bank(f"y{i}") for i in range(3)]
        r_bank = m.bank("r")
        w_in, ranks_made, hid_in = m.sem("w_in"), m.sem("ranks_made"), [m.sem(f"hid_in{i}") for i in range(2)]
        norm_made, turned, xT_made, dve_step = m.sem("norm_made"), m.sem("turned"), m.sem("xT_made"), m.sem("dve_step")
        routed, expo_made, passed = m.sem("routed"), m.sem("expo_made"), m.sem("passed")
        up_done, relu_made, squared = m.sem("up_done"), [m.sem(f"relu_made{i}") for i in range(2)], m.sem("squared")
        down_done, summed, acc_out = m.sem("down_done"), m.sem("summed"), [m.sem(f"acc_out{i}") for i in range(2)]
        h_tiles = hidden1.rearrange("b n d -> (b n) d").rearrange("(t p) d -> p t d", p=128)
        o_tiles = out.rearrange("b n d -> (b n) d").rearrange("(t p) d -> p t d", p=128)
        DOWNS = [(EXPERTS, [(12, 0, 128), (13, 0, 64)])]
        for i in range(EXPERTS // 2):
            DOWNS += [(2 * i, [(3 * i, 0, 128), (3 * i + 1, 0, 64)]), (2 * i + 1, [(3 * i + 2, 0, 128), (3 * i + 1, 64, 64)])]
        UPS = [12, 13] + list(range(12))

        with nc.Block() as block:

            @block.sync
            def _(sp):
                for s in (down_done, turned, *acc_out, xT_made, *relu_made, summed):
                    sp.sem_inc(s, PRIMED)
                def load(it, s):
                    sp.dma_start(hid[:, s, :, :], h_tiles[:, bass.ds(it * TB, TB), :]).then_inc(hid_in[s], 16)

                def store(it, s):
                    sp.wait_ge(summed, (it + 1) * TB * MLPS + PRIMED)
                    sp.dma_start(o_tiles[:, bass.ds(it * TB, TB), :], acc[:, s, :, :]).then_inc(acc_out[s], 16)
                load(0, 0)
                load(1, 1)
                with sp.Fori(0, (BLOCKS - 3) // 2) as pair:
                    ii = pair * 2
                    for s in range(2):
                        store(ii + s, s)
                        load(ii + s + 2, s)
                store(BLOCKS - 3, 0)
                load(BLOCKS - 1, 0)
                store(BLOCKS - 2, 1)
                store(BLOCKS - 1, 0)
                sp.wait_ge(acc_out[0], 16 * (BLOCKS // 2 + 1) + PRIMED)
                sp.wait_ge(acc_out[1], 16 * (BLOCKS // 2) + PRIMED)

            @block.gpsimd
            def _(pool):
                make_identity(pool, nc, ident, ranks_made)
                nc.gpsimd.iota(ranks[:, :], [[-1, EXPERTS]], base=EXPERTS, channel_multiplier=0,
                               allow_small_or_imprecise_dtypes=True).then_inc(ranks_made, 1)
                for e in range(EXPERTS):
                    pool.dma_start(up0[:, e * DIM:(e + 1) * DIM], w1[e, 0:C0, :]).then_inc(w_in, 16)
                    pool.dma_start(up1[:, e * DIM:(e + 1) * DIM], w1[e, C0:DIM, :]).then_inc(w_in, 16)
                pool.dma_start(up0[:, EXPERTS * DIM:], w_fc_sh[0:C0, :]).then_inc(w_in, 16)
                pool.dma_start(up1[:, EXPERTS * DIM:], w_fc_sh[C0:DIM, :]).then_inc(w_in, 16)
                pool.dma_start(down[:, 0:12, :], w2.rearrange("e h d -> (e h) d").rearrange("(t p) d -> p t d", p=128)).then_inc(w_in, 16)
                pool.dma_start(down[:, 12, :], w_proj_sh[0:128, :]).then_inc(w_in, 16)
                pool.dma_start(down[0:64, 13, :], w_proj_sh[128:DIM, :]).then_inc(w_in, 16)
                with nc.allow_non_contiguous_dma(reason="a small weight, transposed"):
                    pool.dma_start(rw0[:, :], router_w[:, 0:C0].rearrange("e c -> c e")).then_inc(w_in, 16)
                    pool.dma_start(rw1[:, :], router_w[:, C0:DIM].rearrange("e c -> c e")).then_inc(w_in, 16)
                pool.dma_start(bb[:, :], bass.AP(tensor=balance_bias.tensor, offset=balance_bias.offset,
                                                 ap=[[0, 128], [1, EXPERTS]])).then_inc(w_in, 16)
                pool.wait_ge(w_in, 16 * (2 * MLPS + 6))
                with pool.Fori(0, BLOCKS) as it:
                    pool.wait_ge(down_done, it * TB * MLPS + PRIMED)
                    for n in range(HT):
                        j = UPS[n]
                        rows = 64 if j == 13 else 128
                        pool.wait_ge(relu_made[n % 2], it * (HT // 2) + n // 2 + 1 + PRIMED)
                        nc.gpsimd.tensor_tensor(hidden[0:rows, j, :], relu[0:rows, n % 4, :], relu[0:rows, n % 4, :], ALU.mult
                                                ).then_inc(squared, 1)

            @block.scalar
            def _(act):
                def turn_copy(k, s):
                    act.wait_ge(mv_made, k + 1)
                    nc.scalar.activation(sd[:, :, :], mv[:, :, 1:2], ACT.Sqrt, bias=eps[:, :]).then_inc(sd_made, 1)
                    act.wait_ge(turned, k + 1 + PRIMED)
                    nc.scalar.activation(xT0[:, s, :], t_bank[0][:, 0:BT], ACT.Copy)
                    nc.scalar.activation(xT1[:, s, :], t_bank[1][0:C1, 0:BT], ACT.Copy).then_inc(xT_made, 1)

                def body(it, s, last=False):
                    act.wait_ge(routed, it + 1)
                    nc.scalar.activation(expo[:, :, :], r_bank[:, 0:TB * EXPERTS].rearrange("p (t e) -> p t e", t=TB),
                                         ACT.Exp, scale=-1.0).then_inc(expo_made, 1)
                    for n in range(HT // 2):
                        act.wait_ge(up_done, it * HT + 2 * n + 1)
                        if n >= 2:
                            act.wait_ge(squared, it * HT + 2 * n - 3)
                        nc.scalar.activation(relu[:, 2 * n % 4, :], h_bank[0][:, 0:BT], ACT.Relu).then_inc(relu_made[0], 1)
                    if not last:
                        turn_copy(it + 1, 1 - s)

                turn_copy(0, 0)
                with act.Fori(0, (BLOCKS - 1) // 2) as pair:
                    ii = pair * 2
                    body(ii, 0)
                    body(ii + 1, 1)
                body(BLOCKS - 1, 0, last=True)

            @block.vector
            def _(dve):
                def layernorm(k, s, st):
                    for t in range(TB):
                        ins = nc.vector.bn_stats(stat[:, t, :], hid[:, s, t, :])
                    st.did(ins)
                    st.settle_apart(passed)
                    for t in range(TB):
                        ins = nc.vector.bn_aggr(mv[:, t, :], stat[:, t, :])
                    ins.then_inc(mv_made, 1)
                    dve.wait_ge(sd_made, k + 1)
                    st.did(nc.vector.reciprocal(sd[:, :, :], sd[:, :, :]))
                    st.settle()
                    dve.wait_ge(turned, k + PRIMED)
                    for t in range(TB):
                        ins = nc.vector.tensor_scalar(norm[:, t, :], hid[:, s, t, :], mv[:, t, 0:1], sd[:, t, :],
                                                      ALU.subtract, ALU.mult)
                    ins.then_inc(norm_made, 1)

                def route(it, st):
                    def step(ins):
                        st.did(ins)
                        st.settle()

                    def wide(ap):
                        return view(ap, [[1, TB], [0, EXPERTS]])

                    def const(ap):
                        return view(ap, [[0, TB], [1, EXPERTS]])

                    dve.wait_ge(expo_made, it + 1)
                    step(nc.vector.tensor_scalar(expo[:, :, :], expo[:, :, :], 1.0, None, ALU.add))
                    step(nc.vector.reciprocal(sc[:, :, :], expo[:, :, :]))
                    step(nc.vector.tensor_tensor(sb_[:, :, :], sc[:, :, :], const(bb[:, :]), ALU.add))
                    cur = sb_
                    for pick in (first, second):
                        step(nc.vector.tensor_reduce(top[:, :, 0], cur[:, :, :], AX.X, ALU.max))
                        step(nc.vector.tensor_tensor(eq[:, :, :], cur[:, :, :], wide(top[:, :, 0]), ALU.is_equal))
                        step(nc.vector.tensor_tensor(eq[:, :, :], eq[:, :, :], const(ranks[:, :]), ALU.mult))
                        step(nc.vector.tensor_reduce(top[:, :, 0], eq[:, :, :], AX.X, ALU.max))
                        step(nc.vector.tensor_tensor(pick[:, :, :], eq[:, :, :], wide(top[:, :, 0]), ALU.is_equal))
                        if pick is first:
                            step(nc.vector.scalar_tensor_tensor(left[:, :, :], first[:, :, :], -1e30, sb_[:, :, :], ALU.mult, ALU.add))
                            cur = left
                    step(nc.vector.tensor_tensor(eq[:, :, :], first[:, :, :], second[:, :, :], ALU.add))
                    step(nc.vector.tensor_tensor(weight[:, :, :], eq[:, :, :], sc[:, :, :], ALU.mult))
                    step(nc.vector.reduce_sum(top[:, :, 0], weight[:, :, :], AX.X))
                    step(nc.vector.tensor_scalar(top[:, :, :], top[:, :, :], 1e-20, None, ALU.add))
                    step(nc.vector.reciprocal(top[:, :, :], top[:, :, :]))
                    step(nc.vector.tensor_tensor(gate[:, :, :], weight[:, :, :], wide(top[:, :, 0]), ALU.mult))

                R = 20
                KI = 2 + R

                def relus(it):
                    for n in range(HT // 2):
                        rows = 64 if UPS[2 * n + 1] == 13 else 128
                        dve.wait_ge(up_done, it * HT + 2 * n + 2)
                        if n >= 2:
                            dve.wait_ge(squared, it * HT + 2 * n - 2)
                        nc.vector.tensor_scalar(relu[0:rows, (2 * n + 1) % 4, :], h_bank[1][0:rows, 0:BT], 0.0, None, ALU.max
                                                ).then_inc(relu_made[1], 1)

                def sums(it, s, k):
                    e = DOWNS[k][0]
                    for t in range(TB):
                        n = it * TB * MLPS + k * TB + t
                        dve.wait_ge(down_done, n + 1 + PRIMED)
                        y = y_bank[t][:, 0:DIM]
                        if k == 0:
                            nc.vector.tensor_tensor(acc[:, s, t, :], y, hid[:, s, t, :], ALU.add).then_inc(summed, 1)
                        else:
                            if t == 0:
                                dve.wait_ge(summed, it * TB * MLPS + k * TB + PRIMED)
                            nc.vector.scalar_tensor_tensor(acc[:, s, t, :], y, gate[:, t, e:e + 1], acc[:, s, t, :],
                                                           ALU.mult, ALU.add).then_inc(summed, 1)

                def body(it, s, stores, next_loaded):
                    st = Steps(dve, dve_step, 2 + it * KI)
                    route(it, st)
                    relus(it)
                    dve.wait_ge(acc_out[s], stores + PRIMED)
                    for k in range(3):
                        sums(it, s, k)
                    if next_loaded is not None:
                        dve.wait_ge(hid_in[1 - s], next_loaded)
                        layernorm(it + 1, 1 - s, st)
                        assert st.n == KI, st.n
                    for k in range(3, MLPS):
                        sums(it, s, k)

                dve.wait_ge(w_in, 16 * (2 * MLPS + 6))
                dve.wait_ge(ranks_made, 3)
                nc.vector.memset(eps[:, :], EPS)
                dve.wait_ge(hid_in[0], 16)
                layernorm(0, 0, Steps(dve, dve_step, 0))
                with dve.Fori(0, (BLOCKS - 1) // 2) as pair:
                    ii = pair * 2
                    for s in range(2):
                        body(ii + s, s, ii * 8, ii * 8 + 16 * (s + 1))
                body(BLOCKS - 1, 0, 16 * (BLOCKS // 2), None)

            @block.tensor
            def _(pe):
                def turn(k):
                    pe.wait_ge(norm_made, k + 1)
                    pe.wait_ge(xT_made, k + PRIMED)
                    for t in range(TB):
                        cols = slice(t * 128, (t + 1) * 128)
                        nc.tensor.transpose(t_bank[0][:, cols], norm[:, t, 0:C0], ident[:, :])
                        ins = nc.tensor.transpose(t_bank[1][0:C1, cols], norm[:, t, C0:DIM], ident[:, :])
                    ins.then_inc(turned, 1)

                def up(it, s, n):
                    j = UPS[n]
                    rows = 64 if j == 13 else 128
                    if n % 2 == 0:
                        pe.wait_ge(relu_made[0], it * (HT // 2) + n // 2 + PRIMED)
                    else:
                        pe.wait_ge(relu_made[1], it * (HT // 2) + n // 2 + PRIMED)
                    o = h_bank[n % 2][0:rows, 0:BT]
                    nc.tensor.matmul(o, up0[:, 128 * j:128 * j + rows], xT0[:, s, :], start=True, stop=False)
                    nc.tensor.matmul(o, up1[:, 128 * j:128 * j + rows], xT1[:, s, :], start=False, stop=True).then_inc(up_done, 1)

                def down_(it, k):
                    for t in range(TB):
                        n = it * TB * MLPS + k * TB + t
                        if k:
                            pe.wait_ge(summed, n - TB + 1 + PRIMED)
                        else:
                            pe.wait_ge(summed, it * TB * MLPS + PRIMED)
                        parts = DOWNS[k][1]
                        for i, (j, r0, rows) in enumerate(parts):
                            ins = nc.tensor.matmul(y_bank[t][:, 0:DIM], hidden[r0:r0 + rows, j, t * 128:(t + 1) * 128],
                                                   down[r0:r0 + rows, j, :], start=(i == 0), stop=(i == len(parts) - 1))
                        ins.then_inc(down_done, 1)

                def body(it, s, last=False):
                    pe.wait_ge(xT_made, it + 1 + PRIMED)
                    for t in range(TB):
                        cols = slice(t * 128, (t + 1) * 128)
                        o = r_bank[:, t * EXPERTS:(t + 1) * EXPERTS]
                        nc.tensor.matmul(o, xT0[:, s, cols], rw0[:, :], start=True, stop=False)
                        ins = nc.tensor.matmul(o, xT1[:, s, cols], rw1[:, :], start=False, stop=True)
                    ins.then_inc(routed, 1)
                    for n in range(HT):
                        up(it, s, n)
                    pe.wait_ge(squared, (it + 1) * HT)
                    for k in range(3):
                        down_(it, k)
                    if not last:
                        turn(it + 1)
                    for k in range(3, MLPS):
                        down_(it, k)

                pe.wait_ge(w_in, 16 * (2 * MLPS + 6))
                pe.wait_ge(ranks_made, 2)
                turn(0)
                with pe.Fori(0, (BLOCKS - 1) // 2) as pair:
                    ii = pair * 2
                    body(ii, 0)
                    body(ii + 1, 1)
                body(BLOCKS - 1, 0, last=True)


def vit_tower(nc, x, cls_tok, ln1_g, ln1_b, w_proj, b_proj, ln2_g, ln2_b, pos, cls_token, qkv_w, proj_w, proj_b,
              tab_kv, tab_kh, tab_vv, tab_vh, w_fc_sh, w_proj_sh, w1, w2, router_w, balance_bias, out):
    hidden0 = nc.dram_tensor("hidden0", [B, NTOK, DIM], fp32, kind="Internal").ap()
    hidden1 = nc.dram_tensor("hidden1", [B, NTOK, DIM], fp32, kind="Internal").ap()
    tokens_stage(nc, x, cls_tok, ln1_g, ln1_b, w_proj, b_proj, ln2_g, ln2_b, pos, cls_token, hidden0)
    attention_stage(nc, hidden0, qkv_w, proj_w, proj_b, tab_kv, tab_kh, tab_vv, tab_vh, hidden1)
    experts_stage(nc, hidden1, w_fc_sh, w_proj_sh, w1, w2, router_w, balance_bias, out)


_INS = ['x', 'cls_tok', 'L0_tok_ln1_g', 'L0_tok_ln1_b', 'L0_tok_W_proj', 'L0_tok_b_proj', 'L0_tok_ln2_g',
        'L0_tok_ln2_b', 'L0_tok_pos_embedding', 'L0_tok_cls_token', 'L0_attn_qkv_w', 'L0_attn_proj_w',
        'L0_attn_proj_b', 'L0_attn_tab_kv', 'L0_attn_tab_kh', 'L0_attn_tab_vv', 'L0_attn_tab_vh',
        'L0_ffn_w_fc_sh', 'L0_ffn_w_proj_sh', 'L0_ffn_w1', 'L0_ffn_w2', 'L0_ffn_router_w', 'L0_ffn_balance_bias']


def kernel(**inputs):
    import concourse.bacc as bacc
    from concourse.bass_utils import run_bass_kernel_spmd

    nc = bacc.Bacc("TRN2", target_bir_lowering=False, num_devices=1)
    arrays, args = {}, []
    for name in _INS:
        a = np.ascontiguousarray(inputs[name])
        arrays[f"in_{name}"] = a
        args.append(nc.dram_tensor(f"in_{name}", a.shape, mybir.dt.from_np(a.dtype), kind="ExternalInput").ap())
    args.append(nc.dram_tensor("out_hidden", (B, NTOK, DIM), fp32, kind="ExternalOutput").ap())
    vit_tower(nc, *args)
    r = run_bass_kernel_spmd(nc, [arrays], core_ids=[0])
    return r.results[0]["out_hidden"]
```

```python
import numpy as np
import concourse.bass as bass
from concourse import mybir
from contextlib import ExitStack

fp32 = mybir.dt.float32
ALU = mybir.AluOpType
ACT = mybir.ActivationFunctionType
AX = mybir.AxisListType

B, CH, IMG, PATCH = 64, 3, 224, 16
SIDE = IMG // PATCH
NTOK = SIDE * SIDE + 2
DIM = 192
PDIM = PATCH * PATCH * CH
HEADS, HD = 12, 64
PAIRS = HEADS // 2
EXPERTS = 8
EPS = 1e-5
SCALE = HD ** -0.5
GB = 8
GROUPS = B // GB
GT = GB * NTOK
HALF = NTOK // 2
TILES = 2 * GB
PRIMED = 1
C0, C1 = 128, DIM - 128


class Steps:

    def __init__(self, eng, sem, base=0):
        self.eng, self.sem, self.base, self.n = eng, sem, base, 0

    def did(self, ins):
        ins.then_inc(self.sem, 1)
        self.n += 1

    def settle(self):
        self.eng.wait_ge(self.sem, self.base + self.n)

    def settle_apart(self, passed):
        self.settle()
        self.eng.sem_inc(passed, 1)


class Memory:

    def __init__(self, nc, ctx, stage):
        self.nc, self.ctx, self.stage = nc, ctx, stage

    def sb(self, name, shape, dt=fp32):
        return self.ctx.enter_context(self.nc.sbuf_tensor(f"{self.stage}_{name}", shape, dt))

    def bank(self, name):
        return self.ctx.enter_context(self.nc.psum_tensor(f"{self.stage}_{name}", [128, 512], fp32))

    def sem(self, name):
        return self.ctx.enter_context(self.nc.semaphore(f"{self.stage}_{name}"))


def view(ap, dims, offset=0):
    return bass.AP(tensor=ap.tensor, offset=ap.offset + offset, ap=[list(ap.ap[0])] + [list(d) for d in dims])


def make_identity(pool, nc, ident, sem):
    nc.gpsimd.memset(ident[:, :], 0.0).then_inc(sem, 1)
    pool.wait_ge(sem, 1)
    nc.gpsimd.affine_select(out=ident[:, :], in_=ident[:, :], compare_op=ALU.not_equal, fill=1.0, base=0,
                            pattern=[[-1, 128]], channel_multiplier=1).then_inc(sem, 1)


def tokens_stage(nc, x, cls_tok, ln1_g, ln1_b, w_proj, b_proj, ln2_g, ln2_b, pos, cls_token, hidden0):
    P = GB * SIDE
    KC = PDIM // 128
    XROW = PATCH * IMG
    with ExitStack() as ctx:
        m = Memory(nc, ctx, "tok")
        pixels = m.sb("pixels", [P, 2, CH, XROW])
        normed = m.sb("normed", [P, 2, PDIM])
        patchT = m.sb("patchT", [128, 2, KC, P])
        w = m.sb("w", [128, 2, CH, DIM])
        g1, b1 = m.sb("g1", [128, 2, CH]), m.sb("b1", [128, 2, CH])
        b1x = m.sb("b1x", [128, KC, P])
        bias = m.sb("bias", [P, DIM])
        g2, b2 = m.sb("g2", [P, DIM]), m.sb("b2", [P, DIM])
        posb = m.sb("posb", [P, SIDE, DIM])
        eps = m.sb("eps", [128, 1])
        stat1, mv1 = m.sb("stat1", [P, SIDE, CH, 6]), m.sb("mv1", [P, SIDE, 2])
        rstd1, shift1 = m.sb("rstd1", [P, SIDE, 1]), m.sb("shift1", [P, SIDE, 1])
        stat2, mv2, rstd2 = m.sb("stat2", [P, SIDE, 6]), m.sb("mv2", [P, SIDE, 2]), m.sb("rstd2", [P, SIDE, 1])
        y = m.sb("y", [P, SIDE, DIM])
        rows = m.sb("rows", [P, 2, SIDE, DIM])
        cls = m.sb("cls", [B, 2, DIM])
        clsp = m.sb("clsp", [B, DIM])
        ident = m.sb("ident", [128, 128])
        t_bank = [[m.bank(f"t{v}{i}") for i in range(2)] for v in range(2)]
        y_bank = [m.bank(f"y{v}") for v in range(2)]
        pixels_in = [m.sem(f"pixels_in{s}") for s in range(2)]
        consts_in, ident_made = m.sem("consts_in"), m.sem("ident_made")
        bias_full, w_scaled = m.sem("bias_full"), m.sem("w_scaled")
        dve_step, pool_step, passed = m.sem("dve_step"), m.sem("pool_step"), m.sem("passed")
        mv1_made, sd1_made, shift1_made = m.sem("mv1_made"), m.sem("sd1_made"), m.sem("shift1_made")
        mv2_made, sd2_made, y_made = m.sem("mv2_made"), m.sem("sd2_made"), m.sem("y_made")
        normed_made, turned, patchT_made, projected = (m.sem("normed_made"), m.sem("turned"), m.sem("patchT_made"),
                                                       m.sem("projected"))
        rows_normed, rows_made = m.sem("rows_normed"), m.sem("rows_made")
        rows_out = [m.sem(f"rows_out{s}") for s in range(2)]
        b1x_made, cls_made, cls_out, posb_made = m.sem("b1x_made"), m.sem("cls_made"), m.sem("cls_out"), m.sem("posb_made")
        x_rows = x.rearrange("b c (r p) w -> b r c (p w)", p=PATCH)
        hid_rows = hidden0[:, 2:NTOK, :].rearrange("b (r w) d -> b r w d", w=SIDE)
        CONSTS = 3 + 3 + GB + 3

        with nc.Block() as block:

            @block.sync
            def _(sp):
                for s in (*rows_out, turned, patchT_made, y_made, rows_normed):
                    sp.sem_inc(s, PRIMED)
                def load(g, s):
                    for j in range(GB):
                        sp.dma_start(pixels[SIDE * j:SIDE * (j + 1), s, :, :],
                                     x_rows[bass.ds(g * GB + j, 1)].rearrange("a r c n -> (a r) c n")
                                     ).then_inc(pixels_in[s], 16)
                def store(g, s):
                    sp.wait_ge(rows_made, g + 1)
                    for j in range(GB):
                        sp.dma_start(hid_rows[bass.ds(g * GB + j, 1)].rearrange("a r w d -> (a r) w d"),
                                     rows[SIDE * j:SIDE * (j + 1), s, :, :]).then_inc(rows_out[s], 16)

                load(0, 0)
                load(1, 1)
                with sp.Fori(0, (GROUPS - 2) // 2) as pair:
                    gg = pair * 2
                    for s in range(2):
                        sp.wait_ge(normed_made, (gg + s + 1) * SIDE)
                        load(gg + s + 2, s)
                        store(gg + s, s)
                sp.sem_inc(pixels_in[0], 16 * GB)
                for s in range(2):
                    store(GROUPS - 2 + s, s)
                for s in range(2):
                    sp.wait_ge(rows_out[s], 16 * GB * (GROUPS // 2) + PRIMED)

            @block.scalar
            def _(act):
                act.wait_ge(b1x_made, 1)

                def deviation1(n):
                    act.wait_ge(mv1_made, n)
                    nc.scalar.activation(rstd1[:, :, :], mv1[:, :, 1:2], ACT.Sqrt, bias=eps[0:P, :]).then_inc(sd1_made, 1)

                def normalise(s, wv, t):
                    v = wv % 2
                    if wv >= 2:
                        act.wait_ge(turned, t - 1 + PRIMED)
                    px = view(pixels[:, s, 0, :], [[IMG, CH * PATCH], [1, PATCH]], wv * PATCH)
                    nc.scalar.activation(view(normed[:, v, :], [[PATCH, CH * PATCH], [1, PATCH]]), px, ACT.Identity,
                                         bias=shift1[:, wv, :], scale=rstd1[:, wv, :]).then_inc(normed_made, 1)

                deviation1(1)
                with act.Fori(0, GROUPS // 2) as pair:
                    gg = pair * 2
                    for s in range(2):
                        g = gg + s
                        act.wait_ge(shift1_made, g + 1)
                        normalise(s, 0, g * SIDE)
                        for wv in range(SIDE):
                            v, t = wv % 2, g * SIDE + wv
                            if wv + 1 < SIDE:
                                normalise(s, wv + 1, t + 1)
                            act.wait_ge(turned, t + 1 + PRIMED)
                            for i in range(2):
                                ins = nc.scalar.activation(patchT[:, v, 3 * i:3 * i + 3, :],
                                                           t_bank[v][i][:, 0:3 * P].rearrange("p (k n) -> p k n", k=3),
                                                           ACT.Copy)
                            ins.then_inc(patchT_made, 1)
                        deviation1(g + 2)
                        act.wait_ge(mv2_made, g + 1)
                        nc.scalar.activation(rstd2[:, :, :], mv2[:, :, 1:2], ACT.Sqrt, bias=eps[0:P, :]).then_inc(sd2_made, 1)

            @block.gpsimd
            def _(pool):
                make_identity(pool, nc, ident, ident_made)
                pool.dma_start(w[:, :, :, :], w_proj.rearrange("(h q c) d -> q h c d", q=128, c=CH)).then_inc(consts_in, 16)
                for dst, src in ((g1, ln1_g), (b1, ln1_b)):
                    pool.dma_start(dst[:, :, :], src.rearrange("(h q c) -> q h c", q=128, c=CH)).then_inc(consts_in, 16)
                for dst, src in ((bias, b_proj), (g2, ln2_g), (b2, ln2_b)):
                    pool.dma_start(dst[:, :], bass.AP(tensor=src.tensor, offset=src.offset, ap=[[0, P], [1, DIM]])
                                   ).then_inc(consts_in, 16)
                for j in range(GB):
                    pool.dma_start(posb[SIDE * j:SIDE * (j + 1), :, :],
                                   pos[0, 1:SIDE * SIDE + 1, :].rearrange("(r w) d -> r w d", w=SIDE)).then_inc(consts_in, 16)
                for dst, src in ((cls[:, 0, :], cls_tok[0, 0, :]), (cls[:, 1, :], cls_token[0, 0, :]), (clsp[:, :], pos[0, 0, :])):
                    pool.dma_start(dst, bass.AP(tensor=src.tensor, offset=src.offset, ap=[[0, B], [1, DIM]])
                                   ).then_inc(consts_in, 16)
                pool.wait_ge(consts_in, 16 * CONSTS)
                nc.gpsimd.tensor_tensor(cls[:, 1, :], cls[:, 1, :], clsp[:, :], ALU.add).then_inc(cls_made, 1)
                nc.gpsimd.tensor_tensor(posb[:, :, :], posb[:, :, :],
                                        view(b2[:, :], [[0, SIDE], [1, DIM]]), ALU.add).then_inc(posb_made, 1)
                pool.wait_ge(cls_made, 1)
                pool.dma_start(hidden0[:, 0:2, :], cls[:, :, :]).then_inc(cls_out, 16)
                pool.wait_ge(posb_made, 1)
                with pool.Fori(0, GROUPS // 2) as pair:
                    gg = pair * 2
                    for s in range(2):
                        g = gg + s
                        pool.wait_ge(rows_normed, g + 1 + PRIMED)
                        nc.gpsimd.tensor_tensor(rows[:, s, :, :], rows[:, s, :, :], view(g2[:, :], [[0, SIDE], [1, DIM]]), ALU.mult
                                                ).then_inc(pool_step, 1)
                        pool.wait_ge(pool_step, g + 1)
                        nc.gpsimd.tensor_tensor(rows[:, s, :, :], rows[:, s, :, :], posb[:, :, :], ALU.add).then_inc(rows_made, 1)
                pool.wait_ge(cls_out, 16)

            @block.vector
            def _(dve):
                dve.wait_ge(consts_in, 16 * CONSTS)
                nc.vector.memset(eps[:, :], EPS)
                for k in range(KC):
                    ins = nc.vector.tensor_copy(b1x[:, k, :], b1[:, k % 2, k // 2:k // 2 + 1].broadcast_to([128, P]))
                ins.then_inc(b1x_made, 1)
                dve.wait_ge(bias_full, 1)
                nc.vector.tensor_tensor(bias[:, :], y_bank[0][0:P, 0:DIM], bias[:, :], ALU.add)
                for k in range(KC):
                    ins = nc.vector.tensor_scalar(w[:, k % 2, k // 2, :], w[:, k % 2, k // 2, :], g1[:, k % 2, k // 2:k // 2 + 1], None, ALU.mult)
                ins.then_inc(w_scaled, 1)
                dve.wait_ge(w_scaled, 1)

                def statistics1(s, wv):
                    px = view(pixels[:, s, 0, :], [[IMG, CH * PATCH], [1, PATCH]], wv * PATCH)
                    for c in range(CH):
                        ins = nc.vector.bn_stats(stat1[:, wv, c, :], view(pixels[:, s, c, :], [[IMG, PATCH], [1, PATCH]], wv * PATCH))
                    return ins

                def aggregate(st, mv, stat, made):
                    st.settle_apart(passed)
                    for wv in range(SIDE):
                        ins = nc.vector.bn_aggr(mv[:, wv, :], stat[:, wv, :, :] if len(stat.shape) == 4 else stat[:, wv, :])
                    ins.then_inc(made, 1)

                def scale_shift1(st, n):
                    dve.wait_ge(sd1_made, n)
                    st.did(nc.vector.reciprocal(rstd1[:, :, :], rstd1[:, :, :]))
                    st.settle()
                    nc.vector.scalar_tensor_tensor(shift1[:, :, :], mv1[:, :, 0:1], -1.0, rstd1[:, :, :], ALU.mult, ALU.mult
                                                   ).then_inc(shift1_made, 1)

                st = Steps(dve, dve_step, 0)
                dve.wait_ge(pixels_in[0], 16 * GB)
                for wv in range(SIDE):
                    ins = statistics1(0, wv)
                st.did(ins)
                aggregate(st, mv1, stat1, mv1_made)
                scale_shift1(st, 1)
                PER_GROUP = SIDE + 3
                with dve.Fori(0, GROUPS // 2) as pair:
                    gg = pair * 2
                    for s in range(2):
                        g = gg + s
                        st = Steps(dve, dve_step, 2 + g * PER_GROUP)
                        dve.wait_ge(pixels_in[1 - s], gg * (8 * GB) + 16 * GB * (s + 1))
                        dve.wait_ge(rows_normed, g + PRIMED)
                        for wv in range(SIDE + 1):
                            t = g * SIDE + wv - 1
                            if wv:
                                dve.wait_ge(projected, t + 1)
                                nc.vector.tensor_tensor(y[:, wv - 1, :], y_bank[(wv - 1) % 2][0:P, 0:DIM], bias[:, :], ALU.add
                                                        ).then_inc(y_made, 1)
                            if wv < SIDE:
                                ins = statistics1(1 - s, wv)
                                if wv == SIDE - 1:
                                    st.did(ins)
                            if wv:
                                dve.wait_ge(y_made, t + 1 + PRIMED)
                                st.did(nc.vector.bn_stats(stat2[:, wv - 1, :], y[:, wv - 1, :]))
                        dve.wait_ge(normed_made, (g + 1) * SIDE)
                        aggregate(st, mv1, stat1, mv1_made)
                        aggregate(st, mv2, stat2, mv2_made)
                        scale_shift1(st, g + 2)
                        dve.wait_ge(sd2_made, g + 1)
                        st.did(nc.vector.reciprocal(rstd2[:, :, :], rstd2[:, :, :]))
                        st.settle()
                        dve.wait_ge(rows_out[s], gg * (8 * GB) + PRIMED)
                        for wv in range(SIDE):
                            ins = nc.vector.tensor_scalar(rows[:, s, wv, :], y[:, wv, :], mv2[:, wv, 0:1], rstd2[:, wv, :],
                                                          ALU.subtract, ALU.mult)
                            if wv == SIDE - 1:
                                ins.then_inc(rows_normed, 1)
                        assert st.n == PER_GROUP, st.n

            @block.tensor
            def _(pe):
                pe.wait_ge(b1x_made, 1)
                for k in range(KC):
                    ins = nc.tensor.matmul(y_bank[0][0:P, 0:DIM], b1x[:, k, :], w[:, k % 2, k // 2, :], start=(k == 0), stop=(k == KC - 1))
                ins.then_inc(bias_full, 1)
                pe.wait_ge(w_scaled, 1)
                pe.wait_ge(ident_made, 2)

                def turn(wv, t, g):
                    v = wv % 2
                    pe.wait_ge(normed_made, t + 1)
                    if wv >= 2:
                        pe.wait_ge(patchT_made, t - 1 + PRIMED)
                    else:
                        pe.wait_ge(patchT_made, g * SIDE + PRIMED)
                    for k in range(KC):
                        ins = nc.tensor.transpose(t_bank[v][k // 3][:, (k % 3) * P:(k % 3 + 1) * P],
                                                  normed[:, v, 128 * k:128 * (k + 1)], ident[0:P, 0:P])
                    ins.then_inc(turned, 1)

                def project(wv, t, g):
                    v = wv % 2
                    pe.wait_ge(patchT_made, t + 1 + PRIMED)
                    if wv >= 2:
                        pe.wait_ge(y_made, t - 1 + PRIMED)
                    else:
                        pe.wait_ge(y_made, g * SIDE + PRIMED)
                    for k in range(KC):
                        ins = nc.tensor.matmul(y_bank[v][0:P, 0:DIM], patchT[:, v, k, :], w[:, k % 2, k // 2, :],
                                               start=(k == 0), stop=(k == KC - 1))
                    ins.then_inc(projected, 1)

                with pe.Fori(0, GROUPS) as g:
                    for wv in range(SIDE + 1):
                        if wv < SIDE:
                            turn(wv, g * SIDE + wv, g)
                        if wv:
                            project(wv - 1, g * SIDE + wv - 1, g)


def attention_stage(nc, hidden0, qkv_w, proj_w, proj_b, tab_kv, tab_kh, tab_vv, tab_vh, hidden1):
    ROWS = 30
    EXT = 32
    NG = 30
    CLSG = 15
    HC = 396
    UNIT = TILES
    STEPS = PAIRS * UNIT
    TURN, FIRST, LAST = 8, 20, 16
    with ExitStack() as ctx:
        m = Memory(nc, ctx, "att")
        hid = m.sb("hid", [HALF, TILES, DIM])
        resid = m.sb("resid", [HALF, TILES, DIM])
        norm = m.sb("norm", [HALF, 4, DIM])
        xT0, xT1 = m.sb("xT0", [C0, GT]), m.sb("xT1", [C1, GT])
        wT0, wT1 = m.sb("wT0", [C0, 3, PAIRS, 128]), m.sb("wT1", [C1, 3, PAIRS, 128])
        pw = m.sb("pw", [128, PAIRS, DIM])
        pbias = m.sb("pbias", [HALF, DIM])
        raw = m.sb("raw", [128, 2, 256])
        q2 = m.sb("q2", [128, GT])
        qx, kx = m.sb("qx", [128, 2, 2, GT]), m.sb("kx", [128, 2, 2, GT])
        vx = m.sb("vx", [HALF, 2, TILES, 160])
        oT = m.sb("oT", [128, 2, GT])
        rx = m.sb("rx", [96, 2, GT])
        tq = m.sb("tq", [128, NG, 64])
        tv = m.sb("tv", [96, NG, 128])
        tabT = m.sb("tabT", [128, 2, ROWS])
        onehot = m.sb("onehot", [EXT, 1 + 15 * SIDE])
        rowhot = m.sb("rowhot", [EXT, 1 + 15 * SIDE])
        ident = m.sb("ident", [128, 128])
        prob = m.sb("prob", [HALF, 2, 2, NTOK])
        probT = m.sb("probT", [HALF, 2, 2 * NTOK])
        npeak, total = m.sb("npeak", [HALF, 2, 2]), m.sb("total", [HALF, 2, 2])
        stat, mv, sd = m.sb("stat", [HALF, TILES, 6]), m.sb("mv", [HALF, TILES, 2]), m.sb("sd", [HALF, TILES, 1])
        eps = m.sb("eps", [128, 1])
        p_bank = [m.bank(f"p{i}") for i in range(2)]
        s_bank = [m.bank(f"s{i}") for i in range(2)]
        t_bank = [m.bank(f"t{i}") for i in range(2)]
        o_bank = [m.bank(f"o{i}") for i in range(2)]
        mv_made, sd_made = m.sem("mv_made"), m.sem("sd_made")
        consts_in, onehot_made, zeroed = m.sem("consts_in"), m.sem("onehot_made"), m.sem("zeroed")
        tables_in, tables_made, raw_in = m.sem("tables_in"), m.sem("tables_made"), [m.sem(f"raw_in{i}") for i in range(2)]
        hid_in, resid_made = m.sem("hid_in"), m.sem("resid_made")
        norm_made, dve_step, passed = m.sem("norm_made"), m.sem("dve_step"), m.sem("passed")
        full = [m.sem(f"full{i}") for i in range(2)]
        free = [m.sem(f"free{i}") for i in range(2)]
        prep_full, prep_free = m.sem("prep_full"), m.sem("prep_free")
        scores, peaks, exps, probs, turned, probT_made, outs, outs_used = (
            m.sem("scores"), m.sem("peaks"), m.sem("exps"), m.sem("probs"), m.sem("turned"), m.sem("probT_made"),
            m.sem("outs"), m.sem("outs_used"))
        hidden_out = m.sem("hidden_out")

        h0_tiles = hidden0.rearrange("b (h p) d -> p (b h) d", p=HALF)
        h1_tiles = hidden1.rearrange("b (h p) d -> p (b h) d", p=HALF)
        QROWS = 3 * HEADS * HD

        def q_cols(a):
            if a < CLSG:
                row = 14 - a
                return 1 + SIDE * row, (SIDE if row < SIDE else 1), 1
            if a == CLSG:
                return 0, 1, 1
            return 1 + (13 - (a - 16)), SIDE, SIDE

        def group_rhs(src, a):
            off, n, step = q_cols(a)
            return view(src, [[NTOK, GB], [step, n]], off)

        ROWBANKS = [[(CLSG, 0)] + [(14 - r, 1 + SIDE * r) for r in range(4)],
                    [(14 - r, SIDE * (r - 4)) for r in range(4, 8)],
                    [(14 - r, SIDE * (r - 8)) for r in range(8, 12)],
                    [(14 - r, SIDE * (r - 12)) for r in range(12, 15)]]
        ROWSPAN = [(0, 57), (57, 56), (113, 56), (169, 29)]
        COLBANKS = [range(0, 4), range(4, 8), range(8, 12), range(12, 14)]

        def prep_jobs():
            return [("qkv", t) for t in range(QROWS // 128)] + [("proj", p) for p in range(PAIRS)]

        def first_jobs(p):
            return [("first", p, j) for j in range(FIRST)]

        def last_jobs(p):
            return [("last", p, j) for j in range(LAST)]

        opening = [("turn", 0, j) for j in range(TURN)] + first_jobs(0)
        between = [[] for _ in range(STEPS)]
        for p in range(PAIRS):
            jobs = (first_jobs(p + 1) if p + 1 < PAIRS else []) + (last_jobs(p - 1) if p else [])
            begin = 5 if p + 1 == PAIRS else 0
            for k, job in enumerate(jobs):
                between[p * UNIT + begin + k * (UNIT - begin) // len(jobs)].append(job)
        closing = last_jobs(PAIRS - 1)
        order = {job: k for k, job in enumerate(opening + [j for js in between for j in js] + closing)}
        G_JOBS = len(order) // 2

        def through(base, kind, p, j, bank):
            k = order[kind, p, j]
            return base + k // 2 + (1 if k % 2 >= bank else 0)

        with nc.Block() as block:

            @block.sync
            def _(sp):
                for s in (hidden_out, *free):
                    sp.sem_inc(s, PRIMED)
                sp.dma_start(hid[:, :, :], h0_tiles[:, 0:TILES, :]).then_inc(hid_in, 16)
                with sp.Fori(0, GROUPS) as g:
                    sp.wait_ge(norm_made, (g + 1) * TURN)
                    sp.wait_ge(resid_made, g + 1)
                    sp.dma_start(hid[:, :, :], h0_tiles[:, bass.ds(((g + 1) % GROUPS) * TILES, TILES), :]).then_inc(hid_in, 16)
                    for bank in range(2):
                        sp.wait_ge(free[bank], (g + 1) * G_JOBS + PRIMED)
                    sp.dma_start(h1_tiles[:, bass.ds(g * TILES, TILES), :], resid[:, :, :]).then_inc(hidden_out, 16)
                sp.wait_ge(hid_in, 16 * (GROUPS + 1))
                sp.wait_ge(hidden_out, 16 * GROUPS + PRIMED)

            @block.gpsimd
            def _(pool):
                for t in (qx, kx, rx, tq, tv):
                    ins = nc.gpsimd.memset(t[:], 0.0)
                ins.then_inc(zeroed, 1)
                make_identity(pool, nc, ident, onehot_made)
                W = 1 + 15 * SIDE
                nc.gpsimd.memset(onehot[:, :], 0.0)
                nc.gpsimd.memset(rowhot[:, :], 1.0).then_inc(onehot_made, 1)
                cols = onehot[:, 1:W].rearrange("p (r c) -> p r c", c=SIDE)
                for n, (dst, pattern, base, mult, op, fill) in enumerate((
                        (cols, [[0, 15], [1, SIDE]], 16, -1, ALU.not_equal, 1.0),
                        (onehot[:, 0:1], [[0, 1]], -15, 1, ALU.not_equal, 1.0),
                        (onehot[:, 0:1], [[0, 1]], -30, 1, ALU.not_equal, 1.0),
                        (rowhot[:, :], [[1, W]], -1, -SIDE, ALU.is_ge, 0.0),
                        (rowhot[:, :], [[-1, W]], SIDE, SIDE, ALU.is_ge, 0.0))):
                    pool.wait_ge(onehot_made, 3 + n)
                    nc.gpsimd.affine_select(out=dst, in_=dst, compare_op=op, fill=fill, base=base, pattern=pattern,
                                            channel_multiplier=mult).then_inc(onehot_made, 1)
                pool.wait_ge(onehot_made, 8)
                nc.gpsimd.tensor_tensor(onehot[:, :], onehot[:, :], rowhot[:, :], ALU.add).then_inc(onehot_made, 1)

                pool.wait_ge(zeroed, 1)
                for half, head in ((64, 0), (32, 1)):
                    def rows_of(p, n, a, na, tab, first, astep):
                        pool.dma_start(tv[half + p:half + p + n, a:a + na, 64 * head:64 * head + 64],
                                       bass.AP(tensor=tab.tensor, offset=tab.offset + first * HD,
                                               ap=[[HD if astep >= 0 else 0, n], [max(astep, 0) * HD, na], [1, HD]])
                                       ).then_inc(tables_in, 16)
                    rows_of(0, 15, 0, 15, tab_vv, 1, 1)
                    rows_of(15, 1, 0, 15, tab_vv, 0, 0)
                    rows_of(0, 16, CLSG, 1, tab_vv, 0, -1)
                    rows_of(16, 15, CLSG, 1, tab_vh, 0, -1)
                    rows_of(16, 14, 0, 1, tab_vh, 15, 0)
                    rows_of(30, 1, 0, 1, tab_vh, 0, 0)
                    rows_of(16, 14, 16, 14, tab_vh, 2, 1)
                    rows_of(30, 1, 16, 14, tab_vh, 0, 0)
                for half in range(2):
                    for i, tab in enumerate((tab_kv, tab_kh)):
                        with nc.allow_non_contiguous_dma(reason="a small table, transposed"):
                            pool.dma_start(tabT[64 * half:64 * half + 64, i, :], tab.rearrange("r d -> d r")).then_inc(consts_in, 16)
                pool.dma_start(pbias[:, :], bass.AP(tensor=proj_b.tensor, offset=proj_b.offset, ap=[[0, HALF], [1, DIM]])
                               ).then_inc(consts_in, 16)
                pool.wait_ge(tables_in, 16 * 16)
                pool.wait_ge(consts_in, 16 * 5)
                pool.wait_ge(prep_free, len(prep_jobs()))

                with pool.Fori(0, GROUPS) as g:
                    pool.wait_ge(hid_in, g * 16 + 16)
                    pool.wait_ge(hidden_out, g * 16 + PRIMED)
                    nc.gpsimd.tensor_tensor(resid[:, :, :], hid[:, :, :], view(pbias[:, :], [[0, TILES], [1, DIM]]),
                                            ALU.add).then_inc(resid_made, 1)

            @block.scalar
            def _(act):
                for n, (kind, t) in enumerate(prep_jobs()):
                    if n >= 2:
                        act.wait_ge(prep_full, n - 1)
                    dst = raw[:, n % 2, :]
                    if kind == "qkv":
                        act.dma_start(dst[:, 0:DIM], qkv_w[128 * t:128 * t + 128, :]).then_inc(raw_in[n % 2], 16)
                    else:
                        act.dma_start(dst[:, 0:128], proj_w[0:128, 128 * t:128 * t + 128]).then_inc(raw_in[n % 2], 16)
                        act.dma_start(dst[0:C1, 128:256], proj_w[128:DIM, 128 * t:128 * t + 128]).then_inc(raw_in[n % 2], 16)

                act.wait_ge(tables_made, 1)
                act.wait_ge(mv_made, 1)
                nc.scalar.activation(sd[:, :, :], mv[:, :, 1:2], ACT.Sqrt, bias=eps[0:HALF, :]).then_inc(sd_made, 1)
                with act.Fori(0, GROUPS) as g:
                    base = g * G_JOBS

                    def job(kind, p, j):
                        k, s = order[kind, p, j], p % 2
                        if kind == "last" or (kind == "first" and 12 <= j < 16):
                            return
                        bank = p_bank[k % 2]
                        act.wait_ge(full[k % 2], base + k // 2 + 1)
                        if kind == "turn":
                            cols = slice(j * NTOK, (j + 1) * NTOK)
                            nc.scalar.activation(xT0[:, cols], bank[:, 0:NTOK], ACT.Copy)
                            ins = nc.scalar.activation(xT1[:, cols], bank[0:C1, NTOK:2 * NTOK], ACT.Copy)
                        elif j < 4:
                            cols = slice(j * HC, (j + 1) * HC)
                            nc.scalar.activation(q2[:, cols], bank[:, 0:HC], ACT.Copy, scale=SCALE)
                            nc.scalar.activation(qx[0:64, s, 0, cols], bank[0:64, 0:HC], ACT.Copy, scale=SCALE)
                            ins = nc.scalar.activation(qx[64:128, s, 1, cols], bank[64:128, 0:HC], ACT.Copy, scale=SCALE)
                        elif j < 8:
                            cols = slice((j - 4) * HC, (j - 3) * HC)
                            nc.scalar.activation(kx[0:64, s, 0, cols], bank[0:64, 0:HC], ACT.Copy)
                            ins = nc.scalar.activation(kx[64:128, s, 1, cols], bank[64:128, 0:HC], ACT.Copy)
                        elif j < 12:
                            first, n = ROWSPAN[j - 8]
                            for src, lo, head in ((32, 64, 0), (0, 32, 1)):
                                ins = nc.scalar.activation(view(qx[lo:lo + 32, s, head, :], [[NTOK, GB], [1, n]], first),
                                                           view(bank[src:src + 32, :], [[n, GB], [1, n]]), ACT.Copy)
                        else:
                            ins = nc.scalar.activation(
                                view(vx[:, s, 4 * (j - 16):4 * (j - 15), :], [[160, 4], [96, 2], [1, HD]]),
                                view(bank[0:HALF, :], [[128, 4], [HD, 2], [1, HD]]), ACT.Copy)
                        ins.then_inc(free[k % 2], 1)

                    for j in opening:
                        job(*j)
                    for i in range(STEPS + 2):
                        n = g * STEPS + i
                        if i < STEPS:
                            act.wait_ge(peaks, n + 1)
                            if i >= 2:
                                act.wait_ge(turned, n - 1)
                            for h in range(2):
                                ins = nc.scalar.activation(prob[:, i % 2, h, :], s_bank[i % 2][0:HALF, h * NTOK:(h + 1) * NTOK],
                                                           ACT.Exp, bias=npeak[:, i % 2, h:h + 1],
                                                           accum_out=total[:, i % 2, h:h + 1])
                            ins.then_inc(exps, 1)
                            for j in between[i]:
                                job(*j)
                        if i >= 2:
                            act.wait_ge(turned, n - 2 + 1)
                            if i >= 4:
                                act.wait_ge(outs, n - 3)
                            nc.scalar.activation(probT[:, i % 2, :], t_bank[i % 2][0:HALF, 0:2 * NTOK], ACT.Copy
                                                 ).then_inc(probT_made, 1)
                    act.wait_ge(mv_made, g + 2)
                    nc.scalar.activation(sd[:, :, :], mv[:, :, 1:2], ACT.Sqrt, bias=eps[0:HALF, :]).then_inc(sd_made, 1)

            @block.vector
            def _(dve):
                nc.vector.memset(eps[:, :], EPS)
                dve.wait_ge(consts_in, 16 * 5)
                dve.wait_ge(zeroed, 1)
                for lo, at in ((0, 32), (64, 0)):
                    src = tabT[lo:lo + 64, :, :]

                    def table(a, na, col, n, which, first, cstep, astep):
                        nc.vector.tensor_copy(tq[lo:lo + 64, a:a + na, at + col:at + col + n],
                                              view(src, [[astep, na], [cstep, n]], which * ROWS + first))
                    table(0, 15, 0, 15, 0, 1, 1, 1)
                    table(0, 15, 15, 1, 0, 0, 0, 0)
                    table(CLSG, 1, 0, 16, 0, 0, 0, 0)
                    table(CLSG, 1, 16, 15, 1, 0, 0, 0)
                    table(0, 1, 16, 14, 1, 15, 1, 0)
                    table(0, 1, 30, 1, 1, 0, 0, 0)
                    table(16, 14, 16, 14, 1, 2, 1, 1)
                    table(16, 14, 30, 1, 1, 0, 0, 0)
                dve.wait_ge(onehot_made, 9)
                for s in range(2):
                    for lo, head in ((64, 0), (32, 1)):
                        ins = nc.vector.tensor_copy(view(kx[lo:lo + 32, s, head, :], [[NTOK, GB], [1, NTOK]]),
                                                    view(onehot[:, :], [[0, GB], [1, NTOK]]))
                ins.then_inc(tables_made, 1)
                for n, (kind, t) in enumerate(prep_jobs()):
                    dve.wait_ge(prep_full, n + 1)
                    bank = p_bank[n % 2]
                    if kind == "qkv":
                        nc.vector.tensor_copy(wT0[:, t // 6, t % 6, :], bank[:, 0:128])
                        nc.vector.tensor_copy(wT1[:, t // 6, t % 6, :], bank[0:C1, 128:256]).then_inc(prep_free, 1)
                    else:
                        nc.vector.tensor_copy(pw[:, t, 0:DIM], bank[:, 0:DIM]).then_inc(prep_free, 1)
                for h in range(2):
                    dve.wait_ge(prep_full, 1 + h + len(prep_jobs()))
                    for s in range(2):
                        ins = nc.vector.tensor_copy(view(vx[:, s, h:h + 1, 64:96], [[2 * 160, GB], [1, EXT]]),
                                                    view(s_bank[h][0:HALF, 0:EXT], [[0, GB], [1, EXT]]))
                ins.then_inc(tables_made, 1)

                PER_GROUP = 1 + STEPS + TILES
                st = Steps(dve, dve_step, 0)
                dve.wait_ge(hid_in, 16)
                for t in range(TILES):
                    ins = nc.vector.bn_stats(stat[:, t, :], hid[:, t, :])
                st.did(ins)
                st.settle_apart(passed)
                for t in range(TILES):
                    ins = nc.vector.bn_aggr(mv[:, t, :], stat[:, t, :])
                ins.then_inc(mv_made, 1)
                with dve.Fori(0, GROUPS) as g:
                    st = Steps(dve, dve_step, 1 + g * PER_GROUP)
                    base = g * G_JOBS
                    dve.wait_ge(sd_made, g + 1)
                    st.did(nc.vector.reciprocal(sd[:, :, :], sd[:, :, :]))
                    st.settle()
                    for j in range(TURN):
                        if j >= 2:
                            dve.wait_ge(full[j % 2], base + j // 2)
                        for t in (2 * j, 2 * j + 1):
                            ins = nc.vector.tensor_scalar(norm[:, t % 4, :], hid[:, t, :], mv[:, t, 0:1], sd[:, t, :],
                                                          ALU.subtract, ALU.mult)
                        ins.then_inc(norm_made, 1)

                    def job(kind, p, j):
                        k, s = order[kind, p, j], p % 2
                        bank, up_to = p_bank[k % 2], base + k // 2 + 1
                        if kind == "first" and 12 <= j < 16:
                            span = COLBANKS[j - 12]
                            n = len(span)
                            if j == 12:
                                for b in range(2):
                                    dve.wait_ge(free[b], through(base, kind, p, 11, b) + PRIMED)
                            dve.wait_ge(full[k % 2], up_to)
                            for src, lo, head in ((32, 64, 0), (0, 32, 1)):
                                dst = view(qx[lo:lo + 32, s, head, :], [[NTOK, GB], [SIDE, SIDE], [1, n]], 1 + span[0])
                                ins = nc.vector.tensor_tensor(
                                    dst, view(bank[src:src + 32, :], [[n * SIDE, GB], [1, SIDE], [SIDE, n]]), dst, ALU.add)
                        elif kind == "last" and j < 4:
                            first, n = ROWSPAN[j]
                            if j == 0:
                                dve.wait_ge(outs_used, g * STEPS + (p + 1) * UNIT)
                            dve.wait_ge(full[k % 2], up_to)
                            dst = view(oT[:, s, :], [[NTOK, GB], [1, n]], first)
                            ins = nc.vector.tensor_tensor(dst, view(bank[:, :], [[n, GB], [1, n]]), dst, ALU.add)
                        elif kind == "last" and j < 8:
                            span = COLBANKS[j - 4]
                            n = len(span)
                            if j == 4:
                                for b in range(2):
                                    dve.wait_ge(free[b], through(base, kind, p, 3, b) + PRIMED)
                            dve.wait_ge(full[k % 2], up_to)
                            dst = view(oT[:, s, :], [[NTOK, GB], [SIDE, SIDE], [1, n]], 1 + span[0])
                            ins = nc.vector.tensor_tensor(
                                dst, view(bank[:, :], [[n * SIDE, GB], [1, SIDE], [SIDE, n]]), dst, ALU.add)
                        elif kind == "last":
                            if p == 0:
                                dve.wait_ge(resid_made, g + 1)
                            elif j == 8:
                                for b in range(2):
                                    dve.wait_ge(free[b], through(base, kind, p - 1, 15, b) + PRIMED)
                            dve.wait_ge(full[k % 2], up_to)
                            dst = resid[:, 2 * (j - 8):2 * (j - 7), :]
                            ins = nc.vector.tensor_tensor(dst, bank[0:HALF, 0:2 * DIM].rearrange("p (t d) -> p t d", t=2),
                                                          dst, ALU.add)
                        else:
                            return
                        ins.then_inc(free[k % 2], 1)

                    for j in opening:
                        job(*j)
                    for i in range(STEPS + 4):
                        n = g * STEPS + i
                        if i < STEPS:
                            dve.wait_ge(scores, n + 1)
                            nc.vector.tensor_reduce(npeak[:, i % 2, :], s_bank[i % 2][0:HALF, 0:2 * NTOK].rearrange(
                                "p (h k) -> p h k", h=2), AX.X, ALU.max, negate=True).then_inc(peaks, 1)
                        if i >= 4:
                            j = i - 4
                            p, b, head = j // UNIT, j % UNIT // 2, j % 2
                            dve.wait_ge(outs, n - 4 + 1)
                            cols = slice(b * NTOK, (b + 1) * NTOK)
                            lo, ext = (64, 32) if head else (0, 64)
                            nc.vector.tensor_copy(oT[lo:lo + 64, p % 2, cols], o_bank[j % 2][lo:lo + 64, 0:NTOK])
                            nc.vector.tensor_copy(rx[ext:ext + 32, p % 2, cols], o_bank[j % 2][ext:ext + 32, 0:NTOK]
                                                  ).then_inc(outs_used, 1)
                        if 1 <= i <= STEPS:
                            j = i - 1
                            dve.wait_ge(exps, n - 1 + 1)
                            st.did(nc.vector.reciprocal(total[:, j % 2, :], total[:, j % 2, :]))
                            st.settle()
                            for h in range(2):
                                ins = nc.vector.tensor_scalar(prob[:, j % 2, h, :], prob[:, j % 2, h, :],
                                                              total[:, j % 2, h:h + 1], None, ALU.mult)
                            ins.then_inc(probs, 1)
                        if i < STEPS:
                            for j in between[i]:
                                job(*j)
                        if 4 * UNIT <= i < 5 * UNIT:
                            t = i - 4 * UNIT
                            if t == 0:
                                dve.wait_ge(hid_in, (g + 2) * 16)
                            st.did(nc.vector.bn_stats(stat[:, t, :], hid[:, t, :]))
                        elif 5 * UNIT <= i < 6 * UNIT:
                            t = i - 5 * UNIT
                            if t == 0:
                                st.settle_apart(passed)
                            ins = nc.vector.bn_aggr(mv[:, t, :], stat[:, t, :])
                            if t == TILES - 1:
                                ins.then_inc(mv_made, 1)
                    for j in closing:
                        job(*j)
                    assert st.n == PER_GROUP

            @block.tensor
            def _(pe):
                pe.wait_ge(onehot_made, 9)
                for n, (kind, t) in enumerate(prep_jobs()):
                    pe.wait_ge(raw_in[n % 2], 16 * sum(1 if k == "qkv" else 2 for k, _ in prep_jobs()[n % 2:n + 1:2]))
                    if n >= 2:
                        pe.wait_ge(prep_free, n - 1)
                    src, bank = raw[:, n % 2, :], p_bank[n % 2]
                    if kind == "qkv":
                        nc.tensor.transpose(bank[:, 0:128], src[:, 0:C0], ident[:, :])
                        ins = nc.tensor.transpose(bank[0:C1, 128:256], src[:, C0:DIM], ident[:, :])
                    else:
                        nc.tensor.transpose(bank[:, 0:128], src[:, 0:128], ident[:, :])
                        ins = nc.tensor.transpose(bank[:, 128:DIM], src[0:C1, 128:256], ident[0:C1, 0:C1])
                    ins.then_inc(prep_full, 1)
                for h in range(2):
                    nc.tensor.transpose(s_bank[h][0:HALF, 0:EXT], onehot[:, h * HALF:(h + 1) * HALF], ident[0:EXT, 0:EXT]
                                        ).then_inc(prep_full, 1)
                pe.wait_ge(prep_free, len(prep_jobs()))
                pe.wait_ge(tables_made, 2)
                pe.wait_ge(tables_in, 16 * 16)

                with pe.Fori(0, GROUPS) as g:
                    base = g * G_JOBS

                    def all_read(kind, p, j):
                        for b in range(2):
                            pe.wait_ge(free[b], through(base, kind, p, j, b) + PRIMED)

                    def job(kind, p, j):
                        k, s = order[kind, p, j], p % 2
                        bank = p_bank[k % 2]
                        if kind == "turn":
                            pe.wait_ge(norm_made, g * TURN + j + 1)
                        if kind == "first" and j == 0 and p == 0:
                            all_read("turn", 0, TURN - 1)
                        if kind == "first" and j == 8:
                            all_read("first", p, 3)
                        if kind == "last" and j == 0:
                            pe.wait_ge(outs_used, g * STEPS + (p + 1) * UNIT)
                        if kind == "last" and j == 8:
                            all_read("last", p, 7)
                        pe.wait_ge(free[k % 2], base + k // 2 + PRIMED)
                        if kind == "turn":
                            for t in range(2):
                                src = norm[:, (2 * j + t) % 4, :]
                                nc.tensor.transpose(bank[:, t * HALF:(t + 1) * HALF], src[:, 0:C0], ident[0:HALF, 0:HALF])
                                ins = nc.tensor.transpose(bank[0:C1, NTOK + t * HALF:NTOK + (t + 1) * HALF], src[:, C0:DIM],
                                                          ident[0:HALF, 0:HALF])
                        elif kind == "first" and j < 8:
                            cols = slice(j % 4 * HC, (j % 4 + 1) * HC)
                            nc.tensor.matmul(bank[:, 0:HC], wT0[:, j // 4, p, :], xT0[:, cols], start=True, stop=False)
                            ins = nc.tensor.matmul(bank[:, 0:HC], wT1[:, j // 4, p, :], xT1[:, cols], start=False, stop=True)
                        elif kind == "first" and j < 12:
                            n = ROWSPAN[j - 8][1]
                            for a, col in ROWBANKS[j - 8]:
                                ins = nc.tensor.matmul(view(bank[0:64, :], [[n, GB], [1, q_cols(a)[1]]], col), tq[:, a, :],
                                                       group_rhs(q2[:, :], a), start=True, stop=True)
                        elif kind == "first" and j < 16:
                            span = COLBANKS[j - 12]
                            n = len(span)
                            for i, c in enumerate(span):
                                ins = nc.tensor.matmul(view(bank[0:64, :], [[n * SIDE, GB], [1, SIDE]], i * SIDE), tq[:, 16 + 13 - c, :],
                                                       group_rhs(q2[:, :], 16 + 13 - c), start=True, stop=True)
                        elif kind == "first":
                            for t in range(4):
                                cols = slice((4 * (j - 16) + t) * HALF, (4 * (j - 16) + t + 1) * HALF)
                                out = bank[0:HALF, t * 128:(t + 1) * 128]
                                nc.tensor.matmul(out, xT0[:, cols], wT0[:, 2, p, :], start=True, stop=False)
                                ins = nc.tensor.matmul(out, xT1[:, cols], wT1[:, 2, p, :], start=False, stop=True)
                        elif j < 4:
                            n = ROWSPAN[j][1]
                            for a, col in ROWBANKS[j]:
                                ins = nc.tensor.matmul(view(bank[:, :], [[n, GB], [1, q_cols(a)[1]]], col), tv[:, a, :],
                                                       group_rhs(rx[:, s, :], a), start=True, stop=True)
                        elif j < 8:
                            span = COLBANKS[j - 4]
                            n = len(span)
                            for i, c in enumerate(span):
                                ins = nc.tensor.matmul(view(bank[:, :], [[n * SIDE, GB], [1, SIDE]], i * SIDE), tv[:, 16 + 13 - c, :],
                                                       group_rhs(rx[:, s, :], 16 + 13 - c), start=True, stop=True)
                        else:
                            for t in range(2):
                                cols = slice((2 * (j - 8) + t) * HALF, (2 * (j - 8) + t + 1) * HALF)
                                ins = nc.tensor.matmul(bank[0:HALF, t * DIM:(t + 1) * DIM], oT[:, s, cols], pw[:, p, :],
                                                       start=True, stop=True)
                        ins.then_inc(full[k % 2], 1)

                    for j in opening:
                        job(*j)
                    for i in range(STEPS + 3):
                        n = g * STEPS + i
                        if i < STEPS:
                            p, b, head = i // UNIT, i % UNIT // 2, i % 2
                            if i % UNIT == 0:
                                all_read("first", p, FIRST - 1)
                            K = 128 if head else 96
                            if i >= 2:
                                pe.wait_ge(exps, n - 1)
                            for h in range(2):
                                q0 = b * NTOK + h * HALF
                                ins = nc.tensor.matmul(s_bank[i % 2][0:HALF, h * NTOK:(h + 1) * NTOK],
                                                       qx[0:K, p % 2, head, q0:q0 + HALF],
                                                       kx[0:K, p % 2, head, b * NTOK:(b + 1) * NTOK], start=True, stop=True)
                            ins.then_inc(scores, 1)
                        if 2 <= i < STEPS + 2:
                            j = i - 2
                            pe.wait_ge(probs, n - 2 + 1)
                            if i >= 4:
                                pe.wait_ge(probT_made, n - 3)
                            for k in range(2):
                                for h in range(2):
                                    ins = nc.tensor.transpose(
                                        t_bank[j % 2][0:HALF, k * NTOK + h * HALF:k * NTOK + (h + 1) * HALF],
                                        prob[:, j % 2, h, k * HALF:(k + 1) * HALF], ident[0:HALF, 0:HALF])
                            ins.then_inc(turned, 1)
                        if i < STEPS:
                            for j in between[i]:
                                job(*j)
                        if i >= 3:
                            j = i - 3
                            p, b, head = j // UNIT, j % UNIT // 2, j % 2
                            M, v0 = (128, 32) if head else (96, 0)
                            pe.wait_ge(probT_made, n - 3 + 1)
                            if i >= 5:
                                pe.wait_ge(outs_used, n - 4)
                            for k in range(2):
                                ins = nc.tensor.matmul(o_bank[j % 2][0:M, 0:NTOK], vx[:, p % 2, 2 * b + k, v0:v0 + M],
                                                       probT[:, j % 2, k * NTOK:(k + 1) * NTOK],
                                                       start=(k == 0), stop=(k == 1))
                            ins.then_inc(outs, 1)
                    for j in closing:
                        job(*j)


def experts_stage(nc, hidden1, w_fc_sh, w_proj_sh, w1, w2, router_w, balance_bias, out):
    TB = 3
    BT = TB * 128
    BLOCKS = B * NTOK // BT
    MLPS = EXPERTS + 1
    HID = MLPS * DIM
    HT = (HID + 127) // 128
    with ExitStack() as ctx:
        m = Memory(nc, ctx, "ffn")
        hid = m.sb("hid", [128, 2, TB, DIM])
        norm = m.sb("norm", [128, TB, DIM])
        acc = m.sb("acc", [128, 2, TB, DIM])
        xT0, xT1 = m.sb("xT0", [C0, 2, BT]), m.sb("xT1", [C1, 2, BT])
        up0, up1 = m.sb("up0", [C0, HID]), m.sb("up1", [C1, HID])
        down = m.sb("down", [128, HT, DIM])
        hidden = m.sb("hidden", [128, HT, BT])
        relu = m.sb("relu", [128, 4, BT])
        rw0, rw1 = m.sb("rw0", [C0, EXPERTS]), m.sb("rw1", [C1, EXPERTS])
        bb, ranks = m.sb("bb", [128, EXPERTS]), m.sb("ranks", [128, EXPERTS])
        ident = m.sb("ident", [128, 128])
        stat, mv, sd = m.sb("stat", [128, TB, 6]), m.sb("mv", [128, TB, 2]), m.sb("sd", [128, TB, 1])
        eps = m.sb("eps", [128, 1])
        mv_made, sd_made = m.sem("mv_made"), m.sem("sd_made")
        expo, sc, sb_, eq, first, left, second, weight, gate = (m.sb(n, [128, TB, EXPERTS]) for n in (
            "expo", "score", "biased", "eq", "first", "left", "second", "weight", "gate"))
        top = m.sb("top", [128, TB, 1])
        t_bank = [m.bank(f"t{i}") for i in range(2)]
        h_bank = [m.bank(f"h{i}") for i in range(2)]
        y_bank = [m.bank(f"y{i}") for i in range(3)]
        r_bank = m.bank("r")
        w_in, ranks_made, hid_in = m.sem("w_in"), m.sem("ranks_made"), [m.sem(f"hid_in{i}") for i in range(2)]
        norm_made, turned, xT_made, dve_step = m.sem("norm_made"), m.sem("turned"), m.sem("xT_made"), m.sem("dve_step")
        routed, expo_made, passed = m.sem("routed"), m.sem("expo_made"), m.sem("passed")
        up_done, relu_made, squared = m.sem("up_done"), [m.sem(f"relu_made{i}") for i in range(2)], m.sem("squared")
        down_done, summed, acc_out = m.sem("down_done"), m.sem("summed"), [m.sem(f"acc_out{i}") for i in range(2)]
        h_tiles = hidden1.rearrange("b n d -> (b n) d").rearrange("(t p) d -> p t d", p=128)
        o_tiles = out.rearrange("b n d -> (b n) d").rearrange("(t p) d -> p t d", p=128)
        DOWNS = [(EXPERTS, [(12, 0, 128), (13, 0, 64)])]
        for i in range(EXPERTS // 2):
            DOWNS += [(2 * i, [(3 * i, 0, 128), (3 * i + 1, 0, 64)]), (2 * i + 1, [(3 * i + 2, 0, 128), (3 * i + 1, 64, 64)])]
        UPS = [12, 13] + list(range(12))

        with nc.Block() as block:

            @block.sync
            def _(sp):
                for s in (down_done, turned, *acc_out, xT_made, *relu_made, summed):
                    sp.sem_inc(s, PRIMED)
                def load(it, s):
                    sp.dma_start(hid[:, s, :, :], h_tiles[:, bass.ds(it * TB, TB), :]).then_inc(hid_in[s], 16)

                def store(it, s):
                    sp.wait_ge(summed, (it + 1) * TB * MLPS + PRIMED)
                    sp.dma_start(o_tiles[:, bass.ds(it * TB, TB), :], acc[:, s, :, :]).then_inc(acc_out[s], 16)
                load(0, 0)
                load(1, 1)
                with sp.Fori(0, (BLOCKS - 3) // 2) as pair:
                    ii = pair * 2
                    for s in range(2):
                        store(ii + s, s)
                        load(ii + s + 2, s)
                store(BLOCKS - 3, 0)
                load(BLOCKS - 1, 0)
                store(BLOCKS - 2, 1)
                store(BLOCKS - 1, 0)
                sp.wait_ge(acc_out[0], 16 * (BLOCKS // 2 + 1) + PRIMED)
                sp.wait_ge(acc_out[1], 16 * (BLOCKS // 2) + PRIMED)

            @block.gpsimd
            def _(pool):
                make_identity(pool, nc, ident, ranks_made)
                nc.gpsimd.iota(ranks[:, :], [[-1, EXPERTS]], base=EXPERTS, channel_multiplier=0,
                               allow_small_or_imprecise_dtypes=True).then_inc(ranks_made, 1)
                for e in range(EXPERTS):
                    pool.dma_start(up0[:, e * DIM:(e + 1) * DIM], w1[e, 0:C0, :]).then_inc(w_in, 16)
                    pool.dma_start(up1[:, e * DIM:(e + 1) * DIM], w1[e, C0:DIM, :]).then_inc(w_in, 16)
                pool.dma_start(up0[:, EXPERTS * DIM:], w_fc_sh[0:C0, :]).then_inc(w_in, 16)
                pool.dma_start(up1[:, EXPERTS * DIM:], w_fc_sh[C0:DIM, :]).then_inc(w_in, 16)
                pool.dma_start(down[:, 0:12, :], w2.rearrange("e h d -> (e h) d").rearrange("(t p) d -> p t d", p=128)).then_inc(w_in, 16)
                pool.dma_start(down[:, 12, :], w_proj_sh[0:128, :]).then_inc(w_in, 16)
                pool.dma_start(down[0:64, 13, :], w_proj_sh[128:DIM, :]).then_inc(w_in, 16)
                with nc.allow_non_contiguous_dma(reason="a small weight, transposed"):
                    pool.dma_start(rw0[:, :], router_w[:, 0:C0].rearrange("e c -> c e")).then_inc(w_in, 16)
                    pool.dma_start(rw1[:, :], router_w[:, C0:DIM].rearrange("e c -> c e")).then_inc(w_in, 16)
                pool.dma_start(bb[:, :], bass.AP(tensor=balance_bias.tensor, offset=balance_bias.offset,
                                                 ap=[[0, 128], [1, EXPERTS]])).then_inc(w_in, 16)
                pool.wait_ge(w_in, 16 * (2 * MLPS + 6))
                with pool.Fori(0, BLOCKS) as it:
                    pool.wait_ge(down_done, it * TB * MLPS + PRIMED)
                    for n in range(HT):
                        j = UPS[n]
                        rows = 64 if j == 13 else 128
                        pool.wait_ge(relu_made[n % 2], it * (HT // 2) + n // 2 + 1 + PRIMED)
                        nc.gpsimd.tensor_tensor(hidden[0:rows, j, :], relu[0:rows, n % 4, :], relu[0:rows, n % 4, :], ALU.mult
                                                ).then_inc(squared, 1)

            @block.scalar
            def _(act):
                def turn_copy(k, s):
                    act.wait_ge(mv_made, k + 1)
                    nc.scalar.activation(sd[:, :, :], mv[:, :, 1:2], ACT.Sqrt, bias=eps[:, :]).then_inc(sd_made, 1)
                    act.wait_ge(turned, k + 1 + PRIMED)
                    nc.scalar.activation(xT0[:, s, :], t_bank[0][:, 0:BT], ACT.Copy)
                    nc.scalar.activation(xT1[:, s, :], t_bank[1][0:C1, 0:BT], ACT.Copy).then_inc(xT_made, 1)

                def body(it, s, last=False):
                    act.wait_ge(routed, it + 1)
                    nc.scalar.activation(expo[:, :, :], r_bank[:, 0:TB * EXPERTS].rearrange("p (t e) -> p t e", t=TB),
                                         ACT.Exp, scale=-1.0).then_inc(expo_made, 1)
                    for n in range(HT // 2):
                        act.wait_ge(up_done, it * HT + 2 * n + 1)
                        if n >= 2:
                            act.wait_ge(squared, it * HT + 2 * n - 3)
                        nc.scalar.activation(relu[:, 2 * n % 4, :], h_bank[0][:, 0:BT], ACT.Relu).then_inc(relu_made[0], 1)
                    if not last:
                        turn_copy(it + 1, 1 - s)

                turn_copy(0, 0)
                with act.Fori(0, (BLOCKS - 1) // 2) as pair:
                    ii = pair * 2
                    body(ii, 0)
                    body(ii + 1, 1)
                body(BLOCKS - 1, 0, last=True)

            @block.vector
            def _(dve):
                def layernorm(k, s, st):
                    for t in range(TB):
                        ins = nc.vector.bn_stats(stat[:, t, :], hid[:, s, t, :])
                    st.did(ins)
                    st.settle_apart(passed)
                    for t in range(TB):
                        ins = nc.vector.bn_aggr(mv[:, t, :], stat[:, t, :])
                    ins.then_inc(mv_made, 1)
                    dve.wait_ge(sd_made, k + 1)
                    st.did(nc.vector.reciprocal(sd[:, :, :], sd[:, :, :]))
                    st.settle()
                    dve.wait_ge(turned, k + PRIMED)
                    for t in range(TB):
                        ins = nc.vector.tensor_scalar(norm[:, t, :], hid[:, s, t, :], mv[:, t, 0:1], sd[:, t, :],
                                                      ALU.subtract, ALU.mult)
                    ins.then_inc(norm_made, 1)

                def route(it, st):
                    def step(ins):
                        st.did(ins)
                        st.settle()

                    def wide(ap):
                        return view(ap, [[1, TB], [0, EXPERTS]])

                    def const(ap):
                        return view(ap, [[0, TB], [1, EXPERTS]])

                    dve.wait_ge(expo_made, it + 1)
                    step(nc.vector.tensor_scalar(expo[:, :, :], expo[:, :, :], 1.0, None, ALU.add))
                    step(nc.vector.reciprocal(sc[:, :, :], expo[:, :, :]))
                    step(nc.vector.tensor_tensor(sb_[:, :, :], sc[:, :, :], const(bb[:, :]), ALU.add))
                    cur = sb_
                    for pick in (first, second):
                        step(nc.vector.tensor_reduce(top[:, :, 0], cur[:, :, :], AX.X, ALU.max))
                        step(nc.vector.tensor_tensor(eq[:, :, :], cur[:, :, :], wide(top[:, :, 0]), ALU.is_equal))
                        step(nc.vector.tensor_tensor(eq[:, :, :], eq[:, :, :], const(ranks[:, :]), ALU.mult))
                        step(nc.vector.tensor_reduce(top[:, :, 0], eq[:, :, :], AX.X, ALU.max))
                        step(nc.vector.tensor_tensor(pick[:, :, :], eq[:, :, :], wide(top[:, :, 0]), ALU.is_equal))
                        if pick is first:
                            step(nc.vector.scalar_tensor_tensor(left[:, :, :], first[:, :, :], -1e30, sb_[:, :, :], ALU.mult, ALU.add))
                            cur = left
                    step(nc.vector.tensor_tensor(eq[:, :, :], first[:, :, :], second[:, :, :], ALU.add))
                    step(nc.vector.tensor_tensor(weight[:, :, :], eq[:, :, :], sc[:, :, :], ALU.mult))
                    step(nc.vector.reduce_sum(top[:, :, 0], weight[:, :, :], AX.X))
                    step(nc.vector.tensor_scalar(top[:, :, :], top[:, :, :], 1e-20, None, ALU.add))
                    step(nc.vector.reciprocal(top[:, :, :], top[:, :, :]))
                    step(nc.vector.tensor_tensor(gate[:, :, :], weight[:, :, :], wide(top[:, :, 0]), ALU.mult))

                R = 20
                KI = 2 + R

                def relus(it):
                    for n in range(HT // 2):
                        rows = 64 if UPS[2 * n + 1] == 13 else 128
                        dve.wait_ge(up_done, it * HT + 2 * n + 2)
                        if n >= 2:
                            dve.wait_ge(squared, it * HT + 2 * n - 2)
                        nc.vector.tensor_scalar(relu[0:rows, (2 * n + 1) % 4, :], h_bank[1][0:rows, 0:BT], 0.0, None, ALU.max
                                                ).then_inc(relu_made[1], 1)

                def sums(it, s, k):
                    e = DOWNS[k][0]
                    for t in range(TB):
                        n = it * TB * MLPS + k * TB + t
                        dve.wait_ge(down_done, n + 1 + PRIMED)
                        y = y_bank[t][:, 0:DIM]
                        if k == 0:
                            nc.vector.tensor_tensor(acc[:, s, t, :], y, hid[:, s, t, :], ALU.add).then_inc(summed, 1)
                        else:
                            if t == 0:
                                dve.wait_ge(summed, it * TB * MLPS + k * TB + PRIMED)
                            nc.vector.scalar_tensor_tensor(acc[:, s, t, :], y, gate[:, t, e:e + 1], acc[:, s, t, :],
                                                           ALU.mult, ALU.add).then_inc(summed, 1)

                def body(it, s, stores, next_loaded):
                    st = Steps(dve, dve_step, 2 + it * KI)
                    route(it, st)
                    relus(it)
                    dve.wait_ge(acc_out[s], stores + PRIMED)
                    for k in range(3):
                        sums(it, s, k)
                    if next_loaded is not None:
                        dve.wait_ge(hid_in[1 - s], next_loaded)
                        layernorm(it + 1, 1 - s, st)
                        assert st.n == KI, st.n
                    for k in range(3, MLPS):
                        sums(it, s, k)

                dve.wait_ge(w_in, 16 * (2 * MLPS + 6))
                dve.wait_ge(ranks_made, 3)
                nc.vector.memset(eps[:, :], EPS)
                dve.wait_ge(hid_in[0], 16)
                layernorm(0, 0, Steps(dve, dve_step, 0))
                with dve.Fori(0, (BLOCKS - 1) // 2) as pair:
                    ii = pair * 2
                    for s in range(2):
                        body(ii + s, s, ii * 8, ii * 8 + 16 * (s + 1))
                body(BLOCKS - 1, 0, 16 * (BLOCKS // 2), None)

            @block.tensor
            def _(pe):
                def turn(k):
                    pe.wait_ge(norm_made, k + 1)
                    pe.wait_ge(xT_made, k + PRIMED)
                    for t in range(TB):
                        cols = slice(t * 128, (t + 1) * 128)
                        nc.tensor.transpose(t_bank[0][:, cols], norm[:, t, 0:C0], ident[:, :])
                        ins = nc.tensor.transpose(t_bank[1][0:C1, cols], norm[:, t, C0:DIM], ident[:, :])
                    ins.then_inc(turned, 1)

                def up(it, s, n):
                    j = UPS[n]
                    rows = 64 if j == 13 else 128
                    if n % 2 == 0:
                        pe.wait_ge(relu_made[0], it * (HT // 2) + n // 2 + PRIMED)
                    else:
                        pe.wait_ge(relu_made[1], it * (HT // 2) + n // 2 + PRIMED)
                    o = h_bank[n % 2][0:rows, 0:BT]
                    nc.tensor.matmul(o, up0[:, 128 * j:128 * j + rows], xT0[:, s, :], start=True, stop=False)
                    nc.tensor.matmul(o, up1[:, 128 * j:128 * j + rows], xT1[:, s, :], start=False, stop=True).then_inc(up_done, 1)

                def down_(it, k):
                    for t in range(TB):
                        n = it * TB * MLPS + k * TB + t
                        if k:
                            pe.wait_ge(summed, n - TB + 1 + PRIMED)
                        else:
                            pe.wait_ge(summed, it * TB * MLPS + PRIMED)
                        parts = DOWNS[k][1]
                        for i, (j, r0, rows) in enumerate(parts):
                            ins = nc.tensor.matmul(y_bank[t][:, 0:DIM], hidden[r0:r0 + rows, j, t * 128:(t + 1) * 128],
                                                   down[r0:r0 + rows, j, :], start=(i == 0), stop=(i == len(parts) - 1))
                        ins.then_inc(down_done, 1)

                def body(it, s, last=False):
                    pe.wait_ge(xT_made, it + 1 + PRIMED)
                    for t in range(TB):
                        cols = slice(t * 128, (t + 1) * 128)
                        o = r_bank[:, t * EXPERTS:(t + 1) * EXPERTS]
                        nc.tensor.matmul(o, xT0[:, s, cols], rw0[:, :], start=True, stop=False)
                        ins = nc.tensor.matmul(o, xT1[:, s, cols], rw1[:, :], start=False, stop=True)
                    ins.then_inc(routed, 1)
                    for n in range(HT):
                        up(it, s, n)
                    pe.wait_ge(squared, (it + 1) * HT)
                    for k in range(3):
                        down_(it, k)
                    if not last:
                        turn(it + 1)
                    for k in range(3, MLPS):
                        down_(it, k)

                pe.wait_ge(w_in, 16 * (2 * MLPS + 6))
                pe.wait_ge(ranks_made, 2)
                turn(0)
                with pe.Fori(0, (BLOCKS - 1) // 2) as pair:
                    ii = pair * 2
                    body(ii, 0)
                    body(ii + 1, 1)
                body(BLOCKS - 1, 0, last=True)


def vit_tower(nc, x, cls_tok, ln1_g, ln1_b, w_proj, b_proj, ln2_g, ln2_b, pos, cls_token, qkv_w, proj_w, proj_b,
              tab_kv, tab_kh, tab_vv, tab_vh, w_fc_sh, w_proj_sh, w1, w2, router_w, balance_bias, out):
    hidden0 = nc.dram_tensor("hidden0", [B, NTOK, DIM], fp32, kind="Internal").ap()
    hidden1 = nc.dram_tensor("hidden1", [B, NTOK, DIM], fp32, kind="Internal").ap()
    tokens_stage(nc, x, cls_tok, ln1_g, ln1_b, w_proj, b_proj, ln2_g, ln2_b, pos, cls_token, hidden0)
    attention_stage(nc, hidden0, qkv_w, proj_w, proj_b, tab_kv, tab_kh, tab_vv, tab_vh, hidden1)
    experts_stage(nc, hidden1, w_fc_sh, w_proj_sh, w1, w2, router_w, balance_bias, out)


_INS = ['x', 'cls_tok', 'L0_tok_ln1_g', 'L0_tok_ln1_b', 'L0_tok_W_proj', 'L0_tok_b_proj', 'L0_tok_ln2_g',
        'L0_tok_ln2_b', 'L0_tok_pos_embedding', 'L0_tok_cls_token', 'L0_attn_qkv_w', 'L0_attn_proj_w',
        'L0_attn_proj_b', 'L0_attn_tab_kv', 'L0_attn_tab_kh', 'L0_attn_tab_vv', 'L0_attn_tab_vh',
        'L0_ffn_w_fc_sh', 'L0_ffn_w_proj_sh', 'L0_ffn_w1', 'L0_ffn_w2', 'L0_ffn_router_w', 'L0_ffn_balance_bias']


def kernel(**inputs):
    import concourse.bacc as bacc
    from concourse.bass_utils import run_bass_kernel_spmd

    nc = bacc.Bacc("TRN2", target_bir_lowering=False, num_devices=1)
    arrays, args = {}, []
    for name in _INS:
        a = np.ascontiguousarray(inputs[name])
        arrays[f"in_{name}"] = a
        args.append(nc.dram_tensor(f"in_{name}", a.shape, mybir.dt.from_np(a.dtype), kind="ExternalInput").ap())
    args.append(nc.dram_tensor("out_hidden", (B, NTOK, DIM), fp32, kind="ExternalOutput").ap())
    vit_tower(nc, *args)
    r = run_bass_kernel_spmd(nc, [arrays], core_ids=[0])
    return r.results[0]["out_hidden"]
```

```python
import numpy as np
import concourse.bass as bass
from concourse import mybir
from contextlib import ExitStack

fp32 = mybir.dt.float32
ALU = mybir.AluOpType
ACT = mybir.ActivationFunctionType
AX = mybir.AxisListType

B, CH, IMG, PATCH = 64, 3, 224, 16
SIDE = IMG // PATCH
NTOK = SIDE * SIDE + 2
DIM = 192
PDIM = PATCH * PATCH * CH
HEADS, HD = 12, 64
PAIRS = HEADS // 2
EXPERTS = 8
EPS = 1e-5
SCALE = HD ** -0.5
GB = 8
GROUPS = B // GB
GT = GB * NTOK
HALF = NTOK // 2
TILES = 2 * GB
PRIMED = 1
C0, C1 = 128, DIM - 128


class Steps:

    def __init__(self, eng, sem, base=0):
        self.eng, self.sem, self.base, self.n = eng, sem, base, 0

    def did(self, ins):
        ins.then_inc(self.sem, 1)
        self.n += 1

    def settle(self):
        self.eng.wait_ge(self.sem, self.base + self.n)

    def settle_apart(self, passed):
        self.settle()
        self.eng.sem_inc(passed, 1)


class Memory:

    def __init__(self, nc, ctx, stage):
        self.nc, self.ctx, self.stage = nc, ctx, stage

    def sb(self, name, shape, dt=fp32):
        return self.ctx.enter_context(self.nc.sbuf_tensor(f"{self.stage}_{name}", shape, dt))

    def bank(self, name):
        return self.ctx.enter_context(self.nc.psum_tensor(f"{self.stage}_{name}", [128, 512], fp32))

    def sem(self, name):
        return self.ctx.enter_context(self.nc.semaphore(f"{self.stage}_{name}"))


def view(ap, dims, offset=0):
    return bass.AP(tensor=ap.tensor, offset=ap.offset + offset, ap=[list(ap.ap[0])] + [list(d) for d in dims])


def make_identity(pool, nc, ident, sem):
    nc.gpsimd.memset(ident[:, :], 0.0).then_inc(sem, 1)
    pool.wait_ge(sem, 1)
    nc.gpsimd.affine_select(out=ident[:, :], in_=ident[:, :], compare_op=ALU.not_equal, fill=1.0, base=0,
                            pattern=[[-1, 128]], channel_multiplier=1).then_inc(sem, 1)


def tokens_stage(nc, x, cls_tok, ln1_g, ln1_b, w_proj, b_proj, ln2_g, ln2_b, pos, cls_token, hidden0):
    P = GB * SIDE
    KC = PDIM // 128
    XROW = PATCH * IMG
    with ExitStack() as ctx:
        m = Memory(nc, ctx, "tok")
        pixels = m.sb("pixels", [P, 2, CH, XROW])
        normed = m.sb("normed", [P, 2, PDIM])
        patchT = m.sb("patchT", [128, 2, KC, P])
        w = m.sb("w", [128, 2, CH, DIM])
        g1, b1 = m.sb("g1", [128, 2, CH]), m.sb("b1", [128, 2, CH])
        b1x = m.sb("b1x", [128, KC, P])
        bias = m.sb("bias", [P, DIM])
        g2, b2 = m.sb("g2", [P, DIM]), m.sb("b2", [P, DIM])
        posb = m.sb("posb", [P, SIDE, DIM])
        eps = m.sb("eps", [128, 1])
        stat1, mv1 = m.sb("stat1", [P, SIDE, CH, 6]), m.sb("mv1", [P, SIDE, 2])
        rstd1, shift1 = m.sb("rstd1", [P, SIDE, 1]), m.sb("shift1", [P, SIDE, 1])
        stat2, mv2, rstd2 = m.sb("stat2", [P, SIDE, 6]), m.sb("mv2", [P, SIDE, 2]), m.sb("rstd2", [P, SIDE, 1])
        y = m.sb("y", [P, SIDE, DIM])
        rows = m.sb("rows", [P, 2, SIDE, DIM])
        cls = m.sb("cls", [B, 2, DIM])
        clsp = m.sb("clsp", [B, DIM])
        ident = m.sb("ident", [128, 128])
        t_bank = [[m.bank(f"t{v}{i}") for i in range(2)] for v in range(2)]
        y_bank = [m.bank(f"y{v}") for v in range(2)]
        pixels_in = [m.sem(f"pixels_in{s}") for s in range(2)]
        consts_in, weights_in, ident_made = m.sem("consts_in"), m.sem("weights_in"), m.sem("ident_made")
        eps_made = m.sem("eps_made")
        bias_full, w_scaled = m.sem("bias_full"), m.sem("w_scaled")
        dve_step, pool_step, passed = m.sem("dve_step"), m.sem("pool_step"), m.sem("passed")
        mv1_made, sd1_made, shift1_made = m.sem("mv1_made"), m.sem("sd1_made"), m.sem("shift1_made")
        mv2_made, sd2_made, y_made = m.sem("mv2_made"), m.sem("sd2_made"), m.sem("y_made")
        normed_made, turned, patchT_made, projected = (m.sem("normed_made"), m.sem("turned"), m.sem("patchT_made"),
                                                       m.sem("projected"))
        rows_normed, rows_made = m.sem("rows_normed"), m.sem("rows_made")
        rows_out = [m.sem(f"rows_out{s}") for s in range(2)]
        b1x_made, cls_made, cls_out, posb_made = m.sem("b1x_made"), m.sem("cls_made"), m.sem("cls_out"), m.sem("posb_made")
        x_rows = x.rearrange("b c (r p) w -> b r c (p w)", p=PATCH)
        hid_rows = hidden0[:, 2:NTOK, :].rearrange("b (r w) d -> b r w d", w=SIDE)
        WEIGHTS, CONSTS = 4, 2 + GB + 3

        with nc.Block() as block:

            @block.sync
            def _(sp):
                for s in (*rows_out, turned, patchT_made, y_made, rows_normed):
                    sp.sem_inc(s, PRIMED)
                def load(g, s):
                    for j in range(GB):
                        sp.dma_start(pixels[SIDE * j:SIDE * (j + 1), s, :, :],
                                     x_rows[bass.ds(g * GB + j, 1)].rearrange("a r c n -> (a r) c n")
                                     ).then_inc(pixels_in[s], 16)
                def store(g, s):
                    sp.wait_ge(rows_made, g + 1)
                    for j in range(GB):
                        sp.dma_start(hid_rows[bass.ds(g * GB + j, 1)].rearrange("a r w d -> (a r) w d"),
                                     rows[SIDE * j:SIDE * (j + 1), s, :, :]).then_inc(rows_out[s], 16)

                load(0, 0)
                load(1, 1)
                with sp.Fori(0, (GROUPS - 2) // 2) as pair:
                    gg = pair * 2
                    for s in range(2):
                        sp.wait_ge(normed_made, (gg + s + 1) * SIDE)
                        load(gg + s + 2, s)
                        store(gg + s, s)
                sp.sem_inc(pixels_in[0], 16 * GB)
                for s in range(2):
                    store(GROUPS - 2 + s, s)
                for s in range(2):
                    sp.wait_ge(rows_out[s], 16 * GB * (GROUPS // 2) + PRIMED)

            @block.scalar
            def _(act):
                act.wait_ge(eps_made, 1)

                def deviation1(n):
                    act.wait_ge(mv1_made, n)
                    nc.scalar.activation(rstd1[:, :, :], mv1[:, :, 1:2], ACT.Sqrt, bias=eps[0:P, :]).then_inc(sd1_made, 1)

                def normalise(s, wv, t):
                    v = wv % 2
                    if wv >= 2:
                        act.wait_ge(turned, t - 1 + PRIMED)
                    px = view(pixels[:, s, 0, :], [[IMG, CH * PATCH], [1, PATCH]], wv * PATCH)
                    nc.scalar.activation(view(normed[:, v, :], [[PATCH, CH * PATCH], [1, PATCH]]), px, ACT.Identity,
                                         bias=shift1[:, wv, :], scale=rstd1[:, wv, :]).then_inc(normed_made, 1)

                deviation1(1)
                with act.Fori(0, GROUPS // 2) as pair:
                    gg = pair * 2
                    for s in range(2):
                        g = gg + s
                        act.wait_ge(shift1_made, g + 1)
                        normalise(s, 0, g * SIDE)
                        for wv in range(SIDE):
                            v, t = wv % 2, g * SIDE + wv
                            if wv + 1 < SIDE:
                                normalise(s, wv + 1, t + 1)
                            act.wait_ge(turned, t + 1 + PRIMED)
                            for i in range(2):
                                ins = nc.scalar.activation(patchT[:, v, 3 * i:3 * i + 3, :],
                                                           t_bank[v][i][:, 0:3 * P].rearrange("p (k n) -> p k n", k=3),
                                                           ACT.Copy)
                            ins.then_inc(patchT_made, 1)
                        deviation1(g + 2)
                        act.wait_ge(mv2_made, g + 1)
                        nc.scalar.activation(rstd2[:, :, :], mv2[:, :, 1:2], ACT.Sqrt, bias=eps[0:P, :]).then_inc(sd2_made, 1)

            @block.gpsimd
            def _(pool):
                make_identity(pool, nc, ident, ident_made)
                pool.dma_start(w[:, :, :, :], w_proj.rearrange("(h q c) d -> q h c d", q=128, c=CH)).then_inc(weights_in, 16)
                for dst, src in ((g1, ln1_g), (b1, ln1_b)):
                    pool.dma_start(dst[:, :, :], src.rearrange("(h q c) -> q h c", q=128, c=CH)).then_inc(weights_in, 16)
                for dst, src, arrived in ((bias, b_proj, weights_in), (g2, ln2_g, consts_in), (b2, ln2_b, consts_in)):
                    pool.dma_start(dst[:, :], bass.AP(tensor=src.tensor, offset=src.offset, ap=[[0, P], [1, DIM]])
                                   ).then_inc(arrived, 16)
                for j in range(GB):
                    pool.dma_start(posb[SIDE * j:SIDE * (j + 1), :, :],
                                   pos[0, 1:SIDE * SIDE + 1, :].rearrange("(r w) d -> r w d", w=SIDE)).then_inc(consts_in, 16)
                for dst, src in ((cls[:, 0, :], cls_tok[0, 0, :]), (cls[:, 1, :], cls_token[0, 0, :]), (clsp[:, :], pos[0, 0, :])):
                    pool.dma_start(dst, bass.AP(tensor=src.tensor, offset=src.offset, ap=[[0, B], [1, DIM]])
                                   ).then_inc(consts_in, 16)
                pool.wait_ge(consts_in, 16 * CONSTS)
                nc.gpsimd.tensor_tensor(cls[:, 1, :], cls[:, 1, :], clsp[:, :], ALU.add).then_inc(cls_made, 1)
                nc.gpsimd.tensor_tensor(posb[:, :, :], posb[:, :, :],
                                        view(b2[:, :], [[0, SIDE], [1, DIM]]), ALU.add).then_inc(posb_made, 1)
                pool.wait_ge(cls_made, 1)
                pool.dma_start(hidden0[:, 0:2, :], cls[:, :, :]).then_inc(cls_out, 16)
                pool.wait_ge(posb_made, 1)
                with pool.Fori(0, GROUPS // 2) as pair:
                    gg = pair * 2
                    for s in range(2):
                        g = gg + s
                        pool.wait_ge(rows_normed, g + 1 + PRIMED)
                        nc.gpsimd.tensor_tensor(rows[:, s, :, :], rows[:, s, :, :], view(g2[:, :], [[0, SIDE], [1, DIM]]), ALU.mult
                                                ).then_inc(pool_step, 1)
                        pool.wait_ge(pool_step, g + 1)
                        nc.gpsimd.tensor_tensor(rows[:, s, :, :], rows[:, s, :, :], posb[:, :, :], ALU.add).then_inc(rows_made, 1)
                pool.wait_ge(cls_out, 16)

            @block.vector
            def _(dve):
                nc.vector.memset(eps[:, :], EPS).then_inc(eps_made, 1)
                dve.wait_ge(weights_in, 16 * WEIGHTS)
                for k in range(KC):
                    ins = nc.vector.tensor_copy(b1x[:, k, :], b1[:, k % 2, k // 2:k // 2 + 1].broadcast_to([128, P]))
                ins.then_inc(b1x_made, 1)

                def statistics1(s, wv):
                    px = view(pixels[:, s, 0, :], [[IMG, CH * PATCH], [1, PATCH]], wv * PATCH)
                    for c in range(CH):
                        ins = nc.vector.bn_stats(stat1[:, wv, c, :], view(pixels[:, s, c, :], [[IMG, PATCH], [1, PATCH]], wv * PATCH))
                    return ins

                def aggregate(st, mv, stat, made):
                    st.settle_apart(passed)
                    for wv in range(SIDE):
                        ins = nc.vector.bn_aggr(mv[:, wv, :], stat[:, wv, :, :] if len(stat.shape) == 4 else stat[:, wv, :])
                    ins.then_inc(made, 1)

                def scale_shift1(st, n):
                    dve.wait_ge(sd1_made, n)
                    st.did(nc.vector.reciprocal(rstd1[:, :, :], rstd1[:, :, :]))
                    st.settle()
                    nc.vector.scalar_tensor_tensor(shift1[:, :, :], mv1[:, :, 0:1], -1.0, rstd1[:, :, :], ALU.mult, ALU.mult
                                                   ).then_inc(shift1_made, 1)

                st = Steps(dve, dve_step, 0)
                dve.wait_ge(pixels_in[0], 16 * GB)
                for wv in range(SIDE):
                    ins = statistics1(0, wv)
                st.did(ins)
                aggregate(st, mv1, stat1, mv1_made)
                dve.wait_ge(bias_full, 1)
                nc.vector.tensor_tensor(bias[:, :], y_bank[0][0:P, 0:DIM], bias[:, :], ALU.add)
                for k in range(KC):
                    ins = nc.vector.tensor_scalar(w[:, k % 2, k // 2, :], w[:, k % 2, k // 2, :], g1[:, k % 2, k // 2:k // 2 + 1], None, ALU.mult)
                ins.then_inc(w_scaled, 1)
                scale_shift1(st, 1)
                dve.wait_ge(w_scaled, 1)
                PER_GROUP = SIDE + 3
                with dve.Fori(0, GROUPS // 2) as pair:
                    gg = pair * 2
                    for s in range(2):
                        g = gg + s
                        st = Steps(dve, dve_step, 2 + g * PER_GROUP)
                        dve.wait_ge(pixels_in[1 - s], gg * (8 * GB) + 16 * GB * (s + 1))
                        dve.wait_ge(rows_normed, g + PRIMED)
                        for wv in range(SIDE + 1):
                            t = g * SIDE + wv - 1
                            if wv:
                                dve.wait_ge(projected, t + 1)
                                nc.vector.tensor_tensor(y[:, wv - 1, :], y_bank[(wv - 1) % 2][0:P, 0:DIM], bias[:, :], ALU.add
                                                        ).then_inc(y_made, 1)
                            if wv < SIDE:
                                ins = statistics1(1 - s, wv)
                                if wv == SIDE - 1:
                                    st.did(ins)
                            if wv:
                                dve.wait_ge(y_made, t + 1 + PRIMED)
                                st.did(nc.vector.bn_stats(stat2[:, wv - 1, :], y[:, wv - 1, :]))
                        dve.wait_ge(normed_made, (g + 1) * SIDE)
                        aggregate(st, mv1, stat1, mv1_made)
                        aggregate(st, mv2, stat2, mv2_made)
                        scale_shift1(st, g + 2)
                        dve.wait_ge(sd2_made, g + 1)
                        st.did(nc.vector.reciprocal(rstd2[:, :, :], rstd2[:, :, :]))
                        st.settle()
                        dve.wait_ge(rows_out[s], gg * (8 * GB) + PRIMED)
                        for wv in range(SIDE):
                            ins = nc.vector.tensor_scalar(rows[:, s, wv, :], y[:, wv, :], mv2[:, wv, 0:1], rstd2[:, wv, :],
                                                          ALU.subtract, ALU.mult)
                            if wv == SIDE - 1:
                                ins.then_inc(rows_normed, 1)
                        assert st.n == PER_GROUP, st.n

            @block.tensor
            def _(pe):
                pe.wait_ge(b1x_made, 1)
                for k in range(KC):
                    ins = nc.tensor.matmul(y_bank[0][0:P, 0:DIM], b1x[:, k, :], w[:, k % 2, k // 2, :], start=(k == 0), stop=(k == KC - 1))
                ins.then_inc(bias_full, 1)
                pe.wait_ge(w_scaled, 1)
                pe.wait_ge(ident_made, 2)

                def turn(wv, t, g):
                    v = wv % 2
                    pe.wait_ge(normed_made, t + 1)
                    if wv >= 2:
                        pe.wait_ge(patchT_made, t - 1 + PRIMED)
                    else:
                        pe.wait_ge(patchT_made, g * SIDE + PRIMED)
                    for k in range(KC):
                        ins = nc.tensor.transpose(t_bank[v][k // 3][:, (k % 3) * P:(k % 3 + 1) * P],
                                                  normed[:, v, 128 * k:128 * (k + 1)], ident[0:P, 0:P])
                    ins.then_inc(turned, 1)

                def project(wv, t, g):
                    v = wv % 2
                    pe.wait_ge(patchT_made, t + 1 + PRIMED)
                    if wv >= 2:
                        pe.wait_ge(y_made, t - 1 + PRIMED)
                    else:
                        pe.wait_ge(y_made, g * SIDE + PRIMED)
                    for k in range(KC):
                        ins = nc.tensor.matmul(y_bank[v][0:P, 0:DIM], patchT[:, v, k, :], w[:, k % 2, k // 2, :],
                                               start=(k == 0), stop=(k == KC - 1))
                    ins.then_inc(projected, 1)

                with pe.Fori(0, GROUPS) as g:
                    for wv in range(SIDE + 1):
                        if wv < SIDE:
                            turn(wv, g * SIDE + wv, g)
                        if wv:
                            project(wv - 1, g * SIDE + wv - 1, g)


def attention_stage(nc, hidden0, qkv_w, proj_w, proj_b, tab_kv, tab_kh, tab_vv, tab_vh, hidden1):
    ROWS = 30
    EXT = 32
    NG = 30
    CLSG = 15
    HC = 396
    UNIT = TILES
    STEPS = PAIRS * UNIT
    TURN, FIRST, LAST = 8, 20, 16
    with ExitStack() as ctx:
        m = Memory(nc, ctx, "att")
        hid = m.sb("hid", [HALF, TILES, DIM])
        resid = m.sb("resid", [HALF, TILES, DIM])
        norm = m.sb("norm", [HALF, 4, DIM])
        xT0, xT1 = m.sb("xT0", [C0, GT]), m.sb("xT1", [C1, GT])
        wT0, wT1 = m.sb("wT0", [C0, 3, PAIRS, 128]), m.sb("wT1", [C1, 3, PAIRS, 128])
        pw = m.sb("pw", [128, PAIRS, DIM])
        pbias = m.sb("pbias", [HALF, DIM])
        q2 = m.sb("q2", [128, GT])
        qx, kx = m.sb("qx", [128, 2, 2, GT]), m.sb("kx", [128, 2, 2, GT])
        vx = m.sb("vx", [HALF, 2, TILES, 160])
        oT = m.sb("oT", [128, 2, GT])
        rx = m.sb("rx", [96, 2, GT])
        tq = m.sb("tq", [128, NG, 64])
        tv = m.sb("tv", [96, NG, 128])
        tabT = m.sb("tabT", [128, 2, ROWS])
        onehot = m.sb("onehot", [EXT, 1 + 15 * SIDE])
        rowhot = m.sb("rowhot", [EXT, 1 + 15 * SIDE])
        ident = m.sb("ident", [128, 128])
        prob = m.sb("prob", [HALF, 2, 2, NTOK])
        probT = m.sb("probT", [HALF, 2, 2 * NTOK])
        npeak, total = m.sb("npeak", [HALF, 2, 2]), m.sb("total", [HALF, 2, 2])
        stat, mv, sd = m.sb("stat", [HALF, TILES, 6]), m.sb("mv", [HALF, TILES, 2]), m.sb("sd", [HALF, TILES, 1])
        eps = m.sb("eps", [128, 1])
        p_bank = [m.bank(f"p{i}") for i in range(2)]
        s_bank = [m.bank(f"s{i}") for i in range(2)]
        t_bank = [m.bank(f"t{i}") for i in range(2)]
        o_bank = [m.bank(f"o{i}") for i in range(2)]
        mv_made, sd_made = m.sem("mv_made"), m.sem("sd_made")
        consts_in, onehot_made, zeroed = m.sem("consts_in"), m.sem("onehot_made"), m.sem("zeroed")
        tables_in, tables_made, raw_in = m.sem("tables_in"), m.sem("tables_made"), m.sem("raw_in")
        hid_in, resid_made = m.sem("hid_in"), m.sem("resid_made")
        norm_made, dve_step, passed = m.sem("norm_made"), m.sem("dve_step"), m.sem("passed")
        full = [m.sem(f"full{i}") for i in range(2)]
        free = [m.sem(f"free{i}") for i in range(2)]
        prep_full, prep_free = m.sem("prep_full"), [m.sem(f"prep_free{i}") for i in range(2)]
        cleared = m.sem("cleared")
        scores, peaks, exps, probs, turned, probT_made, outs, outs_used = (
            m.sem("scores"), m.sem("peaks"), m.sem("exps"), m.sem("probs"), m.sem("turned"), m.sem("probT_made"),
            m.sem("outs"), m.sem("outs_used"))
        hidden_out = m.sem("hidden_out")

        h0_tiles = hidden0.rearrange("b (h p) d -> p (b h) d", p=HALF)
        h1_tiles = hidden1.rearrange("b (h p) d -> p (b h) d", p=HALF)
        QROWS = 3 * HEADS * HD

        def q_cols(a):
            if a < CLSG:
                row = 14 - a
                return 1 + SIDE * row, (SIDE if row < SIDE else 1), 1
            if a == CLSG:
                return 0, 1, 1
            return 1 + (13 - (a - 16)), SIDE, SIDE

        def group_rhs(src, a):
            off, n, step = q_cols(a)
            return view(src, [[NTOK, GB], [step, n]], off)

        ROWBANKS = [[(CLSG, 0)] + [(14 - r, 1 + SIDE * r) for r in range(4)],
                    [(14 - r, SIDE * (r - 4)) for r in range(4, 8)],
                    [(14 - r, SIDE * (r - 8)) for r in range(8, 12)],
                    [(14 - r, SIDE * (r - 12)) for r in range(12, 15)]]
        ROWSPAN = [(0, 57), (57, 56), (113, 56), (169, 29)]
        COLBANKS = [range(0, 4), range(4, 8), range(8, 12), range(12, 14)]

        def prep_jobs():
            return [("qkv", t) for t in range(QROWS // 128)] + [("proj", p) for p in range(PAIRS)]

        RAW = GT // DIM * 2
        raw_qkv = [view(oT[:, :, :], [[1, DIM]], t * DIM) for t in range(RAW)]
        raw_qkv += [q2[:, (t - RAW) * DIM:(t - RAW + 1) * DIM] for t in range(RAW, QROWS // 128)]
        raw_lo, raw_hi = (QROWS // 128 - RAW) * DIM, (QROWS // 128 - RAW) * DIM + HEADS * HD
        raw_p0, raw_p1 = q2[:, raw_lo:raw_hi], xT1[:, 0:HEADS * HD]

        def first_jobs(p):
            return [("first", p, j) for j in range(FIRST)]

        def last_jobs(p):
            return [("last", p, j) for j in range(LAST)]

        opening = [("turn", 0, j) for j in range(TURN)] + first_jobs(0)
        between = [[] for _ in range(STEPS)]
        for p in range(PAIRS):
            f, l = (first_jobs(p + 1) if p + 1 < PAIRS else []), (last_jobs(p - 1) if p else [])
            jobs = f[:12] + l[:4] + f[12:14] + l[4:8] + f[14:17] + l[8:11] + f[17:] + l[11:]
            begin = 5 if p + 1 == PAIRS else 0
            for k, job in enumerate(jobs):
                between[p * UNIT + begin + k * (UNIT - begin) // len(jobs)].append(job)
        closing = last_jobs(PAIRS - 1)
        order = {job: k for k, job in enumerate(opening + [j for js in between for j in js] + closing)}
        G_JOBS = len(order) // 2

        def through(base, kind, p, j, bank):
            k = order[kind, p, j]
            return base + k // 2 + (1 if k % 2 >= bank else 0)

        with nc.Block() as block:

            @block.sync
            def _(sp):
                for s in (hidden_out, *free):
                    sp.sem_inc(s, PRIMED)
                sp.dma_start(hid[:, :, :], h0_tiles[:, 0:TILES, :]).then_inc(hid_in, 16)
                sp.wait_ge(cleared, 1)
                for half, head in ((64, 0), (32, 1)):
                    def rows_of(p, n, a, na, tab, first, astep):
                        sp.dma_start(tv[half + p:half + p + n, a:a + na, 64 * head:64 * head + 64],
                                       bass.AP(tensor=tab.tensor, offset=tab.offset + first * HD,
                                               ap=[[HD if astep >= 0 else 0, n], [max(astep, 0) * HD, na], [1, HD]])
                                       ).then_inc(tables_in, 16)
                    rows_of(0, 15, 0, 15, tab_vv, 1, 1)
                    rows_of(15, 1, 0, 15, tab_vv, 0, 0)
                    rows_of(0, 16, CLSG, 1, tab_vv, 0, -1)
                    rows_of(16, 15, CLSG, 1, tab_vh, 0, -1)
                    rows_of(16, 14, 0, 1, tab_vh, 15, 0)
                    rows_of(30, 1, 0, 1, tab_vh, 0, 0)
                    rows_of(16, 14, 16, 14, tab_vh, 2, 1)
                    rows_of(30, 1, 16, 14, tab_vh, 0, 0)
                with sp.Fori(0, GROUPS) as g:
                    sp.wait_ge(norm_made, (g + 1) * TURN)
                    sp.wait_ge(resid_made, g + 1)
                    sp.dma_start(hid[:, :, :], h0_tiles[:, bass.ds(((g + 1) % GROUPS) * TILES, TILES), :]).then_inc(hid_in, 16)
                    for bank in range(2):
                        sp.wait_ge(free[bank], (g + 1) * G_JOBS + PRIMED)
                    sp.dma_start(h1_tiles[:, bass.ds(g * TILES, TILES), :], resid[:, :, :]).then_inc(hidden_out, 16)
                sp.wait_ge(hid_in, 16 * (GROUPS + 1))
                sp.wait_ge(hidden_out, 16 * GROUPS + PRIMED)

            @block.gpsimd
            def _(pool):
                make_identity(pool, nc, ident, onehot_made)
                W = 1 + 15 * SIDE
                nc.gpsimd.memset(onehot[:, :], 0.0)
                nc.gpsimd.memset(rowhot[:, :], 1.0).then_inc(onehot_made, 1)
                cols = onehot[:, 1:W].rearrange("p (r c) -> p r c", c=SIDE)
                for n, (dst, pattern, base, mult, op, fill) in enumerate((
                        (cols, [[0, 15], [1, SIDE]], 16, -1, ALU.not_equal, 1.0),
                        (onehot[:, 0:1], [[0, 1]], -15, 1, ALU.not_equal, 1.0),
                        (onehot[:, 0:1], [[0, 1]], -30, 1, ALU.not_equal, 1.0),
                        (rowhot[:, :], [[1, W]], -1, -SIDE, ALU.is_ge, 0.0),
                        (rowhot[:, :], [[-1, W]], SIDE, SIDE, ALU.is_ge, 0.0))):
                    pool.wait_ge(onehot_made, 3 + n)
                    nc.gpsimd.affine_select(out=dst, in_=dst, compare_op=op, fill=fill, base=base, pattern=pattern,
                                            channel_multiplier=mult).then_inc(onehot_made, 1)
                pool.wait_ge(onehot_made, 8)
                nc.gpsimd.tensor_tensor(onehot[:, :], onehot[:, :], rowhot[:, :], ALU.add).then_inc(onehot_made, 1)

                for half in range(2):
                    for i, tab in enumerate((tab_kv, tab_kh)):
                        with nc.allow_non_contiguous_dma(reason="a small table, transposed"):
                            pool.dma_start(tabT[64 * half:64 * half + 64, i, :], tab.rearrange("r d -> d r")).then_inc(consts_in, 16)
                pool.dma_start(pbias[:, :], bass.AP(tensor=proj_b.tensor, offset=proj_b.offset, ap=[[0, HALF], [1, DIM]])
                               ).then_inc(consts_in, 16)
                for t in (qx, rx):
                    ins = nc.gpsimd.memset(t[:], 0.0)
                ins.then_inc(zeroed, 1)
                pool.wait_ge(consts_in, 16 * 5)

                with pool.Fori(0, GROUPS) as g:
                    pool.wait_ge(hid_in, g * 16 + 16)
                    pool.wait_ge(hidden_out, g * 16 + PRIMED)
                    nc.gpsimd.tensor_tensor(resid[:, :, :], hid[:, :, :], view(pbias[:, :], [[0, TILES], [1, DIM]]),
                                            ALU.add).then_inc(resid_made, 1)

            @block.scalar
            def _(act):
                for src, dst in ((qkv_w[0:128 * RAW, :].rearrange("(t p) c -> p t c", p=128),
                                  view(oT[:, :, :], [[DIM, RAW], [1, DIM]])),
                                 (qkv_w[128 * RAW:QROWS, :].rearrange("(t p) c -> p t c", p=128),
                                  view(q2[:, :], [[DIM, QROWS // 128 - RAW], [1, DIM]])),
                                 (proj_w[0:128, :], raw_p0), (proj_w[128:DIM, :], raw_p1)):
                    act.dma_start(dst, src).then_inc(raw_in, 16)
                for n in range(1, len(prep_jobs()), 2):
                    kind, t = prep_jobs()[n]
                    act.wait_ge(prep_full, n + 1)
                    bank = p_bank[1]
                    if kind == "qkv":
                        nc.scalar.activation(wT0[:, t // 6, t % 6, :], bank[:, 0:128], ACT.Copy)
                        nc.scalar.activation(wT1[:, t // 6, t % 6, :], bank[0:C1, 128:256], ACT.Copy).then_inc(prep_free[1], 1)
                    else:
                        nc.scalar.activation(pw[:, t, 0:DIM], bank[:, 0:DIM], ACT.Copy).then_inc(prep_free[1], 1)

                act.wait_ge(tables_made, 1)
                act.wait_ge(mv_made, 1)
                nc.scalar.activation(sd[:, :, :], mv[:, :, 1:2], ACT.Sqrt, bias=eps[0:HALF, :]).then_inc(sd_made, 1)
                with act.Fori(0, GROUPS) as g:
                    base = g * G_JOBS

                    def job(kind, p, j):
                        k, s = order[kind, p, j], p % 2
                        if kind == "last" or (kind == "first" and 12 <= j < 16):
                            return
                        bank = p_bank[k % 2]
                        act.wait_ge(full[k % 2], base + k // 2 + 1)
                        if kind == "turn":
                            cols = slice(j * NTOK, (j + 1) * NTOK)
                            nc.scalar.activation(xT0[:, cols], bank[:, 0:NTOK], ACT.Copy)
                            ins = nc.scalar.activation(xT1[:, cols], bank[0:C1, NTOK:2 * NTOK], ACT.Copy)
                        elif j < 4:
                            cols = slice(j * HC, (j + 1) * HC)
                            nc.scalar.activation(q2[:, cols], bank[:, 0:HC], ACT.Copy, scale=SCALE)
                            nc.scalar.activation(qx[0:64, s, 0, cols], bank[0:64, 0:HC], ACT.Copy, scale=SCALE)
                            ins = nc.scalar.activation(qx[64:128, s, 1, cols], bank[64:128, 0:HC], ACT.Copy, scale=SCALE)
                        elif j < 8:
                            cols = slice((j - 4) * HC, (j - 3) * HC)
                            nc.scalar.activation(kx[0:64, s, 0, cols], bank[0:64, 0:HC], ACT.Copy)
                            ins = nc.scalar.activation(kx[64:128, s, 1, cols], bank[64:128, 0:HC], ACT.Copy)
                        elif j < 12:
                            first, n = ROWSPAN[j - 8]
                            for src, lo, head in ((32, 64, 0), (0, 32, 1)):
                                ins = nc.scalar.activation(view(qx[lo:lo + 32, s, head, :], [[NTOK, GB], [1, n]], first),
                                                           view(bank[src:src + 32, :], [[n, GB], [1, n]]), ACT.Copy)
                        else:
                            ins = nc.scalar.activation(
                                view(vx[:, s, 4 * (j - 16):4 * (j - 15), :], [[160, 4], [96, 2], [1, HD]]),
                                view(bank[0:HALF, :], [[128, 4], [HD, 2], [1, HD]]), ACT.Copy)
                        ins.then_inc(free[k % 2], 1)

                    for j in opening:
                        job(*j)
                    for i in range(STEPS + 2):
                        n = g * STEPS + i
                        if i < STEPS:
                            act.wait_ge(peaks, n + 1)
                            if i >= 2:
                                act.wait_ge(turned, n - 1)
                            for h in range(2):
                                ins = nc.scalar.activation(prob[:, i % 2, h, :], s_bank[i % 2][0:HALF, h * NTOK:(h + 1) * NTOK],
                                                           ACT.Exp, bias=npeak[:, i % 2, h:h + 1],
                                                           accum_out=total[:, i % 2, h:h + 1])
                            ins.then_inc(exps, 1)
                            for j in between[i]:
                                job(*j)
                        if i >= 2:
                            act.wait_ge(turned, n - 2 + 1)
                            if i >= 4:
                                act.wait_ge(outs, n - 3)
                            nc.scalar.activation(probT[:, i % 2, :], t_bank[i % 2][0:HALF, 0:2 * NTOK], ACT.Copy
                                                 ).then_inc(probT_made, 1)
                    act.wait_ge(mv_made, g + 2)
                    nc.scalar.activation(sd[:, :, :], mv[:, :, 1:2], ACT.Sqrt, bias=eps[0:HALF, :]).then_inc(sd_made, 1)

            @block.vector
            def _(dve):
                nc.vector.memset(eps[:, :], EPS)
                for t in (tv, tq, kx):
                    nc.vector.memset(t[:], 0.0).then_inc(cleared, 1)
                PER_GROUP = 1 + STEPS + TILES
                st = Steps(dve, dve_step, 0)
                dve.wait_ge(hid_in, 16)
                for t in range(TILES):
                    ins = nc.vector.bn_stats(stat[:, t, :], hid[:, t, :])
                st.did(ins)
                st.settle_apart(passed)
                for t in range(TILES):
                    ins = nc.vector.bn_aggr(mv[:, t, :], stat[:, t, :])
                ins.then_inc(mv_made, 1)
                dve.wait_ge(consts_in, 16 * 5)
                dve.wait_ge(cleared, 3)
                for lo, at in ((0, 32), (64, 0)):
                    src = tabT[lo:lo + 64, :, :]

                    def table(a, na, col, n, which, first, cstep, astep):
                        nc.vector.tensor_copy(tq[lo:lo + 64, a:a + na, at + col:at + col + n],
                                              view(src, [[astep, na], [cstep, n]], which * ROWS + first))
                    table(0, 15, 0, 15, 0, 1, 1, 1)
                    table(0, 15, 15, 1, 0, 0, 0, 0)
                    table(CLSG, 1, 0, 16, 0, 0, 0, 0)
                    table(CLSG, 1, 16, 15, 1, 0, 0, 0)
                    table(0, 1, 16, 14, 1, 15, 1, 0)
                    table(0, 1, 30, 1, 1, 0, 0, 0)
                    table(16, 14, 16, 14, 1, 2, 1, 1)
                    table(16, 14, 30, 1, 1, 0, 0, 0)
                dve.wait_ge(onehot_made, 9)
                for s in range(2):
                    for lo, head in ((64, 0), (32, 1)):
                        ins = nc.vector.tensor_copy(view(kx[lo:lo + 32, s, head, :], [[NTOK, GB], [1, NTOK]]),
                                                    view(onehot[:, :], [[0, GB], [1, NTOK]]))
                ins.then_inc(tables_made, 1)
                for n in range(0, len(prep_jobs()), 2):
                    kind, t = prep_jobs()[n]
                    dve.wait_ge(prep_full, n + 1)
                    bank = p_bank[0]
                    if kind == "qkv":
                        nc.vector.tensor_copy(wT0[:, t // 6, t % 6, :], bank[:, 0:128])
                        nc.vector.tensor_copy(wT1[:, t // 6, t % 6, :], bank[0:C1, 128:256]).then_inc(prep_free[0], 1)
                    else:
                        nc.vector.tensor_copy(pw[:, t, 0:DIM], bank[:, 0:DIM]).then_inc(prep_free[0], 1)
                for h in range(2):
                    dve.wait_ge(prep_full, 1 + h + len(prep_jobs()))
                    for s in range(2):
                        ins = nc.vector.tensor_copy(view(vx[:, s, h:h + 1, 64:96], [[2 * 160, GB], [1, EXT]]),
                                                    view(s_bank[h][0:HALF, 0:EXT], [[0, GB], [1, EXT]]))
                ins.then_inc(tables_made, 1)

                with dve.Fori(0, GROUPS) as g:
                    st = Steps(dve, dve_step, 1 + g * PER_GROUP)
                    base = g * G_JOBS
                    dve.wait_ge(sd_made, g + 1)
                    st.did(nc.vector.reciprocal(sd[:, :, :], sd[:, :, :]))
                    st.settle()
                    for j in range(TURN):
                        if j >= 2:
                            dve.wait_ge(full[j % 2], base + j // 2)
                        for t in (2 * j, 2 * j + 1):
                            ins = nc.vector.tensor_scalar(norm[:, t % 4, :], hid[:, t, :], mv[:, t, 0:1], sd[:, t, :],
                                                          ALU.subtract, ALU.mult)
                        ins.then_inc(norm_made, 1)

                    def job(kind, p, j):
                        k, s = order[kind, p, j], p % 2
                        bank, up_to = p_bank[k % 2], base + k // 2 + 1
                        if kind == "first" and 12 <= j < 16:
                            span = COLBANKS[j - 12]
                            n = len(span)
                            if j == 12:
                                for b in range(2):
                                    dve.wait_ge(free[b], through(base, kind, p, 11, b) + PRIMED)
                            dve.wait_ge(full[k % 2], up_to)
                            for src, lo, head in ((32, 64, 0), (0, 32, 1)):
                                dst = view(qx[lo:lo + 32, s, head, :], [[NTOK, GB], [SIDE, SIDE], [1, n]], 1 + span[0])
                                ins = nc.vector.tensor_tensor(
                                    dst, view(bank[src:src + 32, :], [[n * SIDE, GB], [1, SIDE], [SIDE, n]]), dst, ALU.add)
                        elif kind == "last" and j < 4:
                            first, n = ROWSPAN[j]
                            if j == 0:
                                dve.wait_ge(outs_used, g * STEPS + (p + 1) * UNIT)
                            dve.wait_ge(full[k % 2], up_to)
                            dst = view(oT[:, s, :], [[NTOK, GB], [1, n]], first)
                            ins = nc.vector.tensor_tensor(dst, view(bank[:, :], [[n, GB], [1, n]]), dst, ALU.add)
                        elif kind == "last" and j < 8:
                            span = COLBANKS[j - 4]
                            n = len(span)
                            if j == 4:
                                for b in range(2):
                                    dve.wait_ge(free[b], through(base, kind, p, 3, b) + PRIMED)
                            dve.wait_ge(full[k % 2], up_to)
                            dst = view(oT[:, s, :], [[NTOK, GB], [SIDE, SIDE], [1, n]], 1 + span[0])
                            ins = nc.vector.tensor_tensor(
                                dst, view(bank[:, :], [[n * SIDE, GB], [1, SIDE], [SIDE, n]]), dst, ALU.add)
                        elif kind == "last":
                            if p == 0:
                                dve.wait_ge(resid_made, g + 1)
                            elif j == 8:
                                for b in range(2):
                                    dve.wait_ge(free[b], through(base, kind, p - 1, 15, b) + PRIMED)
                            dve.wait_ge(full[k % 2], up_to)
                            dst = resid[:, 2 * (j - 8):2 * (j - 7), :]
                            ins = nc.vector.tensor_tensor(dst, bank[0:HALF, 0:2 * DIM].rearrange("p (t d) -> p t d", t=2),
                                                          dst, ALU.add)
                        else:
                            return
                        ins.then_inc(free[k % 2], 1)

                    for j in opening:
                        job(*j)
                    for i in range(STEPS + 4):
                        n = g * STEPS + i
                        if i < STEPS:
                            dve.wait_ge(scores, n + 1)
                            nc.vector.tensor_reduce(npeak[:, i % 2, :], s_bank[i % 2][0:HALF, 0:2 * NTOK].rearrange(
                                "p (h k) -> p h k", h=2), AX.X, ALU.max, negate=True).then_inc(peaks, 1)
                        if i >= 4:
                            j = i - 4
                            p, b, head = j // UNIT, j % UNIT // 2, j % 2
                            dve.wait_ge(outs, n - 4 + 1)
                            cols = slice(b * NTOK, (b + 1) * NTOK)
                            lo, ext = (64, 32) if head else (0, 64)
                            nc.vector.tensor_copy(oT[lo:lo + 64, p % 2, cols], o_bank[j % 2][lo:lo + 64, 0:NTOK])
                            nc.vector.tensor_copy(rx[ext:ext + 32, p % 2, cols], o_bank[j % 2][ext:ext + 32, 0:NTOK]
                                                  ).then_inc(outs_used, 1)
                        if 1 <= i <= STEPS:
                            j = i - 1
                            dve.wait_ge(exps, n - 1 + 1)
                            st.did(nc.vector.reciprocal(total[:, j % 2, :], total[:, j % 2, :]))
                            st.settle()
                            for h in range(2):
                                ins = nc.vector.tensor_scalar(prob[:, j % 2, h, :], prob[:, j % 2, h, :],
                                                              total[:, j % 2, h:h + 1], None, ALU.mult)
                            ins.then_inc(probs, 1)
                        if i < STEPS:
                            for j in between[i]:
                                job(*j)
                        if 4 * UNIT <= i < 5 * UNIT:
                            t = i - 4 * UNIT
                            if t == 0:
                                dve.wait_ge(hid_in, (g + 2) * 16)
                            st.did(nc.vector.bn_stats(stat[:, t, :], hid[:, t, :]))
                        elif 5 * UNIT <= i < 6 * UNIT:
                            t = i - 5 * UNIT
                            if t == 0:
                                st.settle_apart(passed)
                            ins = nc.vector.bn_aggr(mv[:, t, :], stat[:, t, :])
                            if t == TILES - 1:
                                ins.then_inc(mv_made, 1)
                    for j in closing:
                        job(*j)
                    assert st.n == PER_GROUP

            @block.tensor
            def _(pe):
                pe.wait_ge(onehot_made, 9)
                pe.wait_ge(raw_in, 16 * 4)
                for n, (kind, t) in enumerate(prep_jobs()):
                    if n >= 2:
                        pe.wait_ge(prep_free[n % 2], n // 2)
                    bank = p_bank[n % 2]
                    if kind == "qkv":
                        nc.tensor.transpose(bank[:, 0:128], raw_qkv[t][:, 0:C0], ident[:, :])
                        ins = nc.tensor.transpose(bank[0:C1, 128:256], raw_qkv[t][:, C0:DIM], ident[:, :])
                    else:
                        cols = slice(128 * t, 128 * t + 128)
                        nc.tensor.transpose(bank[:, 0:128], raw_p0[:, cols], ident[:, :])
                        ins = nc.tensor.transpose(bank[:, 128:DIM], raw_p1[:, cols], ident[0:C1, 0:C1])
                    ins.then_inc(prep_full, 1)
                for h in range(2):
                    nc.tensor.transpose(s_bank[h][0:HALF, 0:EXT], onehot[:, h * HALF:(h + 1) * HALF], ident[0:EXT, 0:EXT]
                                        ).then_inc(prep_full, 1)
                for b in range(2):
                    pe.wait_ge(prep_free[b], len(prep_jobs()) // 2)
                pe.wait_ge(tables_made, 2)
                pe.wait_ge(zeroed, 1)
                pe.wait_ge(tables_in, 16 * 16)

                with pe.Fori(0, GROUPS) as g:
                    base = g * G_JOBS

                    def all_read(kind, p, j, banks=(0, 1)):
                        for b in banks:
                            pe.wait_ge(free[b], through(base, kind, p, j, b) + PRIMED)

                    def job(kind, p, j):
                        k, s = order[kind, p, j], p % 2
                        bank = p_bank[k % 2]
                        other = (1 - k % 2,)
                        if kind == "turn":
                            pe.wait_ge(norm_made, g * TURN + j + 1)
                        if kind == "first" and j == 0 and p == 0:
                            all_read("turn", 0, TURN - 1, other)
                        if kind == "first" and j == 8:
                            all_read("first", p, 3, other)
                        if kind == "last" and j == 0:
                            pe.wait_ge(outs_used, g * STEPS + (p + 1) * UNIT)
                        if kind == "last" and j == 8:
                            all_read("last", p, 7, other)
                        pe.wait_ge(free[k % 2], base + k // 2 + PRIMED)
                        if kind == "turn":
                            for t in range(2):
                                src = norm[:, (2 * j + t) % 4, :]
                                nc.tensor.transpose(bank[:, t * HALF:(t + 1) * HALF], src[:, 0:C0], ident[0:HALF, 0:HALF])
                                ins = nc.tensor.transpose(bank[0:C1, NTOK + t * HALF:NTOK + (t + 1) * HALF], src[:, C0:DIM],
                                                          ident[0:HALF, 0:HALF])
                        elif kind == "first" and j < 8:
                            cols = slice(j % 4 * HC, (j % 4 + 1) * HC)
                            nc.tensor.matmul(bank[:, 0:HC], wT0[:, j // 4, p, :], xT0[:, cols], start=True, stop=False)
                            ins = nc.tensor.matmul(bank[:, 0:HC], wT1[:, j // 4, p, :], xT1[:, cols], start=False, stop=True)
                        elif kind == "first" and j < 12:
                            n = ROWSPAN[j - 8][1]
                            for a, col in ROWBANKS[j - 8]:
                                ins = nc.tensor.matmul(view(bank[0:64, :], [[n, GB], [1, q_cols(a)[1]]], col), tq[:, a, :],
                                                       group_rhs(q2[:, :], a), start=True, stop=True)
                        elif kind == "first" and j < 16:
                            span = COLBANKS[j - 12]
                            n = len(span)
                            for i, c in enumerate(span):
                                ins = nc.tensor.matmul(view(bank[0:64, :], [[n * SIDE, GB], [1, SIDE]], i * SIDE), tq[:, 16 + 13 - c, :],
                                                       group_rhs(q2[:, :], 16 + 13 - c), start=True, stop=True)
                        elif kind == "first":
                            for t in range(4):
                                cols = slice((4 * (j - 16) + t) * HALF, (4 * (j - 16) + t + 1) * HALF)
                                out = bank[0:HALF, t * 128:(t + 1) * 128]
                                nc.tensor.matmul(out, xT0[:, cols], wT0[:, 2, p, :], start=True, stop=False)
                                ins = nc.tensor.matmul(out, xT1[:, cols], wT1[:, 2, p, :], start=False, stop=True)
                        elif j < 4:
                            n = ROWSPAN[j][1]
                            for a, col in ROWBANKS[j]:
                                ins = nc.tensor.matmul(view(bank[:, :], [[n, GB], [1, q_cols(a)[1]]], col), tv[:, a, :],
                                                       group_rhs(rx[:, s, :], a), start=True, stop=True)
                        elif j < 8:
                            span = COLBANKS[j - 4]
                            n = len(span)
                            for i, c in enumerate(span):
                                ins = nc.tensor.matmul(view(bank[:, :], [[n * SIDE, GB], [1, SIDE]], i * SIDE), tv[:, 16 + 13 - c, :],
                                                       group_rhs(rx[:, s, :], 16 + 13 - c), start=True, stop=True)
                        else:
                            for t in range(2):
                                cols = slice((2 * (j - 8) + t) * HALF, (2 * (j - 8) + t + 1) * HALF)
                                ins = nc.tensor.matmul(bank[0:HALF, t * DIM:(t + 1) * DIM], oT[:, s, cols], pw[:, p, :],
                                                       start=True, stop=True)
                        ins.then_inc(full[k % 2], 1)

                    for j in opening:
                        job(*j)
                    for i in range(STEPS + 3):
                        n = g * STEPS + i
                        if i < STEPS:
                            p, b, head = i // UNIT, i % UNIT // 2, i % 2
                            if i % UNIT == 0:
                                all_read("first", p, FIRST - 1)
                            K = 128 if head else 96
                            if i >= 2:
                                pe.wait_ge(exps, n - 1)
                            for h in range(2):
                                q0 = b * NTOK + h * HALF
                                ins = nc.tensor.matmul(s_bank[i % 2][0:HALF, h * NTOK:(h + 1) * NTOK],
                                                       qx[0:K, p % 2, head, q0:q0 + HALF],
                                                       kx[0:K, p % 2, head, b * NTOK:(b + 1) * NTOK], start=True, stop=True)
                            ins.then_inc(scores, 1)
                        if 2 <= i < STEPS + 2:
                            j = i - 2
                            pe.wait_ge(probs, n - 2 + 1)
                            if i >= 4:
                                pe.wait_ge(probT_made, n - 3)
                            for k in range(2):
                                for h in range(2):
                                    ins = nc.tensor.transpose(
                                        t_bank[j % 2][0:HALF, k * NTOK + h * HALF:k * NTOK + (h + 1) * HALF],
                                        prob[:, j % 2, h, k * HALF:(k + 1) * HALF], ident[0:HALF, 0:HALF])
                            ins.then_inc(turned, 1)
                        if i < STEPS:
                            for j in between[i]:
                                job(*j)
                        if i >= 3:
                            j = i - 3
                            p, b, head = j // UNIT, j % UNIT // 2, j % 2
                            M, v0 = (128, 32) if head else (96, 0)
                            pe.wait_ge(probT_made, n - 3 + 1)
                            if i >= 5:
                                pe.wait_ge(outs_used, n - 4)
                            for k in range(2):
                                ins = nc.tensor.matmul(o_bank[j % 2][0:M, 0:NTOK], vx[:, p % 2, 2 * b + k, v0:v0 + M],
                                                       probT[:, j % 2, k * NTOK:(k + 1) * NTOK],
                                                       start=(k == 0), stop=(k == 1))
                            ins.then_inc(outs, 1)
                    for j in closing:
                        job(*j)


def experts_stage(nc, hidden1, w_fc_sh, w_proj_sh, w1, w2, router_w, balance_bias, out):
    TB = 3
    BT = TB * 128
    BLOCKS = B * NTOK // BT
    MLPS = EXPERTS + 1
    HID = MLPS * DIM
    HT = (HID + 127) // 128
    fp32r = mybir.dt.float32r
    with ExitStack() as ctx:
        m = Memory(nc, ctx, "ffn")
        hid = m.sb("hid", [128, 2, TB, DIM])
        norm = m.sb("norm", [128, TB, DIM])
        acc = m.sb("acc", [128, 2, TB, DIM])
        x0h, x0l = m.sb("x0h", [C0, BT], fp32r), m.sb("x0l", [C0, BT], fp32r)
        x1 = m.sb("x1", [128, BT], fp32r)
        raw0, raw1 = m.sb("raw0", [C0, HID + EXPERTS]), m.sb("raw1", [C1, HID + EXPERTS])
        w0h, w0l = m.sb("w0h", [C0, HID + EXPERTS], fp32r), m.sb("w0l", [C0, HID + EXPERTS], fp32r)
        w1h, w1l = m.sb("w1h", [128, HID + EXPERTS], fp32r), m.sb("w1l", [128, HID + EXPERTS], fp32r)
        down = m.sb("down", [128, HT, DIM])
        hidden = m.sb("hidden", [128, HT, BT])
        relu = m.sb("relu", [128, 4, BT])
        bb, ranks = m.sb("bb", [128, EXPERTS]), m.sb("ranks", [128, EXPERTS])
        ident = m.sb("ident", [128, 128])
        stat, mv, sd = m.sb("stat", [128, TB, 6]), m.sb("mv", [128, TB, 2]), m.sb("sd", [128, TB, 1])
        eps = m.sb("eps", [128, 1])
        mv_made, sd_made = m.sem("mv_made"), m.sem("sd_made")
        expo, sc, sb_, eq, first, left, second, weight = (m.sb(n, [128, TB, EXPERTS]) for n in (
            "expo", "score", "biased", "eq", "first", "left", "second", "weight"))
        gate = m.sb("gate", [128, 2, TB, EXPERTS])
        top = m.sb("top", [128, TB, 1])
        t_bank = [m.bank(f"t{i}") for i in range(2)]
        h_bank = [m.bank(f"h{i}") for i in range(2)]
        y_bank = [m.bank(f"y{i}") for i in range(3)]
        r_bank = m.bank("r")
        w_in, router_in, w_made, ranks_made, hid_in = m.sem("w_in"), m.sem("router_in"), m.sem("w_made"), m.sem("ranks_made"), [m.sem(f"hid_in{i}") for i in range(2)]
        norm_made, turned, high_made, xT_made, dve_step = (m.sem("norm_made"), m.sem("turned"), m.sem("high_made"),
                                                           m.sem("xT_made"), m.sem("dve_step"))
        routed, expo_made, passed = m.sem("routed"), m.sem("expo_made"), m.sem("passed")
        up_done, relu_made, squared = m.sem("up_done"), [m.sem(f"relu_made{i}") for i in range(2)], m.sem("squared")
        down_done, summed, acc_out = m.sem("down_done"), m.sem("summed"), [m.sem(f"acc_out{i}") for i in range(2)]
        h_tiles = hidden1.rearrange("b n d -> (b n) d").rearrange("(t p) d -> p t d", p=128)
        o_tiles = out.rearrange("b n d -> (b n) d").rearrange("(t p) d -> p t d", p=128)
        DOWNS = [(EXPERTS, [(12, 0, 128), (13, 0, 64)])]
        for i in range(EXPERTS // 2):
            DOWNS += [(2 * i, [(3 * i, 0, 128), (3 * i + 1, 0, 64)]), (2 * i + 1, [(3 * i + 2, 0, 128), (3 * i + 1, 64, 64)])]
        UPS = [12, 13] + list(range(12))
        AFTER = [[0, 1], [2], [3, 4], [5], [6, 7], [8], [9, 10], [11], [12, 13]]
        RELU_BEFORE = [max(n for n in range(HT) if n % 4 == b) - HT for b in range(4)]
        WEIGHTS = 8

        with nc.Block() as block:

            @block.sync
            def _(sp):
                for s in (*acc_out, *relu_made, summed):
                    sp.sem_inc(s, PRIMED)

                def load(it, s):
                    sp.dma_start(hid[:, s, :, :], h_tiles[:, bass.ds(it * TB, TB), :]).then_inc(hid_in[s], 16)

                def store(it, s):
                    sp.wait_ge(summed, (it + 1) * TB * MLPS + PRIMED)
                    sp.dma_start(o_tiles[:, bass.ds(it * TB, TB), :], acc[:, s, :, :]).then_inc(acc_out[s], 16)

                load(0, 0)
                load(1, 1)
                sp.dma_start(raw0[:, 0:EXPERTS * DIM].rearrange("c (e h) -> c e h", e=EXPERTS),
                             w1[:, 0:C0, :].rearrange("e c h -> c e h")).then_inc(w_in, 16)
                sp.dma_start(raw1[:, 0:EXPERTS * DIM].rearrange("c (e h) -> c e h", e=EXPERTS),
                             w1[:, C0:DIM, :].rearrange("e c h -> c e h")).then_inc(w_in, 16)
                sp.dma_start(raw0[:, EXPERTS * DIM:HID], w_fc_sh[0:C0, :]).then_inc(w_in, 16)
                sp.dma_start(raw1[:, EXPERTS * DIM:HID], w_fc_sh[C0:DIM, :]).then_inc(w_in, 16)
                sp.dma_start(down[:, 0:12, :], w2.rearrange("e h d -> (e h) d").rearrange("(t p) d -> p t d", p=128)).then_inc(w_in, 16)
                sp.dma_start(down[:, 12, :], w_proj_sh[0:128, :]).then_inc(w_in, 16)
                sp.dma_start(down[0:64, 13, :], w_proj_sh[128:DIM, :]).then_inc(w_in, 16)
                sp.dma_start(bb[:, :], bass.AP(tensor=balance_bias.tensor, offset=balance_bias.offset,
                                               ap=[[0, 128], [1, EXPERTS]])).then_inc(w_in, 16)
                with sp.Fori(0, BLOCKS // 2) as pair:
                    for s in range(2):
                        it = pair * 2 + s
                        sp.wait_ge(summed, it * TB * MLPS + TB + PRIMED)
                        load((it + 2) % BLOCKS, s)
                        store(it, s)
                store(BLOCKS - 1, 0)
                sp.wait_ge(hid_in[0], 16 * (BLOCKS // 2 + 1))
                sp.wait_ge(hid_in[1], 16 * (BLOCKS // 2 + 1))
                sp.wait_ge(acc_out[0], 16 * (BLOCKS // 2 + 1) + PRIMED)
                sp.wait_ge(acc_out[1], 16 * (BLOCKS // 2) + PRIMED)

            @block.gpsimd
            def _(pool):
                with nc.allow_non_contiguous_dma(reason="a small weight, transposed"):
                    pool.dma_start(raw0[:, HID:], router_w[:, 0:C0].rearrange("e c -> c e")).then_inc(router_in, 16)
                    pool.dma_start(raw1[:, HID:], router_w[:, C0:DIM].rearrange("e c -> c e")).then_inc(router_in, 16)
                make_identity(pool, nc, ident, ranks_made)
                nc.gpsimd.iota(ranks[:, :], [[-1, EXPERTS]], base=EXPERTS, channel_multiplier=0,
                               allow_small_or_imprecise_dtypes=True).then_inc(ranks_made, 1)
                with pool.Fori(0, BLOCKS) as it:
                    for n in range(HT):
                        j = UPS[n]
                        rows = 64 if j == 13 else 128
                        pool.wait_ge(relu_made[n % 2], it * (HT // 2) + n // 2 + 1 + PRIMED)
                        nc.gpsimd.tensor_tensor(hidden[0:rows, j, :], relu[0:rows, n % 4, :], relu[0:rows, n % 4, :], ALU.mult
                                                ).then_inc(squared, 1)

            @block.scalar
            def _(act):
                def deviation(k):
                    act.wait_ge(mv_made, k + 1)
                    nc.scalar.activation(sd[:, :, :], mv[:, :, 1:2], ACT.Sqrt, bias=eps[:, :]).then_inc(sd_made, 1)

                def high(k):
                    act.wait_ge(turned, k + 1)
                    nc.scalar.activation(x0h[:, :], t_bank[0][:, 0:BT], ACT.Copy)
                    nc.scalar.activation(x1[0:C1, :], t_bank[1][0:C1, 0:BT], ACT.Copy).then_inc(high_made, 1)

                def exponentials(k):
                    act.wait_ge(routed, k + 1)
                    nc.scalar.activation(expo[:, :, :], r_bank[:, 0:TB * EXPERTS].rearrange("p (t e) -> p t e", t=TB),
                                         ACT.Exp, scale=-1.0).then_inc(expo_made, 1)

                def relus(k, numbers):
                    for n in numbers:
                        if n % 2 == 0:
                            act.wait_ge(up_done, k * HT + n + 1)
                            before = n - 4 if n >= 4 else RELU_BEFORE[n]
                            if n >= 4 or not isinstance(k, int):
                                act.wait_ge(squared, k * HT + before + 1)
                            nc.scalar.activation(relu[:, n % 4, :], h_bank[0][:, 0:BT], ACT.Relu).then_inc(relu_made[0], 1)

                act.wait_ge(w_made, 1)
                deviation(0)
                high(0)
                exponentials(0)
                relus(0, range(HT))
                deviation(1)
                with act.Fori(0, BLOCKS - 1) as it:
                    high(it + 1)
                    exponentials(it + 1)
                    for k, numbers in enumerate(AFTER):
                        relus(it + 1, numbers)
                        if k == 5:
                            deviation(it + 2)

            @block.vector
            def _(dve):
                nc.vector.memset(eps[:, :], EPS).then_inc(w_made, 1)

                def statistics(s, st):
                    for t in range(TB):
                        ins = nc.vector.bn_stats(stat[:, t, :], hid[:, s, t, :])
                    st.did(ins)
                    st.settle_apart(passed)
                    for t in range(TB):
                        ins = nc.vector.bn_aggr(mv[:, t, :], stat[:, t, :])
                    ins.then_inc(mv_made, 1)

                def layernorm(k, s, st):
                    dve.wait_ge(sd_made, k + 1)
                    st.did(nc.vector.reciprocal(sd[:, :, :], sd[:, :, :]))
                    st.settle()
                    for t in range(TB):
                        ins = nc.vector.tensor_scalar(norm[:, t, :], hid[:, s, t, :], mv[:, t, 0:1], sd[:, t, :],
                                                      ALU.subtract, ALU.mult)
                    ins.then_inc(norm_made, 1)

                def low(k):
                    dve.wait_ge(high_made, k + 1)
                    nc.vector.tensor_tensor(x0l[:, :], t_bank[0][:, 0:BT], x0h[:, :].bitcast(fp32), ALU.subtract)
                    nc.vector.tensor_tensor(x1[C1:128, :], t_bank[1][0:C1, 0:BT], x1[0:C1, :].bitcast(fp32), ALU.subtract
                                            ).then_inc(xT_made, 1)

                def route(it, s, st, parts):
                    def step(ins):
                        st.did(ins)
                        st.settle()

                    def wide(ap):
                        return view(ap, [[1, TB], [0, EXPERTS]])

                    def const(ap):
                        return view(ap, [[0, TB], [1, EXPERTS]])

                    if 0 in parts:
                        dve.wait_ge(expo_made, it + 1)
                        step(nc.vector.tensor_scalar(expo[:, :, :], expo[:, :, :], 1.0, None, ALU.add))
                        step(nc.vector.reciprocal(sc[:, :, :], expo[:, :, :]))
                        step(nc.vector.tensor_tensor(sb_[:, :, :], sc[:, :, :], const(bb[:, :]), ALU.add))
                    for part, cur, pick in ((1, sb_, first), (2, left, second)):
                        if part in parts:
                            step(nc.vector.tensor_reduce(top[:, :, 0], cur[:, :, :], AX.X, ALU.max))
                            step(nc.vector.tensor_tensor(eq[:, :, :], cur[:, :, :], wide(top[:, :, 0]), ALU.is_equal))
                            step(nc.vector.tensor_tensor(eq[:, :, :], eq[:, :, :], const(ranks[:, :]), ALU.mult))
                            step(nc.vector.tensor_reduce(top[:, :, 0], eq[:, :, :], AX.X, ALU.max))
                            step(nc.vector.tensor_tensor(pick[:, :, :], eq[:, :, :], wide(top[:, :, 0]), ALU.is_equal))
                        if part == 1 and part in parts:
                            step(nc.vector.scalar_tensor_tensor(left[:, :, :], first[:, :, :], -1e30, sb_[:, :, :], ALU.mult, ALU.add))
                    if 3 in parts:
                        step(nc.vector.tensor_tensor(eq[:, :, :], first[:, :, :], second[:, :, :], ALU.add))
                        step(nc.vector.tensor_tensor(weight[:, :, :], eq[:, :, :], sc[:, :, :], ALU.mult))
                        step(nc.vector.reduce_sum(top[:, :, 0], weight[:, :, :], AX.X))
                        step(nc.vector.tensor_scalar(top[:, :, :], top[:, :, :], 1e-20, None, ALU.add))
                        step(nc.vector.reciprocal(top[:, :, :], top[:, :, :]))
                        step(nc.vector.tensor_tensor(gate[:, s, :, :], weight[:, :, :], wide(top[:, :, 0]), ALU.mult))

                def relus(k, numbers):
                    for n in numbers:
                        if n % 2:
                            rows = 64 if UPS[n] == 13 else 128
                            dve.wait_ge(up_done, k * HT + n + 1)
                            before = n - 4 if n >= 4 else RELU_BEFORE[n]
                            if n >= 4 or not isinstance(k, int):
                                dve.wait_ge(squared, k * HT + before + 1)
                            nc.vector.tensor_scalar(relu[0:rows, n % 4, :], h_bank[1][0:rows, 0:BT], 0.0, None, ALU.max
                                                    ).then_inc(relu_made[1], 1)

                def sums(it, s, k):
                    e = DOWNS[k][0]
                    for t in range(TB):
                        n = it * TB * MLPS + k * TB + t
                        dve.wait_ge(down_done, n + 1)
                        y = y_bank[t][:, 0:DIM]
                        if k == 0:
                            nc.vector.tensor_tensor(acc[:, s, t, :], y, hid[:, s, t, :], ALU.add).then_inc(summed, 1)
                        else:
                            if t == 0:
                                dve.wait_ge(summed, it * TB * MLPS + k * TB + PRIMED)
                            nc.vector.scalar_tensor_tensor(acc[:, s, t, :], y, gate[:, s, t, e:e + 1], acc[:, s, t, :],
                                                           ALU.mult, ALU.add).then_inc(summed, 1)

                dve.wait_ge(hid_in[0], 16)
                first_steps = Steps(dve, dve_step, 0)
                statistics(0, first_steps)
                layernorm(0, 0, first_steps)
                dve.wait_ge(w_in, 16 * WEIGHTS)
                dve.wait_ge(router_in, 32)
                nc.vector.tensor_copy(w0h[:, :], raw0[:, :])
                for lo in (0, C1):
                    ins = nc.vector.tensor_copy(w1h[lo:lo + C1, :], raw1[:, :])
                ins.then_inc(w_made, 1)
                dve.wait_ge(w_made, 2)
                nc.vector.tensor_tensor(w0l[:, :], raw0[:, :], w0h[:, :].bitcast(fp32), ALU.subtract)
                for lo in (0, C1):
                    ins = nc.vector.tensor_tensor(w1l[lo:lo + C1, :], raw1[:, :], w1h[0:C1, :].bitcast(fp32), ALU.subtract)
                ins.then_inc(w_made, 1)
                low(0)
                dve.wait_ge(ranks_made, 3)
                route(0, 0, first_steps, range(4))
                relus(0, range(HT))
                dve.wait_ge(hid_in[1], 16)
                statistics(1, first_steps)
                layernorm(1, 1, first_steps)
                K_BODY = first_steps.n - 2
                with dve.Fori(0, BLOCKS // 2) as pair:
                    for s in range(2):
                        it = pair * 2 + s
                        st = Steps(dve, dve_step, first_steps.n + it * K_BODY)
                        low(it + 1)
                        dve.wait_ge(acc_out[s], pair * 16 + PRIMED)
                        for k in range(MLPS):
                            sums(it, s, k)
                            relus(it + 1, AFTER[k])
                            if 2 <= k <= 5:
                                route(it + 1, 1 - s, st, [k - 2])
                            if k == 5:
                                dve.wait_ge(hid_in[s], pair * 16 + 32)
                                statistics(s, st)
                            if k == 7:
                                layernorm(it + 2, s, st)
                        assert st.n == K_BODY, (st.n, K_BODY)
                dve.wait_ge(acc_out[0], 16 * (BLOCKS // 2) + PRIMED)
                for k in range(MLPS):
                    sums(BLOCKS - 1, 0, k)

            @block.tensor
            def _(pe):
                def turn(k):
                    pe.wait_ge(norm_made, k + 1)
                    for t in range(TB):
                        cols = slice(t * 128, (t + 1) * 128)
                        nc.tensor.transpose(t_bank[0][:, cols], norm[:, t, 0:C0], ident[:, :])
                        ins = nc.tensor.transpose(t_bank[1][0:C1, cols], norm[:, t, C0:DIM], ident[:, :])
                    ins.then_inc(turned, 1)

                def route(k):
                    pe.wait_ge(xT_made, k + 1)
                    for t in range(TB):
                        cols, wc = slice(t * 128, (t + 1) * 128), slice(HID, HID + EXPERTS)
                        o = r_bank[:, t * EXPERTS:(t + 1) * EXPERTS]
                        parts = ((x0h, w0h), (x0l, w0h), (x0h, w0l), (x0l, w0l), (x1, w1h), (x1, w1l))
                        for i, (a, b) in enumerate(parts):
                            ins = nc.tensor.matmul(o, a[:, cols], b[:, wc], start=(i == 0), stop=(i == len(parts) - 1))
                    ins.then_inc(routed, 1)

                def ups(k, numbers):
                    for n in numbers:
                        j = UPS[n]
                        rows = 64 if j == 13 else 128
                        wc = slice(128 * j, 128 * j + rows)
                        pe.wait_ge(relu_made[n % 2], k * (HT // 2) + n // 2 + PRIMED)
                        o = h_bank[n % 2][0:rows, 0:BT]
                        parts = ((w0h, x0h), (w0h, x0l), (w0l, x0h), (w1h, x1), (w1l, x1))
                        for i, (a, b) in enumerate(parts):
                            ins = nc.tensor.matmul(o, a[:, wc], b[:, :], start=(i == 0), stop=(i == len(parts) - 1))
                        ins.then_inc(up_done, 1)

                def down_(it, k):
                    parts = DOWNS[k][1]
                    pe.wait_ge(squared, it * HT + max(UPS.index(j) for j, _, _ in parts) + 1)
                    for t in range(TB):
                        n = it * TB * MLPS + k * TB + t
                        pe.wait_ge(summed, (n - TB + 1 if k else it * TB * MLPS) + PRIMED)
                        for i, (j, r0, rows) in enumerate(parts):
                            ins = nc.tensor.matmul(y_bank[t][:, 0:DIM], hidden[r0:r0 + rows, j, t * 128:(t + 1) * 128],
                                                   down[r0:r0 + rows, j, :], start=(i == 0), stop=(i == len(parts) - 1))
                        ins.then_inc(down_done, 1)

                pe.wait_ge(ranks_made, 2)
                turn(0)
                pe.wait_ge(w_made, 3)
                route(0)
                ups(0, range(HT))
                with pe.Fori(0, BLOCKS - 1) as it:
                    turn(it + 1)
                    down_(it, 0)
                    route(it + 1)
                    ups(it + 1, AFTER[0])
                    for k in range(1, MLPS):
                        down_(it, k)
                        ups(it + 1, AFTER[k])
                for k in range(MLPS):
                    down_(BLOCKS - 1, k)


def vit_tower(nc, x, cls_tok, ln1_g, ln1_b, w_proj, b_proj, ln2_g, ln2_b, pos, cls_token, qkv_w, proj_w, proj_b,
              tab_kv, tab_kh, tab_vv, tab_vh, w_fc_sh, w_proj_sh, w1, w2, router_w, balance_bias, out):
    hidden0 = nc.dram_tensor("hidden0", [B, NTOK, DIM], fp32, kind="Internal").ap()
    hidden1 = nc.dram_tensor("hidden1", [B, NTOK, DIM], fp32, kind="Internal").ap()
    tokens_stage(nc, x, cls_tok, ln1_g, ln1_b, w_proj, b_proj, ln2_g, ln2_b, pos, cls_token, hidden0)
    attention_stage(nc, hidden0, qkv_w, proj_w, proj_b, tab_kv, tab_kh, tab_vv, tab_vh, hidden1)
    experts_stage(nc, hidden1, w_fc_sh, w_proj_sh, w1, w2, router_w, balance_bias, out)


_INS = ['x', 'cls_tok', 'L0_tok_ln1_g', 'L0_tok_ln1_b', 'L0_tok_W_proj', 'L0_tok_b_proj', 'L0_tok_ln2_g',
        'L0_tok_ln2_b', 'L0_tok_pos_embedding', 'L0_tok_cls_token', 'L0_attn_qkv_w', 'L0_attn_proj_w',
        'L0_attn_proj_b', 'L0_attn_tab_kv', 'L0_attn_tab_kh', 'L0_attn_tab_vv', 'L0_attn_tab_vh',
        'L0_ffn_w_fc_sh', 'L0_ffn_w_proj_sh', 'L0_ffn_w1', 'L0_ffn_w2', 'L0_ffn_router_w', 'L0_ffn_balance_bias']


def kernel(**inputs):
    import concourse.bacc as bacc
    from concourse.bass_utils import run_bass_kernel_spmd

    nc = bacc.Bacc("TRN2", target_bir_lowering=False, num_devices=1)
    arrays, args = {}, []
    for name in _INS:
        a = np.ascontiguousarray(inputs[name])
        arrays[f"in_{name}"] = a
        args.append(nc.dram_tensor(f"in_{name}", a.shape, mybir.dt.from_np(a.dtype), kind="ExternalInput").ap())
    args.append(nc.dram_tensor("out_hidden", (B, NTOK, DIM), fp32, kind="ExternalOutput").ap())
    vit_tower(nc, *args)
    r = run_bass_kernel_spmd(nc, [arrays], core_ids=[0])
    return r.results[0]["out_hidden"]
```
